# Optimizing a Trainium2 kernel written in Bass

```python
import numpy as np
import jax
import jax.numpy as jnp

def _softmax(x, axis=-1):
    return jax.nn.softmax(x, axis=axis)

def _gelu(x):
    return jax.nn.gelu(x, approximate=True)

def _silu(x):
    return jax.nn.silu(x)

def _sigmoid(x):
    return jax.nn.sigmoid(x)

def _layernorm(x, axis=-1, eps=1e-05):
    m = jnp.mean(x, axis=axis, keepdims=True)
    v = jnp.var(x, axis=axis, keepdims=True)
    return (x - m) / jnp.sqrt(v + eps)

def _scatter_add(tgt, idx, src, axis=0):
    return tgt.at[idx].add(src)

def _segment_sum(src, seg, n):
    return jax.ops.segment_sum(src, seg, n)
kernel_name = 'mk_adaln_attn_ffn_d1_seqx_r4_e086ae'

def setup_inputs(seed: int=0):
    np.random.seed(seed)
    _w = jnp.asarray

    def _rec_inputs():
        import jax
        import jax.numpy as jnp
        _rk = jax.random.key(seed)
        x = -0.0002928 + 1 * jax.random.normal(jax.random.fold_in(_rk, 1), (2, 1024, 256), jnp.float32)
        _lenS = 1024 - jax.random.randint(jax.random.fold_in(_rk, 7), (2,), 0, max(1, 1024 // 4) + 1, jnp.int32)
        _lenS2 = 1024 - jax.random.randint(jax.random.fold_in(_rk, 8), (2,), 0, max(1, 1024 // 4) + 1, jnp.int32)
        cond_256 = -0.106481 + 1.03144 * jax.random.normal(jax.random.fold_in(_rk, 11), (2, 64), jnp.float32)
        _validS = jnp.arange(1024)[None, :] < _lenS[:, None]
        _validS2 = jnp.arange(1024)[None, :] < _lenS2[:, None]
        _causal = jnp.tril(jnp.ones((1024, 1024), dtype=bool))
        mask_SxS_bk1 = jnp.broadcast_to(_validS[0:1, :], (1024, 1024))
        return (x, cond_256, mask_SxS_bk1)
    x, cond_256, mask_SxS_bk1 = _rec_inputs()

    def _L0_cond_setup():
        import jax, jax.numpy as jnp
        import numpy as np
        TOP_K = 2
        EPS = 1e-06
        B, S, H, G, E, M = (2, 512, 256, 64, 8, 512)
        key = jax.random.key(seed)
        ks = jax.random.split(key, 16)
        s_h = 1.0 / np.sqrt(H)
        s_g = 1.0 / np.sqrt(G)
        s_m = 1.0 / np.sqrt(M)
        return {'x': jax.random.normal(ks[0], (B, S, H), jnp.float32), 'genre_embed': jax.random.normal(ks[1], (B, 1, G), jnp.float32), 'rms_w': jnp.ones((H,), jnp.float32), 'wg_W': jax.random.normal(ks[2], (H, E), jnp.float32) * s_h, 'wg_b': jnp.zeros((E,), jnp.float32), 'gg_W': jax.random.normal(ks[3], (G, E), jnp.float32) * s_g, 'gg_b': jnp.zeros((E,), jnp.float32), 'W1': jax.random.normal(ks[4], (E, H, M), jnp.float32) * s_h, 'b1': jnp.zeros((E, M), jnp.float32), 'W2': jax.random.normal(ks[5], (E, M, M), jnp.float32) * s_m, 'b2': jnp.zeros((E, M), jnp.float32), 'W3': jax.random.normal(ks[6], (E, M, H), jnp.float32) * s_m, 'b3': jnp.zeros((E, H), jnp.float32)}
    _L0_cond_all = _L0_cond_setup()
    _L0_cond_in = {k: v for k, v in _L0_cond_all.items() if k in ('rms_w', 'wg_W', 'wg_b', 'gg_W', 'gg_b', 'W1', 'b1', 'W2', 'b2', 'W3', 'b3')}
    del _L0_cond_all

    def _L0_attn_setup():
        import jax, jax.numpy as jnp
        import numpy as np
        D_MODEL = 256
        D_FF = 1024
        FFN_H = int(2 * D_FF / 3)
        B, S = (4, 1024)
        LN_EPS = 1e-05
        ATTN_EPS = 1e-06

        def layer_norm(x, g, b):
            mu = jnp.mean(x, axis=-1, keepdims=True)
            var = jnp.mean(jnp.square(x - mu), axis=-1, keepdims=True)
            return (x - mu) * jax.lax.rsqrt(var + LN_EPS) * g + b
        key = jax.random.key(seed)
        ks = jax.random.split(key, 16)
        s = 0.02
        return {'x': jax.random.normal(ks[0], (B, S, D_MODEL), dtype=jnp.float32), 'Wqkv': jax.random.normal(ks[1], (D_MODEL, 3 * D_MODEL), dtype=jnp.float32) * s, 'bqkv': jnp.zeros((3 * D_MODEL,), jnp.float32), 'Wg': jax.random.normal(ks[2], (D_MODEL, FFN_H), dtype=jnp.float32) * s, 'bg': jnp.zeros((FFN_H,), jnp.float32), 'Wu': jax.random.normal(ks[3], (D_MODEL, FFN_H), dtype=jnp.float32) * s, 'bu': jnp.zeros((FFN_H,), jnp.float32), 'Wd': jax.random.normal(ks[4], (FFN_H, D_MODEL), dtype=jnp.float32) * s, 'bd': jnp.zeros((D_MODEL,), jnp.float32), 'g1': jnp.ones((D_MODEL,), jnp.float32), 'b1': jnp.zeros((D_MODEL,), jnp.float32), 'g2': jnp.ones((D_MODEL,), jnp.float32), 'b2': jnp.zeros((D_MODEL,), jnp.float32)}
    _L0_attn_all = _L0_attn_setup()
    _L0_attn_in = {k: v for k, v in _L0_attn_all.items() if k in ('Wqkv', 'bqkv', 'Wg', 'bg', 'Wu', 'bu', 'Wd', 'bd', 'g1', 'b1', 'g2', 'b2')}
    del _L0_attn_all

    def _L0_cond2_setup():
        import jax, jax.numpy as jnp
        import numpy as np
        EPS = 1e-06
        key = jax.random.key(seed)
        ks = jax.random.split(key, 8)
        B, S, E, C = (2, 512, 256, 64)
        x = jax.random.normal(ks[0], (B, S, E), dtype=jnp.float32)
        mask = jnp.triu(jnp.ones((S, S), dtype=bool), k=1)
        conditioning = jax.random.normal(ks[1], (B, C), dtype=jnp.float32)
        sc = 1.0 / np.sqrt(E)
        Wq = jax.random.normal(ks[2], (E, E), dtype=jnp.float32) * sc
        Wk = jax.random.normal(ks[3], (E, E), dtype=jnp.float32) * sc
        Wv = jax.random.normal(ks[4], (E, E), dtype=jnp.float32) * sc
        Wo = jax.random.normal(ks[5], (E, E), dtype=jnp.float32) * sc
        rms_scale = jnp.ones((E,), dtype=jnp.float32)
        Wc = jax.random.normal(ks[6], (2 * E, C), dtype=jnp.float32) * 0.02
        bc = jax.random.normal(ks[7], (2 * E,), dtype=jnp.float32) * 0.02
        return {'x': x, 'mask': mask, 'conditioning': conditioning, 'Wq': Wq, 'Wk': Wk, 'Wv': Wv, 'Wo': Wo, 'rms_scale': rms_scale, 'Wc': Wc, 'bc': bc}
    _L0_cond2_all = _L0_cond2_setup()
    _L0_cond2_in = {k: v for k, v in _L0_cond2_all.items() if k in ('Wq', 'Wk', 'Wv', 'Wo', 'rms_scale', 'Wc', 'bc')}
    del _L0_cond2_all

    def _L0_ffn_setup():
        import jax, jax.numpy as jnp
        import numpy as np
        B, L, D = (4, 256, 256)
        E, H, K = (16, 128, 8)
        EPS = 1e-12

        def _l2norm(v, axis=-1):
            n = jnp.sqrt(jnp.sum(v * v, axis=axis, keepdims=True))
            return v / jnp.maximum(n, EPS)
        if __name__ == '__main__':
            out = reference(**setup_inputs())
            print(out.shape)
        key = jax.random.key(seed)
        ks = jax.random.split(key, 8)
        s = lambda fan_in: 1.0 / np.sqrt(fan_in)
        return {'x': jax.random.normal(ks[0], (B, L, D), jnp.float32), 'gate_w': jax.random.normal(ks[1], (E, D), jnp.float32) * s(D), 'w_gate': jax.random.normal(ks[2], (E, D, H), jnp.float32) * s(D), 'w_up': jax.random.normal(ks[3], (E, D, H), jnp.float32) * s(D), 'w_down': jax.random.normal(ks[4], (E, H, D), jnp.float32) * s(H), 'sw_gate': jax.random.normal(ks[5], (D, H), jnp.float32) * s(D), 'sw_up': jax.random.normal(ks[6], (D, H), jnp.float32) * s(D), 'sw_down': jax.random.normal(ks[7], (H, D), jnp.float32) * s(H)}
    _L0_ffn_all = _L0_ffn_setup()
    _L0_ffn_in = {k: v for k, v in _L0_ffn_all.items() if k in ('gate_w', 'w_gate', 'w_up', 'w_down', 'sw_gate', 'sw_up', 'sw_down')}
    del _L0_ffn_all
    return {'x': x, 'cond_256': cond_256, 'mask_SxS_bk1': mask_SxS_bk1, 'L0_cond_rms_w': _L0_cond_in['rms_w'], 'L0_cond_wg_W': _L0_cond_in['wg_W'], 'L0_cond_wg_b': _L0_cond_in['wg_b'], 'L0_cond_gg_W': _L0_cond_in['gg_W'], 'L0_cond_gg_b': _L0_cond_in['gg_b'], 'L0_cond_W1': _L0_cond_in['W1'], 'L0_cond_b1': _L0_cond_in['b1'], 'L0_cond_W2': _L0_cond_in['W2'], 'L0_cond_b2': _L0_cond_in['b2'], 'L0_cond_W3': _L0_cond_in['W3'], 'L0_cond_b3': _L0_cond_in['b3'], 'L0_attn_Wqkv': _L0_attn_in['Wqkv'], 'L0_attn_bqkv': _L0_attn_in['bqkv'], 'L0_attn_Wg': _L0_attn_in['Wg'], 'L0_attn_bg': _L0_attn_in['bg'], 'L0_attn_Wu': _L0_attn_in['Wu'], 'L0_attn_bu': _L0_attn_in['bu'], 'L0_attn_Wd': _L0_attn_in['Wd'], 'L0_attn_bd': _L0_attn_in['bd'], 'L0_attn_g1': _L0_attn_in['g1'], 'L0_attn_b1': _L0_attn_in['b1'], 'L0_attn_g2': _L0_attn_in['g2'], 'L0_attn_b2': _L0_attn_in['b2'], 'L0_cond2_Wq': _L0_cond2_in['Wq'], 'L0_cond2_Wk': _L0_cond2_in['Wk'], 'L0_cond2_Wv': _L0_cond2_in['Wv'], 'L0_cond2_Wo': _L0_cond2_in['Wo'], 'L0_cond2_rms_scale': _L0_cond2_in['rms_scale'], 'L0_cond2_Wc': _L0_cond2_in['Wc'], 'L0_cond2_bc': _L0_cond2_in['bc'], 'L0_ffn_gate_w': _L0_ffn_in['gate_w'], 'L0_ffn_w_gate': _L0_ffn_in['w_gate'], 'L0_ffn_w_up': _L0_ffn_in['w_up'], 'L0_ffn_w_down': _L0_ffn_in['w_down'], 'L0_ffn_sw_gate': _L0_ffn_in['sw_gate'], 'L0_ffn_sw_up': _L0_ffn_in['sw_up'], 'L0_ffn_sw_down': _L0_ffn_in['sw_down']}

def reference(x, cond_256, mask_SxS_bk1, L0_cond_rms_w, L0_cond_wg_W, L0_cond_wg_b, L0_cond_gg_W, L0_cond_gg_b, L0_cond_W1, L0_cond_b1, L0_cond_W2, L0_cond_b2, L0_cond_W3, L0_cond_b3, L0_attn_Wqkv, L0_attn_bqkv, L0_attn_Wg, L0_attn_bg, L0_attn_Wu, L0_attn_bu, L0_attn_Wd, L0_attn_bd, L0_attn_g1, L0_attn_b1, L0_attn_g2, L0_attn_b2, L0_cond2_Wq, L0_cond2_Wk, L0_cond2_Wv, L0_cond2_Wo, L0_cond2_rms_scale, L0_cond2_Wc, L0_cond2_bc, L0_ffn_gate_w, L0_ffn_w_gate, L0_ffn_w_up, L0_ffn_w_down, L0_ffn_sw_gate, L0_ffn_sw_up, L0_ffn_sw_down):
    import jax
    import jax.numpy as jnp

    def _L0_cond_ref(x, genre_embed, rms_w, wg_W, wg_b, gg_W, gg_b, W1, b1, W2, b2, W3, b3):
        import jax, jax.numpy as jnp
        import numpy as np
        TOP_K = 2
        EPS = 1e-06
        E = W1.shape[0]
        var = jnp.mean(x * x, axis=-1, keepdims=True)
        xn = rms_w * (x * jax.lax.rsqrt(var + EPS))
        gate = xn @ wg_W + wg_b + (genre_embed @ gg_W + gg_b)
        gate_w = jax.nn.softmax(gate, axis=-1)
        topk_w, topk_i = jax.lax.top_k(gate_w, TOP_K)
        cw = jnp.sum(jax.nn.one_hot(topk_i, E, dtype=x.dtype) * topk_w[..., None], axis=-2)
        h1 = jax.nn.relu(jnp.einsum('bsh,ehm->bsem', x, W1) + b1)
        h2 = jax.nn.relu(jnp.einsum('bsem,emn->bsen', h1, W2) + b2)
        out_e = jnp.einsum('bsen,enh->bseh', h2, W3) + b3
        return jnp.einsum('bseh,bse->bsh', out_e, cw)

    def _L0_attn_ref(x, Wqkv, bqkv, Wg, bg, Wu, bu, Wd, bd, g1, b1, g2, b2):
        import jax, jax.numpy as jnp
        import numpy as np
        D_MODEL = 256
        D_FF = 1024
        FFN_H = int(2 * D_FF / 3)
        B, S = (4, 1024)
        LN_EPS = 1e-05
        ATTN_EPS = 1e-06

        def layer_norm(x, g, b):
            mu = jnp.mean(x, axis=-1, keepdims=True)
            var = jnp.mean(jnp.square(x - mu), axis=-1, keepdims=True)
            return (x - mu) * jax.lax.rsqrt(var + LN_EPS) * g + b
        qkv = jnp.einsum('bsd,de->bse', x, Wqkv) + bqkv
        q, k, v = jnp.split(qkv, 3, axis=-1)
        qp = jax.nn.elu(q) + 1.0
        kp = jax.nn.elu(k) + 1.0
        kv = jnp.einsum('bsd,bse->bde', kp, v)
        num = jnp.einsum('bsd,bde->bse', qp, kv)
        k_sum = jnp.sum(kp, axis=1)
        den = jnp.einsum('bsd,bd->bs', qp, k_sum)[..., None]
        attn = num / (den + ATTN_EPS)
        x = layer_norm(x + attn, g1, b1)
        gate = jnp.einsum('bsd,dh->bsh', x, Wg) + bg
        up = jnp.einsum('bsd,dh->bsh', x, Wu) + bu
        ffn = jnp.einsum('bsh,hd->bsd', jax.nn.silu(gate) * up, Wd) + bd
        return layer_norm(x + ffn, g2, b2)

    def _L0_cond2_ref(x, mask, conditioning, Wq, Wk, Wv, Wo, rms_scale, Wc, bc):
        import jax, jax.numpy as jnp
        import numpy as np
        EPS = 1e-06
        B, S, E = x.shape
        H = 16
        D = E // H
        scale = D ** (-0.5)

        def proj(W):
            return (x @ W.T).reshape(B, S, H, D).transpose(0, 2, 1, 3)
        q, k, v = (proj(Wq), proj(Wk), proj(Wv))
        scores = jnp.einsum('bhsd,bhtd->bhst', q, k) * scale
        scores = jnp.where(mask[None, None, :, :], -jnp.inf, scores)
        attn = jax.nn.softmax(scores, axis=-1)
        out = jnp.einsum('bhst,bhtd->bhsd', attn, v)
        out = out.transpose(0, 2, 1, 3).reshape(B, S, E)
        out = out @ Wo.T
        rms = jnp.sqrt(jnp.mean(out * out, axis=-1, keepdims=True) + EPS)
        xn = out / rms * rms_scale
        mod = jax.nn.silu(conditioning) @ Wc.T + bc
        shift, sc = jnp.split(mod, 2, axis=-1)
        xn = xn * (1.0 + sc[:, None, :]) + shift[:, None, :]
        return xn

    def _L0_ffn_ref(x, gate_w, w_gate, w_up, w_down, sw_gate, sw_up, sw_down):
        import jax, jax.numpy as jnp
        import numpy as np
        B, L, D = (4, 256, 256)
        E, H, K = (16, 128, 8)
        EPS = 1e-12

        def _l2norm(v, axis=-1):
            n = jnp.sqrt(jnp.sum(v * v, axis=axis, keepdims=True))
            return v / jnp.maximum(n, EPS)
        if __name__ == '__main__':
            out = reference(**setup_inputs())
            print(out.shape)
        b, l, d = x.shape
        xf = x.reshape(-1, d)
        logits = _l2norm(xf) @ _l2norm(gate_w).T
        scores = jax.nn.sigmoid(logits)
        topk_scores, topk_idx = jax.lax.top_k(scores, K)
        topk_w = topk_scores / jnp.sum(topk_scores, axis=-1, keepdims=True)
        combine = jnp.sum(jax.nn.one_hot(topk_idx, E, dtype=xf.dtype) * topk_w[..., None], axis=1)
        g = jnp.einsum('nd,edh->neh', xf, w_gate)
        u = jnp.einsum('nd,edh->neh', xf, w_up)
        y = jnp.einsum('neh,ehd->ned', jax.nn.silu(g) * u, w_down)
        routed = jnp.einsum('ned,ne->nd', y, combine)
        shared = jax.nn.silu(xf @ sw_gate) * (xf @ sw_up) @ sw_down
        return (routed + shared).reshape(b, l, d)
    x = x + _L0_attn_ref(_L0_cond_ref(x, cond_256[:, None, :], L0_cond_rms_w, L0_cond_wg_W, L0_cond_wg_b, L0_cond_gg_W, L0_cond_gg_b, L0_cond_W1, L0_cond_b1, L0_cond_W2, L0_cond_b2, L0_cond_W3, L0_cond_b3), L0_attn_Wqkv, L0_attn_bqkv, L0_attn_Wg, L0_attn_bg, L0_attn_Wu, L0_attn_bu, L0_attn_Wd, L0_attn_bd, L0_attn_g1, L0_attn_b1, L0_attn_g2, L0_attn_b2)
    x = x + _L0_ffn_ref(_L0_cond2_ref(x, mask_SxS_bk1, cond_256, L0_cond2_Wq, L0_cond2_Wk, L0_cond2_Wv, L0_cond2_Wo, L0_cond2_rms_scale, L0_cond2_Wc, L0_cond2_bc), L0_ffn_gate_w, L0_ffn_w_gate, L0_ffn_w_up, L0_ffn_w_down, L0_ffn_sw_gate, L0_ffn_sw_up, L0_ffn_sw_down)
    return x

_drawn_inputs = setup_inputs


def setup_inputs(seed=0):
    import zlib

    import numpy as np

    out = dict(_drawn_inputs(seed))
    spreads = {'L0_cond_rms_w': (1.0, 0.2),
     'L0_cond_wg_b': (0.0, 0.1),
     'L0_cond_gg_b': (0.0, 0.1),
     'L0_cond_b1': (0.0, 0.1),
     'L0_cond_b2': (0.0, 0.1),
     'L0_cond_b3': (0.0, 0.1),
     'L0_attn_bqkv': (0.0, 0.1),
     'L0_attn_bg': (0.0, 0.497),
     'L0_attn_bu': (0.0, 0.542),
     'L0_attn_bd': (0.0, 0.1),
     'L0_attn_g1': (1.0, 0.2),
     'L0_attn_b1': (0.0, 0.1),
     'L0_attn_g2': (1.0, 0.2),
     'L0_attn_b2': (0.0, 0.1),
     'L0_cond2_rms_scale': (1.0, 0.2)}
    factors = {}
    for name, (base, spread) in spreads.items():
        noise = np.random.default_rng([zlib.crc32(name.encode()), seed]).standard_normal(out[name].shape)
        drawn = base * np.exp(spread * noise) if base else spread * noise
        out[name] = jnp.asarray(drawn.astype(out[name].dtype))
    for name, factor in factors.items():
        out[name] = (out[name] * factor).astype(out[name].dtype)
    return out
```

```python
from contextlib import ExitStack

import concourse.bass as bass
from concourse import mybir

ALU = mybir.AluOpType
ACT = mybir.ActivationFunctionType
F32 = mybir.dt.float32
F32R = mybir.dt.float32r
BF16 = mybir.dt.bfloat16
I32 = mybir.dt.int32
U32 = mybir.dt.uint32
U8 = mybir.dt.uint8
AX = mybir.AxisListType

P = 128
GT = 512
PASSES = ((0, 0), (0, 1), (1, 0))
MASKED = -1e30


class Chain:

    def __init__(self, eng, sem):
        self.eng, self.sem, self.base, self.k = eng, sem, 0, 0

    def on(self, eng):
        self.eng = eng
        return self

    def link(self, ins):
        self.k += 1
        ins.then_inc(self.sem, 1)
        self.eng.wait_ge(self.sem, self.base + self.k)


def adaln_block(nc, d, out):
    T, D = d["x"].shape
    B = d["cond"].shape[0]
    S = T // B
    C = d["cond"].shape[1]
    NT, KC, G = T // P, D // P, T // GT
    TG = GT // P
    NB = NT // B
    E1, _, M1 = d["W1"].shape
    MC = M1 // P
    F = d["Wg"].shape[1]
    FC = -(-F // P)
    FR = F - (FC - 1) * P
    E2, _, H2 = d["w_gate"].shape
    HD = 16
    NH = D // HD
    HC = NH // KC
    VW = HD + 2
    LW = D + 2
    QT = S // P

    with ExitStack() as ctx:
        def sem(name):
            return ctx.enter_context(nc.semaphore(name))

        def sb(name, shape, dt=F32):
            return ctx.enter_context(nc.sbuf_tensor(name, shape, dt))

        ps = [ctx.enter_context(nc.psum_tensor(f"bank{i}", [P, GT], F32)) for i in range(8)]
        ident = sb("ident", [P, P])
        act_hi = sb("act_hi", [P, KC, T], F32R)
        act_lo = sb("act_lo", [P, KC, T], F32R)
        actT = (act_hi, act_lo)
        y = sb("y", [P, NT, D])
        cw = sb("cw", [P, NT, E1])

        dve_chain = Chain(None, sem("dve_chain"))
        turned, hi_done, lo_done = sem("tr_turned"), sem("tr_hi"), sem("tr_lo")
        turns_done = [0]

        x_tok = d["x"].rearrange("(i p) d -> p i d", p=P)

        def transpose_stage(src):
            n0 = turns_done[0]
            turns_done[0] += KC * G
            with nc.Block() as block:
                @block.tensor
                def _(pe):
                    for u in range(KC * G):
                        k, g = u % KC, u // KC
                        if u >= 4:
                            pe.wait_ge(lo_done, n0 + u - 3)
                        for j in range(TG):
                            t = pe.transpose(ps[u % 4][:, j * P:(j + 1) * P],
                                             src[:, g * TG + j, k * P:(k + 1) * P], ident[:, :])
                        t.then_inc(turned, 1)

                @block.scalar
                def _(act):
                    for u in range(KC * G):
                        k, g = u % KC, u // KC
                        act.wait_ge(turned, n0 + u + 1)
                        act.activation(act_hi[:, k, g * GT:(g + 1) * GT], ps[u % 4][:, :],
                                       ACT.Copy).then_inc(hi_done, 1)

                @block.vector
                def _(dve):
                    for u in range(KC * G):
                        k, g = u % KC, u // KC
                        sl = slice(g * GT, (g + 1) * GT)
                        dve.wait_ge(hi_done, n0 + u + 1)
                        dve.tensor_tensor(act_lo[:, k, sl], ps[u % 4][:, :], act_hi[:, k, sl],
                                          ALU.subtract).then_inc(lo_done, 1)

        def norm_rows(chain, act_req, act_ack, n_done, var_ap, tmp, eps, scale=1.0):
            chain.link(chain.eng.tensor_scalar(tmp, var_ap, scale, eps, ALU.mult, ALU.add))
            chain.eng.tensor_copy(tmp, tmp).then_inc(act_req, 1)
            chain.eng.wait_ge(act_ack, n_done)
            chain.link(chain.eng.reciprocal(tmp, tmp))

        def stage_gate1():
            loaded, tok_in, w_in = [sem(f"g1_xT{g}") for g in range(G)], sem("g1_x"), sem("g1_w")
            idn = sem("g1_ident")
            wready, asplit = sem("g1_wready"), sem("g1_split")
            sq, logit, cbias = sem("g1_sq"), sem("g1_logit"), sem("g1_cbias")
            root_in, root, ein, eout = sem("g1_rootin"), sem("g1_root"), sem("g1_ein"), sem("g1_eout")
            with ExitStack() as st:
                def sbl(name, shape, dt=F32):
                    return st.enter_context(nc.sbuf_tensor(name, shape, dt))
                xT = sbl("g1_xTraw", [P, KC, T])
                xk = sbl("g1_xtok", [P, NT, D])
                junk = sbl("g1_junk", [P, D])
                wg = sbl("g1_wg", [P, KC, E1])
                rw = sbl("g1_rw", [P, KC])
                wgh, wgl = sbl("g1_wgh", [P, KC, E1], F32R), sbl("g1_wgl", [P, KC, E1], F32R)
                bia, bib = sbl("g1_ba", [P, E1]), sbl("g1_bb", [P, E1])
                gg = sbl("g1_gg", [C, E1])
                cT, cTb = sbl("g1_cT", [C, B]), sbl("g1_cTb", [C, B, P])
                ss, r = sbl("g1_ss", [P, NT]), sbl("g1_r", [P, NT])
                bb = sbl("g1_bias", [P, B, E1])
                z, w8 = sbl("g1_z", [P, NT, E1]), sbl("g1_w8", [P, NT, E1])
                mx, sm = sbl("g1_mx", [P, NT]), sbl("g1_sm", [P, NT])
                top, idx, idf = sbl("g1_top", [P, NT, 8]), sbl("g1_idx", [P, NT, 8], U32), sbl("g1_idf", [P, NT, 8])
                io, oh = sbl("g1_iota", [P, E1]), sbl("g1_oh", [P, NT, E1])
                block = st.enter_context(nc.Block())

                @block.sync
                def _(sp):
                    for g in range(G):
                        sp.dma_start(xT[:, :, g * GT:(g + 1) * GT],
                                     d["xT"].rearrange("(k p) t -> p k t", p=P)[:, :, g * GT:(g + 1) * GT]).then_inc(loaded[g], 16)
                    sp.dma_start(wg[:, :, :], d["wg_W"].rearrange("(k p) e -> p k e", p=P)).then_inc(w_in, 16)
                    sp.dma_start(rw[:, :], d["rms_w_cols"]).then_inc(w_in, 16)
                    sp.dma_start(bia[:, :], d["wg_b"].partition_broadcast(P)).then_inc(w_in, 16)
                    sp.dma_start(bib[:, :], d["gg_b"].partition_broadcast(P)).then_inc(w_in, 16)
                    sp.dma_start(gg[:, :], d["gg_W"]).then_inc(w_in, 16)
                    sp.dma_start(cT[:, :], d["condT"]).then_inc(w_in, 16)

                @block.gpsimd
                def _(pool):
                    pool.memset(ident[:, :], 0.0).then_inc(idn, 1)
                    pool.wait_ge(idn, 1)
                    pool.affine_select(out=ident[:, :], in_=ident[:, :], compare_op=ALU.not_equal, fill=1.0,
                                       base=0, pattern=[[-1, P]], channel_multiplier=1).then_inc(idn, 1)
                    pool.iota(io[:, :], pattern=[[1, E1]], base=0, channel_multiplier=0,
                              allow_small_or_imprecise_dtypes=True).then_inc(idn, 1)

                @block.scalar
                def _(act):
                    act.dma_start(xk[:, :, :], x_tok).then_inc(tok_in, 16)
                    act.wait_ge(tok_in, 16)
                    for i in range(NT):
                        if i:
                            act.wait_ge(sq, i)
                        act.activation(junk[:, :], xk[:, i, :], ACT.Square,
                                       accum_out=ss[:, i:i + 1]).then_inc(sq, 1)
                    act.wait_ge(root_in, 1)
                    act.activation(r[:, :], r[:, :], ACT.Sqrt).then_inc(root, 1)
                    act.wait_ge(ein, 1)
                    act.activation(w8[:, :, :], z[:, :, :], ACT.Exp).then_inc(eout, 1)

                @block.vector
                def _(dve):
                    ch = dve_chain.on(dve)
                    dve.wait_ge(w_in, 96)
                    for k in range(KC):
                        ch.link(dve.tensor_scalar(wg[:, k, :], wg[:, k, :], rw[:, k:k + 1], None, ALU.mult))
                    ch.link(dve.tensor_copy(wgh[:, :, :], wg[:, :, :]))
                    dve.tensor_tensor(wgl[:, :, :], wg[:, :, :], wgh[:, :, :], ALU.subtract).then_inc(wready, 1)
                    dve.tensor_copy(cTb[:, :, :], cT[:, :].unsqueeze(2).to_broadcast([C, B, P])).then_inc(wready, 1)
                    ch.link(dve.tensor_tensor(bia[:, :], bia[:, :], bib[:, :], ALU.add))
                    for g in range(G):
                        sl = slice(g * GT, (g + 1) * GT)
                        dve.wait_ge(loaded[g], 16)
                        ch.link(dve.tensor_copy(act_hi[:, :, sl], xT[:, :, sl]))
                        dve.tensor_tensor(act_lo[:, :, sl], xT[:, :, sl], act_hi[:, :, sl],
                                          ALU.subtract).then_inc(asplit, 1)
                    dve.wait_ge(sq, NT)
                    norm_rows(ch, root_in, root, 1, ss[:, :], r[:, :], 1e-6, 1.0 / D)
                    dve.wait_ge(cbias, 1)
                    ch.link(dve.tensor_tensor(bb[:, :, :], ps[1][:, 0:B * E1].rearrange("p (b e) -> p b e", b=B),
                                              bia[:, :].unsqueeze(1).to_broadcast([P, B, E1]), ALU.add))
                    dve.wait_ge(logit, 1)
                    ch.link(dve.tensor_tensor(z[:, :, :], ps[0][:, 0:NT * E1].rearrange("p (i e) -> p i e", i=NT),
                                              r[:, :].unsqueeze(2).to_broadcast([P, NT, E1]), ALU.mult))
                    for b in range(B):
                        ch.link(dve.tensor_tensor(z[:, b * NB:(b + 1) * NB, :], z[:, b * NB:(b + 1) * NB, :],
                                                  bb[:, b, :].unsqueeze(1).to_broadcast([P, NB, E1]), ALU.add))
                    ch.link(dve.tensor_reduce(mx[:, :], z[:, :, :], AX.X, ALU.max))
                    dve.tensor_tensor(z[:, :, :], z[:, :, :], mx[:, :].unsqueeze(2).to_broadcast([P, NT, E1]),
                                      ALU.subtract).then_inc(ein, 1)
                    dve.wait_ge(eout, 1)
                    ch.link(dve.tensor_reduce(sm[:, :], w8[:, :, :], AX.X, ALU.add))
                    ch.link(dve.reciprocal(sm[:, :], sm[:, :]))
                    ch.link(dve.tensor_tensor(w8[:, :, :], w8[:, :, :],
                                              sm[:, :].unsqueeze(2).to_broadcast([P, NT, E1]), ALU.mult))
                    for i in range(NT):
                        last = dve.max(top[:, i, :], w8[:, i, :])
                    ch.link(last)
                    for i in range(NT):
                        last = dve.max_index(idx[:, i, :], top[:, i, :], w8[:, i, :])
                    ch.link(last)
                    ch.link(dve.tensor_copy(idf[:, :, :], idx[:, :, :]))
                    dve.wait_ge(idn, 3)
                    for n in range(2):
                        ch.link(dve.tensor_tensor(oh[:, :, :], io[:, :].unsqueeze(1).to_broadcast([P, NT, E1]),
                                                  idf[:, :, n:n + 1].to_broadcast([P, NT, E1]), ALU.is_equal))
                        dst = cw if n == 0 else oh
                        ch.link(dve.tensor_tensor(dst[:, :, :], oh[:, :, :],
                                                  top[:, :, n:n + 1].to_broadcast([P, NT, E1]), ALU.mult))
                    ch.link(dve.tensor_tensor(cw[:, :, :], cw[:, :, :], oh[:, :, :], ALU.add))

                @block.tensor
                def _(pe):
                    pe.wait_ge(wready, 2)
                    for b in range(B):
                        last = pe.matmul(ps[1][:, b * E1:(b + 1) * E1], cTb[:, b, :], gg[:, :], start=True, stop=True)
                    last.then_inc(cbias, 1)
                    w2 = (wgh, wgl)
                    for i in range(NT):
                        if i % TG == 0:
                            pe.wait_ge(asplit, i // TG + 1)
                        for n, (k, (a, b)) in enumerate((k, p) for k in range(KC) for p in PASSES):
                            last = pe.matmul(ps[0][:, i * E1:(i + 1) * E1], actT[a][:, k, i * P:(i + 1) * P],
                                             w2[b][:, k, :], start=n == 0, stop=n == 3 * KC - 1)
                    last.then_inc(logit, 1)

        def stage_experts1():
            b3_in, b_in = sem("e1_b3in"), sem("e1_bin")
            win, wsp, dch = [sem(f"e1_win{n}") for n in range(3)], sem("e1_wsplit"), sem("e1_dve")
            h_ps, evac, h_hi, h_s = sem("e1_hps"), sem("e1_evac"), sem("e1_hhi"), sem("e1_hsplit")
            o_ps, o_used, cwt, b3d = sem("e1_ops"), sem("e1_oused"), sem("e1_cwt"), sem("e1_b3")
            O2, O3 = KC * M1, KC * M1 + MC * M1
            NW = O3 + MC * D
            PARTS = ((0, O2, KC), (O2, O3, MC), (O3, NW, MC))
            CH = 2 * MC
            NS = 2 * G
            NT0 = NT + 0
            with ExitStack() as st:
                def sbl(name, shape, dt=F32):
                    return st.enter_context(nc.sbuf_tensor(name, shape, dt))
                raw = sbl("e1_raw", [P, NW])
                w = [[sbl(f"e1_w{p}{h}", [P, NW], F32R) for h in "hl"] for p in range(2)]
                h1 = [sbl(f"e1_h1{h}", [P, MC, GT], F32R) for h in "hl"]
                h2 = [sbl(f"e1_h2{h}", [P, MC, GT], F32R) for h in "hl"]
                u = sbl("e1_u", [P, 4, GT])
                rawb, bias = sbl("e1_rawb", [P, 2, MC]), sbl("e1_bias", [P, 2, 2, MC])
                b3s, cwT = sbl("e1_b3s", [E1, D]), sbl("e1_cwT", [E1, T])
                block = st.enter_context(nc.Block())

                def turns(eng, body):
                    with eng.Fori(0, E1 // 2 - 1) as t:
                        body(t, False)
                    body(E1 // 2 - 1, True)

                @block.sync
                def _(sp):
                    sp.dma_start(b3s[:, :], d["b3"]).then_inc(b3_in, 16)

                    def load(e, wait):
                        for n, (name, (o, o_end, c)) in enumerate(zip(("W1", "W2", "W3"), PARTS)):
                            if wait:
                                sp.wait_ge(wsp, 3 * e + n - 2)
                            src = d[name].rearrange("e (c p) n -> p e c n", p=P)[:, bass.ds(e, 1), :, :]
                            sp.dma_start(raw[:, o:o_end].rearrange("p (a c n) -> p a c n", a=1, c=c),
                                         src).then_inc(win[n], 16)
                            if n == 0:
                                for m in range(2):
                                    sp.dma_start(rawb[:, m:m + 1, :],
                                                 d[f"b{m + 1}_cols"][:, bass.ds(e, 1), :]).then_inc(b_in, 16)
                    load(0, False)
                    with sp.Fori(1, E1) as e:
                        load(e, True)

                @block.tensor
                def _(pe):
                    for g in range(G):
                        for j in range(TG):
                            last = pe.transpose(ps[4 + g][0:E1, j * P:(j + 1) * P], cw[:, g * TG + j, :], ident[:, :])
                        last.then_inc(cwt, 1)
                    pe.wait_ge(o_used, G)
                    pe.wait_ge(b3_in, 16)
                    for i in range(NT):
                        if i >= 4:
                            pe.wait_ge(evac, i - 3)
                        pe.matmul(ps[i % 4][:, 0:D], cwT[:, i * P:(i + 1) * P], b3s[:, :],
                                  start=True, stop=True).then_inc(b3d, 1)

                    def hidden(wt, o, kc, src, tok, number, deps):
                        for m in range(MC):
                            pe.wait_ge(evac, NT + number + m - 3)
                            for k in range(kc):
                                if deps is not None and m == 0:
                                    pe.wait_ge(h_s, 4 + deps + k + 1)
                                for n, (a, b) in enumerate(PASSES):
                                    last = pe.matmul(ps[m % 4][:, :],
                                                     wt[a][:, o + k * M1 + m * P:o + k * M1 + (m + 1) * P],
                                                     src[b][:, k, tok], start=k + n == 0,
                                                     stop=k == kc - 1 and n == 2)
                            last.then_inc(h_ps, 1)

                    def layer3(wt, number, tiles):
                        pe.wait_ge(h_s, 4 + number + MC)
                        for j in range(TG):
                            pe.wait_ge(o_used, tiles + j + 1)
                            for n, (k, (a, b)) in enumerate((k, p) for k in range(MC) for p in PASSES):
                                last = pe.matmul(ps[4 + j][:, 0:D], h2[a][:, k, j * P:(j + 1) * P],
                                                 wt[b][:, O3 + k * D:O3 + (k + 1) * D],
                                                 start=n == 0, stop=n == 3 * MC - 1)
                            last.then_inc(o_ps, 1)

                    def body(t, _):
                        for s in range(NS):
                            par, g = s // G, s % G
                            number = (t * NS + s) * CH
                            if g == 0:
                                pe.wait_ge(wsp, (2 * t + par + 1) * 3)
                            hidden(w[par], 0, KC, actT, slice(g * GT, (g + 1) * GT), number, None)
                            if s:
                                layer3(w[(s - 1) // G], number - MC, (t * NS + s - 1) * TG)
                            hidden(w[par], O2, MC, h1, slice(0, GT), number + MC, number)
                        layer3(w[1], (t + 1) * NS * CH - MC, ((t + 1) * NS - 1) * TG)
                    turns(pe, body)

                @block.scalar
                def _(act):
                    for i in range(NT):
                        act.wait_ge(b3d, i + 1)
                        act.activation(y[:, i, :], ps[i % 4][:, 0:D], ACT.Copy).then_inc(evac, 1)

                    def body(t, _):
                        for s in range(NS):
                            par = s // G
                            if s % G == 0:
                                act.wait_ge(wsp, (2 * t + par + 1) * 3)
                            for c in range(CH):
                                number = (t * NS + s) * CH + c
                                act.wait_ge(h_ps, number + 1)
                                act.wait_ge(h_s, number + 1)
                                act.activation(u[:, c % 4, :], ps[c % 4][:, :], ACT.Relu,
                                               bias=bias[:, par, c // MC, c % MC:c % MC + 1])\
                                   .then_inc(evac, 1)
                    turns(act, body)

                @block.gpsimd
                def _(pool):
                    for c in range(4):
                        pool.memset(u[:, c, :], 0.0).then_inc(h_s, 1)

                    def body(t, _):
                        for s in range(NS):
                            for c in range(CH):
                                number = (t * NS + s) * CH + c
                                h = (h1, h2)[c // MC]
                                pool.wait_ge(h_hi, number + 1)
                                pool.tensor_tensor(h[1][:, c % MC, :], u[:, c % 4, :], h[0][:, c % MC, :],
                                                   ALU.subtract).then_inc(h_s, 1)
                    turns(pool, body)

                @block.vector
                def _(dve):
                    ch = Chain(dve, dch)
                    for g in range(G):
                        dve.wait_ge(cwt, g + 1)
                        dve.tensor_copy(cwT[:, g * GT:(g + 1) * GT], ps[4 + g][0:E1, :]).then_inc(o_used, 1)

                    def split_weights(par, e, n):
                        o, o_end, _ = PARTS[n]
                        dve.wait_ge(win[n], 16 * (e + 1))
                        if n == 0:
                            dve.wait_ge(b_in, 32 * (e + 1))
                            ch.link(dve.tensor_copy(bias[:, par, :, :], rawb[:, :, :]))
                        ch.link(dve.tensor_copy(w[par][0][:, o:o_end], raw[:, o:o_end]))
                        dve.tensor_tensor(w[par][1][:, o:o_end], raw[:, o:o_end], w[par][0][:, o:o_end],
                                          ALU.subtract).then_inc(wsp, 1)

                    for n in range(3):
                        split_weights(0, 0, n)
                    before = ch.k

                    def hi(number, c):
                        h = (h1, h2)[c // MC]
                        dve.wait_ge(evac, NT + number + c + 1)
                        dve.tensor_copy(h[0][:, c % MC, :], u[:, c % 4, :]).then_inc(h_hi, 1)

                    def add_tiles(t, s):
                        g = s % G
                        tiles = (t * NS + s) * TG
                        dve.wait_ge(o_used, tiles + TG)
                        for j in range(TG):
                            i = g * TG + j
                            dve.wait_ge(o_ps, tiles + j + 1)
                            dve.scalar_tensor_tensor(out=y[:, i, :], in0=ps[4 + j][:, 0:D],
                                                     scalar=cw[:, i, bass.ds(2 * t + s // G, 1)],
                                                     in1=y[:, i, :], op0=ALU.mult, op1=ALU.add)\
                               .then_inc(o_used, 1)

                    def body(t, last):
                        ch.base, ch.k = before + t * 2 * 4, 0
                        for s in range(NS):
                            par, g = s // G, s % G
                            number = (t * NS + s) * CH
                            if g and not (last and par):
                                split_weights(1 - par, 2 * t + par + 1, g - 1)
                            for c in range(MC):
                                hi(number, c)
                            if s:
                                add_tiles(t, s - 1)
                            for c in range(MC, CH):
                                hi(number, c)
                        add_tiles(t, NS - 1)
                    turns(dve, body)

        def weights_split(dve, ch, pairs, done):
            for raw, hi, lo in pairs:
                ch.link(dve.tensor_copy(hi, raw))
                dve.tensor_tensor(lo, raw, hi, ALU.subtract).then_inc(done, 1)

        def stage_linear_attention():
            kvh = [ctx.enter_context(nc.sbuf_tensor(f"la_kv{h}", [P, B, KC, LW], F32R)) for h in "hl"]
            w_in, wsp = sem("la_win"), sem("la_wsplit")
            qps, qu, qm, qe = sem("la_qps"), sem("la_qu"), sem("la_qm"), sem("la_qe")
            kps, kt, ke, ks = sem("la_kps"), sem("la_kt"), sem("la_ke"), sem("la_ks")
            kvps, kvs, ones = sem("la_kvps"), sem("la_kvs"), sem("la_ones")
            with ExitStack() as st:
                def sbl(name, shape, dt=F32):
                    return st.enter_context(nc.sbuf_tensor(name, shape, dt))
                raw = sbl("la_raw", [P, KC, 3 * D])
                w = [sbl(f"la_w{h}", [P, KC, 3 * D], F32R) for h in "hl"]
                bq, bkv = sbl("la_bq", [P, KC]), sbl("la_bkv", [P, 2 * D])
                qu_sb, qe_sb = sbl("la_qusb", [P, 2, GT]), sbl("la_qesb", [P, 2, GT])
                kv32, kme = sbl("la_kv32", [P, 2, 2 * D]), sbl("la_kme", [P, 2, D])
                kt_s = [[sbl(f"la_kt{p}{h}", [P, 2 * D + 2], F32R) for h in "hl"] for p in range(2)]
                block = st.enter_context(nc.Block())
                NQ = KC * G

                @block.sync
                def _(sp):
                    sp.dma_start(raw[:, :, :], d["Wqkv"].rearrange("(k p) n -> p k n", p=P)).then_inc(w_in, 16)
                    sp.dma_start(bq[:, :], d["bq_cols"]).then_inc(w_in, 16)
                    sp.dma_start(bkv[:, :], d["bqkv"][D:3 * D].partition_broadcast(P)).then_inc(w_in, 16)

                @block.tensor
                def _(pe):
                    pe.wait_ge(wsp, 1)
                    for n in range(NQ):
                        m, g = n % KC, n // KC
                        if n >= 2:
                            pe.wait_ge(qu, n - 1)
                        for i, (k, (a, b)) in enumerate((k, p) for k in range(KC) for p in PASSES):
                            last = pe.matmul(ps[n % 2][:, :], w[a][:, k, m * P:(m + 1) * P],
                                             actT[b][:, k, g * GT:(g + 1) * GT], start=i == 0, stop=i == 3 * KC - 1)
                        last.then_inc(qps, 1)

                    def project(i):
                        if i >= 2:
                            pe.wait_ge(kt, i - 1)
                        for n, (k, (a, b)) in enumerate((k, p) for k in range(KC) for p in PASSES):
                            last = pe.matmul(ps[2 + i % 2][:, :], actT[a][:, k, i * P:(i + 1) * P],
                                             w[b][:, k, D:3 * D], start=n == 0, stop=n == 3 * KC - 1)
                        last.then_inc(kps, 1)

                    project(0)
                    for i in range(NT):
                        if i + 1 < NT:
                            project(i + 1)
                        pe.wait_ge(ks, i + 1)
                        b0, first, fin = i // NB, i % NB == 0, i % NB == NB - 1
                        if i == 0:
                            pe.wait_ge(ones, 6)
                        for c in range(KC):
                            for n, (a, b) in enumerate(PASSES):
                                last = pe.matmul(ps[4 + 2 * (b0 % 2) + c][:, 0:LW], kt_s[i % 2][a][:, c * P:(c + 1) * P],
                                                 kt_s[i % 2][b][:, D:D + LW], start=first and n == 0,
                                                 stop=fin and n == 2)
                        last.then_inc(kvps, 1)

                @block.scalar
                def _(act):
                    act.wait_ge(w_in, 48)
                    for n in range(NQ):
                        act.wait_ge(qps, n + 1)
                        if n >= 2:
                            act.wait_ge(qe, n - 1)
                        act.activation(qu_sb[:, n % 2, :], ps[n % 2][:, :], ACT.Identity,
                                       bias=bq[:, n % KC:n % KC + 1]).then_inc(qu, 1)
                        act.wait_ge(qm, 2 * n + 1)
                        act.activation(qe_sb[:, n % 2, :], qe_sb[:, n % 2, :], ACT.Exp).then_inc(qm, 1)
                    for i in range(NT):
                        act.wait_ge(ke, 2 * i + 1)
                        act.activation(kme[:, i % 2, :], kme[:, i % 2, :], ACT.Exp).then_inc(ke, 1)

                @block.gpsimd
                def _(pool):
                    for p_ in range(2):
                        pool.memset(kt_s[p_][0][:, 2 * D:2 * D + 2].bitcast(F32), 0.0).then_inc(ones, 1)
                        pool.memset(kt_s[p_][1][:, 2 * D:2 * D + 2].bitcast(F32), 0.0).then_inc(ones, 1)
                    pool.wait_ge(ones, 4)
                    for p_ in range(2):
                        pool.memset(kt_s[p_][0][:, 2 * D:2 * D + 1].bitcast(F32), 1.0).then_inc(ones, 1)

                @block.vector
                def _(dve):
                    ch = dve_chain.on(dve)
                    dve.wait_ge(w_in, 48)
                    weights_split(dve, ch, [(raw[:, :, :], w[0][:, :, :], w[1][:, :, :])], wsp)
                    for n in range(NQ):
                        m, g = n % KC, n // KC
                        sl = slice(g * GT, (g + 1) * GT)
                        dve.wait_ge(qu, n + 1)
                        dve.tensor_scalar(qe_sb[:, n % 2, :], qu_sb[:, n % 2, :], 0.0, None, ALU.min).then_inc(qm, 1)
                        dve.wait_ge(qm, 2 * n + 2)
                        ch.link(dve.scalar_tensor_tensor(out=qu_sb[:, n % 2, :], in0=qu_sb[:, n % 2, :], scalar=0.0,
                                                         in1=qe_sb[:, n % 2, :], op0=ALU.max, op1=ALU.add))
                        ch.link(dve.tensor_copy(qp[0][:, m, sl], qu_sb[:, n % 2, :]))
                        dve.tensor_tensor(qp[1][:, m, sl], qu_sb[:, n % 2, :], qp[0][:, m, sl],
                                          ALU.subtract).then_inc(qe, 1)
                        dve.wait_ge(qe, n + 1)
                    for i in range(NT):
                        s_ = i % 2
                        dve.wait_ge(kps, i + 1)
                        dve.tensor_tensor(kv32[:, s_, :], ps[2 + s_][:, :], bkv[:, :], ALU.add).then_inc(kt, 1)
                        dve.wait_ge(kt, i + 1)
                        dve.tensor_scalar(kme[:, s_, :], kv32[:, s_, 0:D], 0.0, None, ALU.min).then_inc(ke, 1)
                        dve.wait_ge(ke, 2 * i + 2)
                        ch.link(dve.scalar_tensor_tensor(out=kv32[:, s_, 0:D], in0=kv32[:, s_, 0:D], scalar=0.0,
                                                         in1=kme[:, s_, :], op0=ALU.max, op1=ALU.add))
                        if i >= 2:
                            dve.wait_ge(kvps, i - 1)
                        ch.link(dve.tensor_copy(kt_s[s_][0][:, 0:2 * D], kv32[:, s_, :]))
                        dve.tensor_tensor(kt_s[s_][1][:, 0:2 * D], kv32[:, s_, :], kt_s[s_][0][:, 0:2 * D],
                                          ALU.subtract).then_inc(ks, 1)
                        dve.wait_ge(ks, i + 1)
                    for b in range(B):
                        dve.wait_ge(kvps, (b + 1) * NB)
                        for c in range(KC):
                            bank = ps[4 + 2 * (b % 2) + c][:, 0:LW]
                            ch.link(dve.tensor_copy(kvh[0][:, b, c, :], bank))
                            ch.link(dve.tensor_tensor(kvh[1][:, b, c, :], bank, kvh[0][:, b, c, :], ALU.subtract))
            return kvh

        def layer_norm(ch, dve, act_sems, src, stats, mv, rstd, gb, n_done, eps=1e-5):
            req, ack = act_sems
            for i in range(NT):
                last = dve.bn_stats(stats[:, i, :], src[:, i, :])
            ch.link(last)
            for i in range(NT):
                last = dve.bn_aggr(mv[:, i, :], stats[:, i, :])
            ch.link(last)
            norm_rows(ch, req, ack, n_done, mv[:, :, 1], rstd[:, :], eps)
            for i in range(NT):
                last = dve.tensor_scalar(src[:, i, :], src[:, i, :], mv[:, i, 0:1], rstd[:, i:i + 1],
                                         ALU.subtract, ALU.mult)
            ch.link(last)
            for n, op in enumerate((ALU.mult, ALU.add)):
                ch.link(dve.tensor_tensor(src[:, :, :], src[:, :, :],
                                          gb[:, n, :].unsqueeze(1).to_broadcast([P, NT, D]), op))

        def stage_linear_out(kvh):
            nps, nuse = sem("lo_ps"), sem("lo_used")
            req, ack, gin = sem("lo_req"), sem("lo_ack"), sem("lo_gin")
            with ExitStack() as st:
                def sbl(name, shape, dt=F32):
                    return st.enter_context(nc.sbuf_tensor(name, shape, dt))
                den = sbl("lo_den", [P, NT])
                stats, mv, rstd = sbl("lo_stats", [P, NT, 6]), sbl("lo_mv", [P, NT, 2]), sbl("lo_rstd", [P, NT])
                gb = sbl("lo_gb", [P, 2, D])
                block = st.enter_context(nc.Block())

                @block.sync
                def _(sp):
                    for n, name in enumerate(("g1", "be1")):
                        sp.dma_start(gb[:, n, :], d[name].partition_broadcast(P)).then_inc(gin, 16)

                @block.tensor
                def _(pe):
                    for i in range(NT):
                        if i >= 4:
                            pe.wait_ge(nuse, i - 3)
                        for n, (c, (a, b)) in enumerate((c, p) for c in range(KC) for p in PASSES):
                            last = pe.matmul(ps[i % 4][:, 0:LW], qp[a][:, c, i * P:(i + 1) * P],
                                             kvh[b][:, i // NB, c, :], start=n == 0, stop=n == 3 * KC - 1)
                        last.then_inc(nps, 1)

                @block.scalar
                def _(act):
                    act.wait_ge(req, 1)
                    act.activation(rstd[:, :], rstd[:, :], ACT.Sqrt).then_inc(ack, 1)

                @block.vector
                def _(dve):
                    ch = dve_chain.on(dve)
                    for i in range(NT):
                        dve.wait_ge(nps, i + 1)
                        ch.link(dve.tensor_scalar(den[:, i:i + 1], ps[i % 4][:, D:D + 1], 1e-6, None, ALU.add))
                        ch.link(dve.reciprocal(den[:, i:i + 1], den[:, i:i + 1]))
                        dve.scalar_tensor_tensor(out=y[:, i, :], in0=ps[i % 4][:, 0:D], scalar=den[:, i:i + 1],
                                                 in1=y[:, i, :], op0=ALU.mult, op1=ALU.add).then_inc(nuse, 1)
                    dve.wait_ge(nuse, NT)
                    dve.wait_ge(gin, 32)
                    layer_norm(ch, dve, (req, ack), y, stats, mv, rstd, gb, 1)

        def stage_feed_forward():
            w_in, wsp = sem("ff_win"), sem("ff_wsplit")
            hps, sil, hsp, hhi = sem("ff_hps"), sem("ff_silu"), sem("ff_hsplit"), sem("ff_hhi")
            h32d, ops, used = sem("ff_h32"), sem("ff_ops"), sem("ff_used")
            req, ack, gin = sem("ff_req"), sem("ff_ack"), sem("ff_gin")
            padded = sem("ff_padded")
            with ExitStack() as st:
                def sbl(name, shape, dt=F32):
                    return st.enter_context(nc.sbuf_tensor(name, shape, dt))
                raw = sbl("ff_raw", [P, KC, F])
                wg = [sbl(f"ff_wg{h}", [P, KC, FC * P], F32R) for h in "hl"]
                wu = [sbl(f"ff_wu{h}", [P, KC, FC * P], F32R) for h in "hl"]
                wd = [sbl(f"ff_wd{h}", [P, FC, D], F32R) for h in "hl"]
                bg, bu = sbl("ff_bg", [P, FC]), sbl("ff_bu", [P, FC])
                sl_sb, h32 = sbl("ff_silusb", [P, 2, GT]), sbl("ff_h32sb", [P, 2, GT])
                hh = [sbl(f"ff_h{h}", [P, FC, GT], F32R) for h in "hl"]
                gb = sbl("ff_gb", [P, 3, D])
                stats, mv, rstd = sbl("ff_stats", [P, NT, 6]), sbl("ff_mv", [P, NT, 2]), sbl("ff_rstd", [P, NT])
                block = st.enter_context(nc.Block())

                @block.sync
                def _(sp):
                    sp.wait_ge(padded, 2)
                    sp.dma_start(raw[:, :, :], d["Wg"].rearrange("(k p) n -> p k n", p=P)).then_inc(w_in, 16)
                    for v, s_ in ((bg, "bg"), (bu, "bu")):
                        sp.dma_start(v[:, 0:FC - 1], d[s_ + "_cols"]).then_inc(gin, 16)
                        sp.dma_start(v[0:FR, FC - 1:FC], d[s_][(FC - 1) * P:F].rearrange("(p a) -> p a", a=1), allow_slow_non_contiguous=True).then_inc(gin, 16)
                    for n, name in enumerate(("g2", "be2", "bd")):
                        sp.dma_start(gb[:, n, :], d[name].partition_broadcast(P)).then_inc(gin, 16)
                    sp.wait_ge(wsp, 1)
                    sp.dma_start(raw[:, :, :], d["Wu"].rearrange("(k p) n -> p k n", p=P)).then_inc(w_in, 16)
                    sp.wait_ge(wsp, 2)
                    rawd = raw[:, :, :].rearrange("p k n -> p (k n)")
                    sp.dma_start(rawd[:, 0:(FC - 1) * D].rearrange("p (c n) -> p c n", n=D),
                                 d["Wd"][0:(FC - 1) * P].rearrange("(c p) n -> p c n", p=P)).then_inc(w_in, 16)
                    sp.wait_ge(wsp, 3)
                    sp.dma_start(rawd[0:FR, 0:D], d["Wd"][(FC - 1) * P:F]).then_inc(w_in, 16)

                @block.tensor
                def _(pe):
                    def up(s):
                        g, m = s // FC, s % FC
                        for v, (wt, bank) in enumerate(((wg, ps[s % 2]), (wu, ps[2 + s % 2]))):
                            if s == 0:
                                pe.wait_ge(wsp, v + 1)
                            if s >= 2:
                                pe.wait_ge((sil, h32d)[v], s - 1)
                            for n, (k, (a, b)) in enumerate((k, p) for k in range(KC) for p in PASSES):
                                last = pe.matmul(bank[:, :], wt[a][:, k, m * P:(m + 1) * P],
                                                 actT[b][:, k, g * GT:(g + 1) * GT], start=n == 0,
                                                 stop=n == 3 * KC - 1)
                            last.then_inc(hps, 1)

                    def down(g):
                        if g == 0:
                            pe.wait_ge(wsp, 4)
                        pe.wait_ge(hsp, (g + 1) * FC)
                        for j in range(TG):
                            i = g * TG + j
                            if i >= 4:
                                pe.wait_ge(used, i - 3)
                            for n, (m, (a, b)) in enumerate((m, p) for m in range(FC) for p in PASSES):
                                last = pe.matmul(ps[4 + j][:, 0:D], hh[a][:, m, j * P:(j + 1) * P],
                                                 wd[b][:, m, :], start=n == 0, stop=n == 3 * FC - 1)
                            last.then_inc(ops, 1)

                    up(0)
                    for g in range(G):
                        for m in range(1, FC):
                            up(g * FC + m)
                        if g + 1 < G:
                            up((g + 1) * FC)
                        down(g)

                @block.scalar
                def _(act):
                    act.wait_ge(gin, 16 * 7)
                    for s in range(G * FC):
                        m = s % FC
                        act.wait_ge(hps, 2 * s + 1)
                        if s >= 2:
                            act.wait_ge(h32d, s - 1)
                        act.activation(sl_sb[:, s % 2, :], ps[s % 2][:, :], ACT.Silu,
                                       bias=bg[:, m:m + 1]).then_inc(sil, 1)
                    act.wait_ge(req, 1)
                    act.activation(rstd[:, :], rstd[:, :], ACT.Sqrt).then_inc(ack, 1)

                @block.gpsimd
                def _(pool):
                    pool.memset(bg[:, FC - 1:FC], 0.0).then_inc(padded, 1)
                    pool.memset(bu[:, FC - 1:FC], 0.0).then_inc(padded, 1)
                    for s in range(G * FC):
                        m = s % FC
                        pool.wait_ge(hhi, s + 1)
                        pool.tensor_tensor(hh[1][:, m, :], h32[:, s % 2, :], hh[0][:, m, :],
                                           ALU.subtract).then_inc(hsp, 1)

                @block.vector
                def _(dve):
                    ch = dve_chain.on(dve)
                    for part in range(2):
                        for wt in (wg, wu):
                            dve.memset(wt[part][:, :, F:FC * P].bitcast(F32), 0.0)
                        last = dve.memset(wd[part][:, FC - 1, :].bitcast(F32), 0.0)
                    ch.link(last)
                    for n, (wt) in enumerate((wg, wu)):
                        dve.wait_ge(w_in, 16 * (n + 1))
                        weights_split(dve, ch, [(raw[:, :, :], wt[0][:, :, 0:F], wt[1][:, :, 0:F])], wsp)
                    rawd = raw[:, :, :].rearrange("p k n -> p (k n)")
                    dve.wait_ge(w_in, 48)
                    weights_split(dve, ch, [(rawd[:, 0:(FC - 1) * D], wd[0][:, 0:FC - 1, :].rearrange("p c n -> p (c n)"),
                                             wd[1][:, 0:FC - 1, :].rearrange("p c n -> p (c n)"))], wsp)
                    dve.wait_ge(w_in, 64)
                    weights_split(dve, ch, [(rawd[0:FR, 0:D], wd[0][0:FR, FC - 1, :], wd[1][0:FR, FC - 1, :])], wsp)
                    dve.wait_ge(gin, 16 * 7)
                    ch.link(dve.tensor_tensor(y[:, :, :], y[:, :, :],
                                              gb[:, 2, :].unsqueeze(1).to_broadcast([P, NT, D]), ALU.add))

                    def hidden(s):
                        m = s % FC
                        dve.wait_ge(sil, s + 1)
                        dve.wait_ge(hps, 2 * s + 2)
                        if s >= 2:
                            dve.wait_ge(hsp, s - 1)
                        dve.scalar_tensor_tensor(out=h32[:, s % 2, :], in0=ps[2 + s % 2][:, :],
                                                 scalar=bu[:, m:m + 1], in1=sl_sb[:, s % 2, :],
                                                 op0=ALU.add, op1=ALU.mult).then_inc(h32d, 1)
                        dve.wait_ge(h32d, s + 1)
                        if s >= FC:
                            dve.wait_ge(ops, (s // FC) * TG)
                        dve.tensor_copy(hh[0][:, m, :], h32[:, s % 2, :]).then_inc(hhi, 1)

                    def add(g):
                        for j in range(TG):
                            i = g * TG + j
                            dve.wait_ge(ops, i + 1)
                            dve.tensor_tensor(y[:, i, :], ps[4 + j][:, 0:D], y[:, i, :], ALU.add).then_inc(used, 1)

                    for g in range(G):
                        for m in range(FC):
                            hidden(g * FC + m)
                        add(g)
                    dve.wait_ge(used, NT)
                    layer_norm(ch, dve, (req, ack), y, stats, mv, rstd, gb, 1)

        def stage_residual():
            xin, radd = [sem(f"re_x{g}") for g in range(G)], sem("re_add")
            with ExitStack() as st:
                xk = st.enter_context(nc.sbuf_tensor("re_xtok", [P, NT, D], F32))
                block = st.enter_context(nc.Block())

                @block.sync
                def _(sp):
                    for g in range(G):
                        sp.dma_start(xk[:, g * TG:(g + 1) * TG, :], x_tok[:, g * TG:(g + 1) * TG, :]).then_inc(xin[g], 16)

                @block.vector
                def _(dve):
                    for g in range(G):
                        sl = slice(g * TG, (g + 1) * TG)
                        dve.wait_ge(xin[g], 16)
                        dve.tensor_tensor(y[:, sl, :], y[:, sl, :], xk[:, sl, :], ALU.add).then_inc(radd, 1)

        def stage_project(kT, v_tok, n_live, live_at, mbias, pen, onesb, identb):
            w_in, wsp = sem("pj_win"), sem("pj_wsplit")
            qps, qhi, qlo, kev, vps, vev = (sem(f"pj_{x}") for x in ("qps", "qhi", "qlo", "kev", "vps", "vev"))
            m_in, cnt_in, cnt_ps, mready, cset = (sem(f"pj_{x}") for x in ("min", "cntin", "cntps", "mready", "cset"))
            with ExitStack() as st:
                def sbl(name, shape, dt=F32):
                    return st.enter_context(nc.sbuf_tensor(name, shape, dt))
                raw = sbl("pj_raw", [P, 3, KC, D])
                w = [sbl(f"pj_w{h}", [P, 3, KC, D], F32R) for h in "hl"]
                m32 = sbl("pj_m32", [P, QT, S // 4], I32)
                m8 = m32[:, :, :].bitcast(U8)
                free = sbl("pj_free", [P, QT, QT])
                cnt, rc, keys = sbl("pj_cnt", [P, QT]), sbl("pj_rc", [P, QT]), sbl("pj_keys", [P, QT])
                one = sbl("pj_one", [P, P])
                rank, rb, srt = sbl("pj_rank", [P, QT]), sbl("pj_rb", [P, QT]), sbl("pj_srt", [P, 8])
                lv, nl = sbl("pj_lv", [P, QT]), sbl("pj_nl", [P, 1])
                block = st.enter_context(nc.Block())

                @block.sync
                def _(sp):
                    for n, name in enumerate(("WqT", "WkT", "WvT")):
                        sp.dma_start(raw[:, n, :, :], d[name].rearrange("(k p) n -> p k n", p=P)).then_inc(w_in, 16)
                    sp.dma_start(m32[:, :, :], d["mask"].rearrange("(q p) t -> p q t", p=P)).then_inc(m_in, 16)

                @block.gpsimd
                def _(pool):
                    pool.memset(one[:, :], 1.0).then_inc(cset, 1)
                    pool.iota(rank[:, :], pattern=[[1, QT]], base=0, channel_multiplier=0,
                              allow_small_or_imprecise_dtypes=True).then_inc(cset, 1)

                @block.tensor
                def _(pe):
                    u = 0
                    for n in range(2):
                        pe.wait_ge(wsp, n + 1)
                        for m in range(KC):
                            for g in range(G):
                                if u >= 4:
                                    v = u - 4
                                    if v < KC * G:
                                        pe.wait_ge(qlo, v + 1)
                                    else:
                                        pe.wait_ge(kev, v - KC * G + 1)
                                for i, (k, (a, b)) in enumerate((k, p) for k in range(KC) for p in PASSES):
                                    last = pe.matmul(ps[u % 4][:, :], w[a][:, n, k, m * P:(m + 1) * P],
                                                     actT[b][:, k, g * GT:(g + 1) * GT], start=i == 0,
                                                     stop=i == 3 * KC - 1)
                                last.then_inc(qps, 1)
                                u += 1
                    pe.wait_ge(wsp, 3)
                    for i in range(NT):
                        if i >= 3:
                            pe.wait_ge(vev, i - 2)
                        for n, (k, (a, b)) in enumerate((k, p) for k in range(KC) for p in PASSES):
                            last = pe.matmul(ps[4 + i % 3][:, 0:D], actT[a][:, k, i * P:(i + 1) * P],
                                             w[b][:, 2, k, :], start=n == 0, stop=n == 3 * KC - 1)
                        last.then_inc(vps, 1)
                    pe.wait_ge(cset, 2)
                    pe.wait_ge(cnt_in, 1)
                    pe.matmul(ps[7][:, 0:QT], one[:, :], keys[:, :], start=True, stop=True).then_inc(cnt_ps, 1)

                @block.scalar
                def _(act):
                    for u in range(KC * G):
                        m, g = u // G, u % G
                        act.wait_ge(qps, u + 1)
                        act.activation(qp[0][:, m, g * GT:(g + 1) * GT], ps[u % 4][:, :], ACT.Copy).then_inc(qhi, 1)
                    for u in range(KC * G):
                        m, g = u // G, u % G
                        act.wait_ge(qps, KC * G + u + 1)
                        act.activation(kT[:, m, g * GT:(g + 1) * GT], ps[u % 4][:, :], ACT.Copy).then_inc(kev, 1)
                    for i in range(NT):
                        act.wait_ge(vps, i + 1)
                        act.activation(v_tok[:, i, :], ps[4 + i % 3][:, 0:D], ACT.Copy).then_inc(vev, 1)

                @block.vector
                def _(dve):
                    ch = dve_chain.on(dve)
                    for n in range(3):
                        dve.wait_ge(w_in, 48)
                        weights_split(dve, ch, [(raw[:, n, :, :], w[0][:, n, :, :], w[1][:, n, :, :])], wsp)
                    for u in range(KC * G):
                        m, g = u // G, u % G
                        sl = slice(g * GT, (g + 1) * GT)
                        dve.wait_ge(qhi, u + 1)
                        dve.tensor_tensor(qp[1][:, m, sl], ps[u % 4][:, :], qp[0][:, m, sl], ALU.subtract).then_inc(qlo, 1)
                    dve.wait_ge(m_in, 16)
                    dve.tensor_scalar(mbias[:, :, :], m8, MASKED, None, ALU.mult).then_inc(mready, 1)
                    ch.link(dve.tensor_copy(identb[:, :], ident[:, :]))
                    ch.link(dve.tensor_reduce(free[:, :, :], m8.rearrange("p q (j t) -> p q j t", t=P),
                                              AX.X, ALU.add))
                    ch.link(dve.tensor_scalar(free[:, :, :], free[:, :, :], -1.0, float(P), ALU.mult, ALU.add))
                    ch.link(dve.tensor_reduce(cnt[:, :], free[:, :, :], AX.X, ALU.add))
                    ch.link(dve.reciprocal(rc[:, :], cnt[:, :]))
                    ch.link(dve.tensor_scalar(pen[:, :], rc[:, :], 0.0, None, ALU.mult))
                    dve.tensor_reduce(keys[:, :], free[:, :, :].rearrange("p q j -> p j q"), AX.X,
                                      ALU.add).then_inc(cnt_in, 1)
                    dve.wait_ge(cnt_ps, 1)
                    ch.link(dve.tensor_scalar(lv[:, :], ps[7][:, 0:QT], 0.0, None, ALU.is_gt))
                    ch.link(dve.tensor_reduce(nl[:, :], lv[:, :], AX.X, ALU.add))
                    ch.link(dve.tensor_scalar(nl[:, :], nl[:, :], 1.0, None, ALU.max))
                    ch.link(dve.tensor_copy(n_live[:, :], nl[:, :]))
                    dve.wait_ge(cset, 2)
                    ch.link(dve.tensor_scalar(rb[:, :], lv[:, :], 1000.0, -900.0, ALU.mult, ALU.add))
                    ch.link(dve.tensor_tensor(rb[:, :], rb[:, :], rank[:, :], ALU.subtract))
                    ch.link(dve.max(srt[:, :], rb[:, :]))
                    ch.link(dve.tensor_scalar(srt[:, :], srt[:, :], -1.0, 100.0, ALU.mult, ALU.add))
                    ch.link(dve.tensor_scalar(rb[:, :], srt[:, :], float(QT), None, ALU.is_lt))
                    ch.link(dve.tensor_tensor(srt[:, :], srt[:, :], rb[:, :], ALU.mult))
                    ch.link(dve.tensor_copy(live_at[:, :], srt[:, :]))
                    dve.wait_ge(mready, 1)

        def stage_attention(kT, v_tok, n_live, live_at, mbias, pen, identb):
            names = ("dve", "built", "sps", "sub", "pex", "ptps", "ptev", "pvps", "pvuse", "alpha", "alex", "init", "used")
            dch, built, sps, sub, pex, ptps, ptev, pvps, pvuse, alpha, alex, init, used = (sem(f"at_{x}") for x in names)
            with ExitStack() as st:
                def sbl(name, shape, dt=F32):
                    return st.enter_context(nc.sbuf_tensor(name, shape, dt))
                hm = sbl("at_hm", [P, HC])
                kb32 = sbl("at_kb32", [P, KC, HC, P])
                kb = [sbl(f"at_kb{h}", [P, KC, HC, P], F32R) for h in "hl"]
                vb = sbl("at_vb", [P, NH, HD + 1])
                mb = sbl("at_mb", [P, QT, P], BF16)
                pn = sbl("at_pn", [P, 2, HC, P])
                pT = sbl("at_pT", [P, 2, HC, P])
                mx = sbl("at_mx", [P, QT, NH])
                mn = sbl("at_mn", [P, 2, HC])
                al = sbl("at_al", [P, 2, HC])
                acc = sbl("at_acc", [P, QT, NH, HD + 1])
                rc = sbl("at_rc", [P, QT, NH])
                block = st.enter_context(nc.Block())
                NSTEP = QT * KC
                scr = lambda s: (ps[2 * (s % 2)], ps[2 * (s % 2) + 1])
                ptb = (ps[4], ps[5])
                HB = GT // P
                SCALE = float(HD) ** -0.5

                @block.gpsimd
                def _(pool):
                    pool.memset(hm[:, :], 1.0).then_inc(init, 1)
                    pool.wait_ge(init, 1)
                    pool.affine_select(out=hm[:, :], in_=hm[:, :], compare_op=ALU.is_ge, fill=0.0, base=0,
                                       pattern=[[-HD, HC]], channel_multiplier=1).then_inc(init, 1)
                    pool.wait_ge(init, 2)
                    pool.affine_select(out=hm[:, :], in_=hm[:, :], compare_op=ALU.is_ge, fill=0.0, base=HD - 1,
                                       pattern=[[HD, HC]], channel_multiplier=-1).then_inc(init, 1)
                    pool.memset(vb[:, :, HD:HD + 1], 1.0).then_inc(init, 1)

                @block.tensor
                def _(pe):
                    n = nc.tensor.value_load(n_live[0:1, 0:1], min_val=1, max_val=QT)
                    def scores(s, step, b):
                        u, c = s // KC, s % KC
                        pe.wait_ge(sub, step + 1)
                        for h2 in range(HC // HB):
                            bank = scr(s)[h2]
                            for i, (a, b_) in enumerate(PASSES):
                                pe.matmul(bank[:, :], qp[a][:, c, b * S + u * P:b * S + (u + 1) * P],
                                          kb[b_][:, c, h2 * HB:(h2 + 1) * HB, :], start=i == 0, stop=False)
                            last = pe.matmul(bank[:, :], identb[:, :],
                                             mb[:, u, :].unsqueeze(1).to_broadcast([P, HB, P]),
                                             start=False, stop=True)
                        last.then_inc(sps, 1)

                    for b in range(B):
                        with pe.Fori(0, n) as j:
                            t = (n * b + j)
                            pe.wait_ge(built, t + 1)
                            scores(0, t * NSTEP, b)
                            for s in range(NSTEP):
                                step = t * NSTEP + s
                                if s + 1 < NSTEP:
                                    scores(s + 1, step + 1, b)
                                pe.wait_ge(pex, step + 1)
                                pe.wait_ge(ptev, step + 1)
                                for h in range(HC):
                                    last = pe.transpose(ptb[h // HB][:, (h % HB) * P:(h % HB + 1) * P],
                                                        pn[:, s % 2, h, :], ident[:, :])
                                last.then_inc(ptps, 1)
                                pe.wait_ge(ptev, step + 2)
                                pe.wait_ge(pvuse, step + 1)
                                for h in range(HC):
                                    last = pe.matmul(ps[6 + s % 2][:, h * (HD + 1):(h + 1) * (HD + 1)],
                                                     pT[:, s % 2, h, :], vb[:, (s % KC) * HC + h, :],
                                                     start=True, stop=True)
                                last.then_inc(pvps, 1)

                @block.scalar
                def _(act):
                    n = nc.scalar.value_load(n_live[0:1, 0:1], min_val=1, max_val=QT)
                    act.nop().then_inc(ptev, 1)
                    for b in range(B):
                        with act.Fori(0, n) as j:
                            t = (n * b + j)
                            for s in range(NSTEP):
                                step = t * NSTEP + s
                                act.wait_ge(alpha, step + 1)
                                act.activation(al[:, s % 2, :], al[:, s % 2, :], ACT.Exp, scale=SCALE).then_inc(alex, 1)
                                act.wait_ge(sub, step + 3)
                                act.activation(pn[:, s % 2, :, :], pn[:, s % 2, :, :], ACT.Exp, scale=SCALE).then_inc(pex, 1)
                                act.wait_ge(ptps, step + 1)
                                for h2 in range(HC // HB):
                                    last = act.activation(pT[:, s % 2, h2 * HB:(h2 + 1) * HB, :],
                                                          ptb[h2][:, :].rearrange("p (h q) -> p h q", q=P), ACT.Copy)
                                last.then_inc(ptev, 1)

                @block.vector
                def _(dve):
                    n = nc.vector.value_load(n_live[0:1, 0:1], min_val=1, max_val=QT)
                    ch = Chain(dve, dch)
                    dve.wait_ge(init, 4)
                    dve.nop().then_inc(sub, 2)
                    dve.nop().then_inc(pvuse, 2)
                    PER = 3 + 5 * NSTEP
                    for b in range(B):
                        zeroed, fin = sem(f"at_zero{b}"), sem(f"at_fin{b}")
                        dve.memset(mx[:, :, :], 3.0 * MASKED).then_inc(zeroed, 1)
                        dve.memset(acc[:, :, :, :], 0.0).then_inc(zeroed, 1)
                        dve.wait_ge(zeroed, 2)
                        with dve.Fori(0, n) as j:
                            t = (n * b + j)
                            ch.base, ch.k = t * PER, 0
                            jt = nc.vector.value_load(live_at[0:1, bass.ds(j, 1)], min_val=0, max_val=QT - 1)
                            dve.wait_ge(pvuse, t * NSTEP + 2)
                            for c in range(KC):
                                last = dve.tensor_tensor(
                                    kb32[:, c, :, :],
                                    kT[:, c, bass.ds(b * S + jt * P, P)].unsqueeze(1).to_broadcast([P, HC, P]),
                                    hm[:, :].unsqueeze(2).to_broadcast([P, HC, P]), ALU.mult)
                            ch.link(last)
                            ch.link(dve.tensor_copy(kb[0][:, :, :, :], kb32[:, :, :, :]))
                            dve.tensor_tensor(kb[1][:, :, :, :], kb32[:, :, :, :], kb[0][:, :, :, :], ALU.subtract)
                            dve.tensor_copy(mb[:, :, :], mbias[:, :, bass.ds(jt * P, P)])
                            ch.link(dve.tensor_copy(vb[:, :, 0:HD],
                                                    v_tok[:, bass.ds(b * QT + jt, 1), :].rearrange("p a (h e) -> p (a h) e", e=HD)))
                            dve.nop().then_inc(built, 1)

                            def front(s):
                                u, c = s // KC, s % KC
                                step = t * NSTEP + s
                                hs = slice(c * HC, (c + 1) * HC)
                                sl = mn[:, s % 2, :]
                                dve.wait_ge(sps, step + 1)
                                for h2 in range(HC // HB):
                                    last = dve.tensor_reduce(mn[:, s % 2, h2 * HB:(h2 + 1) * HB],
                                                             scr(s)[h2][:, :].rearrange("p (h t) -> p h t", t=P),
                                                             AX.X, ALU.max)
                                ch.link(last)
                                ch.link(dve.tensor_tensor(sl, sl, mx[:, u, hs], ALU.max))
                                dve.wait_ge(pvuse, step + 1)
                                dve.tensor_tensor(al[:, s % 2, :], mx[:, u, hs], sl, ALU.subtract).then_inc(alpha, 1)
                                for h2 in range(HC // HB):
                                    last = dve.tensor_tensor(pn[:, s % 2, h2 * HB:(h2 + 1) * HB, :],
                                                             scr(s)[h2][:, :].rearrange("p (h t) -> p h t", t=P),
                                                             mn[:, s % 2, h2 * HB:(h2 + 1) * HB].unsqueeze(2).to_broadcast([P, HB, P]),
                                                             ALU.subtract)
                                last.then_inc(sub, 1)
                                dve.wait_ge(alpha, step + 1)
                                ch.link(dve.tensor_copy(mx[:, u, hs], sl))

                            def back(s):
                                u, c = s // KC, s % KC
                                step = t * NSTEP + s
                                hs = slice(c * HC, (c + 1) * HC)
                                dve.wait_ge(alex, step + 1)
                                ch.link(dve.tensor_tensor(acc[:, u, hs, :], acc[:, u, hs, :],
                                                          al[:, s % 2, :].unsqueeze(2).to_broadcast([P, HC, HD + 1]), ALU.mult))
                                dve.wait_ge(pvps, step + 1)
                                ch.link(dve.tensor_tensor(acc[:, u, hs, :],
                                                          ps[6 + s % 2][:, 0:HC * (HD + 1)].rearrange("p (h e) -> p h e", e=HD + 1),
                                                          acc[:, u, hs, :], ALU.add))
                                dve.nop().then_inc(pvuse, 1)

                            front(0)
                            for s in range(1, NSTEP):
                                front(s)
                                back(s - 1)
                            back(NSTEP - 1)
                            assert ch.k == PER, (ch.k, PER)
                        dve.reciprocal(rc[:, :, :], acc[:, :, :, HD]).then_inc(fin, 1)
                        dve.wait_ge(fin, 1)
                        dve.tensor_tensor(rc[:, :, :], rc[:, :, :],
                                          pen[:, :].unsqueeze(2).to_broadcast([P, QT, NH]), ALU.add).then_inc(fin, 1)
                        dve.wait_ge(fin, 2)
                        for u in range(QT):
                            last = dve.tensor_tensor(v_tok[:, b * QT + u, :].rearrange("p (h e) -> p h e", e=HD),
                                                     acc[:, u, :, 0:HD],
                                                     rc[:, u, :].unsqueeze(2).to_broadcast([P, NH, HD]), ALU.mult)
                        last.then_inc(fin, 1)
                        dve.wait_ge(fin, 3)

        def stage_condition(xc, comb, E2):
            names = ("win", "wsp", "cin", "sil", "csb", "mod", "ops", "used", "sq", "req", "ack")
            w_in, wsp, cin, sil, csb, modp, ops, used, sq, req, ack = (sem(f"cd_{x}") for x in names)
            with ExitStack() as st:
                def sbl(name, shape, dt=F32):
                    return st.enter_context(nc.sbuf_tensor(name, shape, dt))
                raw = sbl("cd_raw", [P, KC, D])
                w = [sbl(f"cd_w{h}", [P, KC, D], F32R) for h in "hl"]
                wc, cT = sbl("cd_wc", [C, 2 * D]), sbl("cd_cT", [C, B])
                cb = sbl("cd_cb", [C, B, P])
                bc, rs = sbl("cd_bc", [P, 2 * D]), sbl("cd_rs", [P, D])
                mod = sbl("cd_mod", [P, B, 2 * D])
                ss, r = sbl("cd_ss", [P, NT]), sbl("cd_r", [P, NT])
                junk = sbl("cd_junk", [P, D])
                block = st.enter_context(nc.Block())

                @block.sync
                def _(sp):
                    sp.dma_start(raw[:, :, :], d["WoT"].rearrange("(k p) n -> p k n", p=P)).then_inc(w_in, 16)
                    sp.dma_start(wc[:, :], d["WcT"]).then_inc(cin, 16)
                    sp.dma_start(cT[:, :], d["condT"]).then_inc(cin, 16)
                    sp.dma_start(bc[:, :], d["bc"].partition_broadcast(P)).then_inc(cin, 16)
                    sp.dma_start(rs[:, :], d["rms_scale"].partition_broadcast(P)).then_inc(cin, 16)

                @block.tensor
                def _(pe):
                    pe.wait_ge(csb, 1)
                    for b in range(B):
                        pe.matmul(ps[4 + b][:, :], cb[:, b, :], wc[:, :], start=True, stop=True).then_inc(modp, 1)
                    pe.wait_ge(wsp, 1)
                    for i in range(NT):
                        if i >= 4:
                            pe.wait_ge(used, i - 3)
                        for n, (k, (a, b)) in enumerate((k, p) for k in range(KC) for p in PASSES):
                            last = pe.matmul(ps[i % 4][:, 0:D], actT[a][:, k, i * P:(i + 1) * P],
                                             w[b][:, k, :], start=n == 0, stop=n == 3 * KC - 1)
                        last.then_inc(ops, 1)

                @block.scalar
                def _(act):
                    act.wait_ge(cin, 64)
                    act.activation(cT[:, :], cT[:, :], ACT.Silu).then_inc(sil, 1)
                    for i in range(NT):
                        act.wait_ge(used, i + 1)
                        if i:
                            act.wait_ge(sq, i)
                        act.activation(junk[:, :], xc[:, i, :], ACT.Square, accum_out=ss[:, i:i + 1]).then_inc(sq, 1)
                    act.wait_ge(req, 1)
                    act.activation(r[:, :], r[:, :], ACT.Sqrt).then_inc(ack, 1)

                @block.vector
                def _(dve):
                    ch = dve_chain.on(dve)
                    dve.wait_ge(sil, 1)
                    dve.tensor_copy(cb[:, :, :], cT[:, :].unsqueeze(2).to_broadcast([C, B, P])).then_inc(csb, 1)
                    dve.wait_ge(w_in, 16)
                    weights_split(dve, ch, [(raw[:, :, :], w[0][:, :, :], w[1][:, :, :])], wsp)
                    for b in range(B):
                        dve.wait_ge(modp, b + 1)
                        ch.link(dve.tensor_tensor(mod[:, b, :], ps[4 + b][:, :], bc[:, :], ALU.add))
                        ch.link(dve.scalar_tensor_tensor(out=mod[:, b, D:2 * D], in0=mod[:, b, D:2 * D], scalar=1.0,
                                                         in1=rs[:, :], op0=ALU.add, op1=ALU.mult))
                    for i in range(NT):
                        dve.wait_ge(ops, i + 1)
                        dve.tensor_copy(xc[:, i, :], ps[i % 4][:, 0:D]).then_inc(used, 1)
                    dve.wait_ge(used, NT)
                    dve.wait_ge(sq, NT)
                    norm_rows(ch, req, ack, 1, ss[:, :], r[:, :], 1e-6, 1.0 / D)
                    for i in range(NT):
                        last = dve.tensor_scalar(xc[:, i, :], xc[:, i, :], r[:, i:i + 1], None, ALU.mult)
                    ch.link(last)
                    for b in range(B):
                        v = xc[:, b * NB:(b + 1) * NB, :]
                        ch.link(dve.tensor_tensor(v, v, mod[:, b, D:2 * D].unsqueeze(1).to_broadcast([P, NB, D]), ALU.mult))
                        ch.link(dve.tensor_tensor(v, v, mod[:, b, 0:D].unsqueeze(1).to_broadcast([P, NB, D]), ALU.add))

        def stage_gate2(xc, comb):
            names = ("gin", "sq", "gate_rows", "gps", "gsp", "lps", "ein", "eout", "isq", "iroot")
            gin, sq, r1, gps, gsp, lps, ein, eout, isq, iroot = (sem(f"g2_{x}") for x in names)
            with ExitStack() as st:
                def sbl(name, shape, dt=F32):
                    return st.enter_context(nc.sbuf_tensor(name, shape, dt))
                gw, gj = sbl("g2_gw", [E2, D]), sbl("g2_gj", [E2, D])
                gn = sbl("g2_gn", [E2, 1])
                gT = [sbl(f"g2_gT{h}", [P, KC, E2], F32R) for h in "hl"]
                ss, junk = sbl("g2_ss", [P, NT]), sbl("g2_junk", [P, D])
                z, sc, rep = sbl("g2_z", [P, NT, E2]), sbl("g2_sc", [P, NT, E2]), sbl("g2_rep", [P, NT, E2])
                top, sm = sbl("g2_top", [P, NT, 8]), sbl("g2_sm", [P, NT])
                block = st.enter_context(nc.Block())

                @block.sync
                def _(sp):
                    sp.dma_start(gw[:, :], d["gate_w"]).then_inc(gin, 16)

                @block.scalar
                def _(act):
                    act.wait_ge(gin, 16)
                    act.activation(gj[:, :], gw[:, :], ACT.Square, accum_out=gn[:, :]).then_inc(isq, 1)
                    for i in range(NT):
                        if i:
                            act.wait_ge(sq, i)
                        act.activation(junk[:, :], xc[:, i, :], ACT.Square, accum_out=ss[:, i:i + 1]).then_inc(sq, 1)
                    act.wait_ge(isq, 1)
                    act.activation(gn[:, :], gn[:, :], ACT.Sqrt).then_inc(iroot, 1)
                    act.wait_ge(sq, NT)
                    act.activation(ss[:, :], ss[:, :], ACT.Sqrt).then_inc(iroot, 1)
                    act.wait_ge(ein, 1)
                    act.activation(z[:, :, :], z[:, :, :], ACT.Exp, scale=-1.0).then_inc(eout, 1)

                @block.tensor
                def _(pe):
                    pe.wait_ge(r1, 1)
                    for k in range(KC):
                        last = pe.transpose(ps[0][:, k * E2:(k + 1) * E2], gw[:, k * P:(k + 1) * P], ident[0:E2, 0:E2])
                    last.then_inc(gps, 1)
                    pe.wait_ge(gsp, 1)
                    for i in range(NT):
                        for n, (k, (a, b)) in enumerate((k, p) for k in range(KC) for p in PASSES):
                            last = pe.matmul(ps[1][:, i * E2:(i + 1) * E2], actT[a][:, k, i * P:(i + 1) * P],
                                             gT[b][:, k, :], start=n == 0, stop=n == 3 * KC - 1)
                    last.then_inc(lps, 1)

                @block.vector
                def _(dve):
                    ch = dve_chain.on(dve)
                    bc3 = lambda v: v.unsqueeze(2).to_broadcast([P, NT, E2])
                    dve.wait_ge(iroot, 2)
                    ch.link(dve.tensor_scalar(gn[:, :], gn[:, :], 1e-12, None, ALU.max))
                    ch.link(dve.reciprocal(gn[:, :], gn[:, :]))
                    dve.tensor_scalar(gw[:, :], gw[:, :], gn[:, 0:1], None, ALU.mult).then_inc(r1, 1)
                    dve.wait_ge(gps, 1)
                    gsrc = ps[0][:, 0:KC * E2].rearrange("p (k e) -> p k e", k=KC)
                    ch.link(dve.tensor_copy(gT[0][:, :, :], gsrc))
                    dve.tensor_tensor(gT[1][:, :, :], gsrc, gT[0][:, :, :], ALU.subtract).then_inc(gsp, 1)
                    ch.link(dve.tensor_scalar(ss[:, :], ss[:, :], 1e-12, None, ALU.max))
                    ch.link(dve.reciprocal(ss[:, :], ss[:, :]))
                    dve.wait_ge(lps, 1)
                    dve.tensor_tensor(z[:, :, :], ps[1][:, 0:NT * E2].rearrange("p (i e) -> p i e", i=NT),
                                      bc3(ss[:, :]), ALU.mult).then_inc(ein, 1)
                    dve.wait_ge(eout, 1)
                    ch.link(dve.tensor_scalar(z[:, :, :], z[:, :, :], 1.0, None, ALU.add))
                    ch.link(dve.reciprocal(sc[:, :, :], z[:, :, :]))
                    for i in range(NT):
                        last = dve.max(top[:, i, :], sc[:, i, :])
                    ch.link(last)
                    for i in range(NT):
                        last = dve.match_replace(out=rep[:, i, :], in_to_replace=top[:, i, :],
                                                 in_values=sc[:, i, :], imm_value=-1.0)
                    ch.link(dve.tensor_reduce(sm[:, :], top[:, :, :], AX.X, ALU.add))
                    ch.link(dve.reciprocal(sm[:, :], sm[:, :]))
                    ch.link(dve.tensor_scalar(rep[:, :, :], rep[:, :, :], 0.0, None, ALU.is_lt))
                    ch.link(dve.tensor_tensor(sc[:, :, :], sc[:, :, :], rep[:, :, :], ALU.mult))
                    dve.memset(comb[:, :, E2:E2 + 1], 1.0)
                    ch.link(dve.tensor_tensor(comb[:, :, 0:E2], sc[:, :, :], bc3(sm[:, :]), ALU.mult))

        def stage_experts2(comb):
            names = ("wsp", "dve", "hps", "sil", "h32", "hhi", "hsp", "ops", "used", "out")
            win = [sem(f"e2_win{n}") for n in range(2)]
            wsp, dch, hps, sil, h32d, hhi, hsp, ops, used, stored = (sem(f"e2_{x}") for x in names)
            LAG = 2
            NE = E2 + 1
            NW = 2 * KC * H2 + D
            OU, OD = KC * H2, 2 * KC * H2
            SP_ = 2 * G
            HS = 4
            with ExitStack() as st:
                def sbl(name, shape, dt=F32):
                    return st.enter_context(nc.sbuf_tensor(name, shape, dt))
                raw = sbl("e2_raw", [P, 2, NW])
                w = [[sbl(f"e2_w{p}{h}", [P, NW], F32R) for h in "hl"] for p in range(2)]
                sl_sb, h32 = sbl("e2_silusb", [P, 2, GT]), sbl("e2_h32sb", [P, 2, GT])
                hh = [sbl(f"e2_h{h}", [P, HS, GT], F32R) for h in "hl"]
                block = st.enter_context(nc.Block())

                @block.sync
                def _(sp):
                    def load(e, slot):
                        for name, o, c, n in (("w_gate", 0, KC, H2), ("w_up", OU, KC, H2), ("w_down", OD, 1, D)):
                            src = d[name].rearrange("e (c p) n -> p e c n", p=P)[:, bass.ds(e, 1), :, :]
                            sp.dma_start(raw[:, slot, o:o + c * n].rearrange("p (a c n) -> p a c n", a=1, c=c),
                                         src).then_inc(win[slot], 16)
                    load(0, 0)
                    load(1, 1)
                    with sp.Fori(1, E2 // 2) as t:
                        for slot in range(2):
                            sp.wait_ge(wsp, 2 * t - 1 + slot)
                            load(2 * t + slot, slot)
                    sp.wait_ge(wsp, E2 - 1)
                    for name, o, c, n in (("sw_gate", 0, KC, H2), ("sw_up", OU, KC, H2), ("sw_down", OD, 1, D)):
                        sp.dma_start(raw[:, 0, o:o + c * n].rearrange("p (c n) -> p c n", c=c),
                                     d[name].rearrange("(c p) n -> p c n", p=P)).then_inc(win[0], 16)
                    o_tok = out.rearrange("(i p) d -> p i d", p=P)
                    for g in range(G):
                        sp.wait_ge(used, (E2 * G + g + 1) * TG + 4)
                        sp.dma_start(o_tok[:, g * TG:(g + 1) * TG, :], y[:, g * TG:(g + 1) * TG, :]).then_inc(stored, 16)
                    sp.wait_ge(stored, 16 * G)

                @block.tensor
                def _(pe):
                    def up(s, step, e):
                        par, g = (s // G) % 2, s % G
                        if g == 0:
                            pe.wait_ge(wsp, e + 1)
                        for v, (o, bank) in enumerate(((0, ps[s % 2]), (OU, ps[2 + s % 2]))):
                            pe.wait_ge((sil, h32d)[v], step + 1)
                            for n, (k, (a, b)) in enumerate((k, p) for k in range(KC) for p in PASSES):
                                last = pe.matmul(bank[:, :], w[par][a][:, o + k * H2:o + (k + 1) * H2],
                                                 actT[b][:, k, g * GT:(g + 1) * GT], start=n == 0,
                                                 stop=n == 3 * KC - 1)
                            last.then_inc(hps, 1)

                    def down(s, step):
                        par = (s // G) % 2
                        pe.wait_ge(hsp, step + 1)
                        for j in range(TG):
                            pe.wait_ge(used, step * TG + j + 1)
                            for n, (a, b) in enumerate(PASSES):
                                last = pe.matmul(ps[4 + j][:, 0:D], hh[a][:, s % HS, j * P:(j + 1) * P],
                                                 w[par][b][:, OD:OD + D], start=n == 0, stop=n == 2)
                            last.then_inc(ops, 1)

                    for s in range(LAG):
                        up(s, s, 0)
                    with pe.Fori(0, E2 // 2) as t:
                        for s in range(SP_):
                            up(s + LAG, t * SP_ + s + LAG, 2 * t + (s + LAG) // G)
                            down(s, t * SP_ + s)
                    for s in range(G):
                        if s + LAG < G:
                            up(s + LAG, E2 * G + s + LAG, E2)
                        down(s, E2 * G + s)

                def hidden_steps(eng, body):
                    for s in range(LAG):
                        body(s, s, None, 0, False)
                    with eng.Fori(0, E2 // 2 - 1) as t:
                        for s in range(SP_):
                            body(s + LAG, t * SP_ + s + LAG, s, t, False)
                    for s in range(SP_):
                        body(s + LAG, (E2 // 2 - 1) * SP_ + s + LAG, s, E2 // 2 - 1, True)
                    for s in range(G):
                        body(s + LAG if s + LAG < G else None, E2 * G + s + LAG, s, E2 // 2, True)

                @block.scalar
                def _(act):
                    act.nop().then_inc(sil, 2)

                    def body(s, step, *_):
                        if s is None:
                            return
                        act.wait_ge(hps, 2 * step + 1)
                        act.wait_ge(h32d, step + 1)
                        act.activation(sl_sb[:, s % 2, :], ps[s % 2][:, :], ACT.Silu).then_inc(sil, 1)
                    hidden_steps(act, body)

                @block.gpsimd
                def _(pool):
                    def body(s, step, *_):
                        if s is None:
                            return
                        pool.wait_ge(hhi, step + 1)
                        pool.tensor_tensor(hh[1][:, s % HS, :], h32[:, s % 2, :], hh[0][:, s % HS, :],
                                           ALU.subtract).then_inc(hsp, 1)
                    hidden_steps(pool, body)

                @block.vector
                def _(dve):
                    dve.nop().then_inc(h32d, 2)
                    dve.nop().then_inc(used, 4)

                    def split(par, loads, ch):
                        dve.wait_ge(win[par], 48 * loads)
                        ch.link(dve.tensor_copy(w[par][0][:, :], raw[:, par, :]))
                        dve.tensor_tensor(w[par][1][:, :], raw[:, par, :], w[par][0][:, :], ALU.subtract).then_inc(wsp, 1)

                    chains = [Chain(dve, dch), Chain(dve, sem("e2_dve2"))]
                    for par in range(2):
                        split(par, 1, chains[par])

                    def body(s, step, out_s, t, last_turn):
                        if s is not None:
                            dve.wait_ge(sil, step + 3)
                            dve.wait_ge(hps, 2 * step + 2)
                            if out_s is not None:
                                dve.wait_ge(hsp, step - 1)
                            dve.tensor_tensor(h32[:, s % 2, :], ps[2 + s % 2][:, :], sl_sb[:, s % 2, :],
                                              ALU.mult).then_inc(h32d, 1)
                            dve.wait_ge(h32d, step + 3)
                            dve.tensor_copy(hh[0][:, s % HS, :], h32[:, s % 2, :]).then_inc(hhi, 1)
                        if out_s is not None:
                            g = out_s % G
                            first = (step - LAG) * TG
                            for j in range(TG):
                                i = g * TG + j
                                dve.wait_ge(ops, first + j + 1)
                                dve.wait_ge(used, first + 1)
                                dve.scalar_tensor_tensor(out=y[:, i, :], in0=ps[4 + j][:, 0:D],
                                                         scalar=comb[:, i, bass.ds(2 * t + out_s // G, 1)],
                                                         in1=y[:, i, :], op0=ALU.mult, op1=ALU.add).then_inc(used, 1)
                            if g == G - 1 and s is not None:
                                par = out_s // G
                                if not (last_turn and par):
                                    chains[par].base, chains[par].k = t + 1, 0
                                    split(par, t + 2, chains[par])
                    hidden_steps(dve, body)

        stage_gate1()
        stage_experts1()
        qp = [sb(f"qp{h}", [P, KC, T], F32R) for h in "hl"]
        transpose_stage(y)
        kvh = stage_linear_attention()
        stage_linear_out(kvh)
        transpose_stage(y)
        stage_feed_forward()
        stage_residual()
        transpose_stage(y)
        v_tok = sb("v_tok", [P, NT, D])
        with ExitStack() as st:
            def sbm(name, shape, dt=F32):
                return st.enter_context(nc.sbuf_tensor(name, shape, dt))
            kT = sbm("kT", [P, KC, T])
            mbias = sbm("mbias", [P, QT, S], BF16)
            n_live, live_at = sbm("n_live", [P, 1], I32), sbm("live_at", [P, 8], I32)
            pen, identb = sbm("pen", [P, QT]), sbm("identb", [P, P], BF16)
            stage_project(kT, v_tok, n_live, live_at, mbias, pen, None, identb)
            stage_attention(kT, v_tok, n_live, live_at, mbias, pen, identb)
        transpose_stage(v_tok)
        comb = sb("comb", [P, NT, E2 + 1])
        stage_condition(v_tok, comb, E2)
        transpose_stage(v_tok)
        stage_gate2(v_tok, comb)
        stage_experts2(comb)


def kernel(**inputs):
    import numpy as np
    import concourse.bacc as bacc
    from concourse import mybir as mb
    from concourse.bass_utils import run_bass_kernel_spmd as run

    a = {k: np.asarray(v) for k, v in inputs.items()}
    x = a["x"]
    arrays = {
        "x": x.reshape(-1, x.shape[-1]), "xT": x.reshape(-1, x.shape[-1]).T,
        "cond": a["cond_256"], "condT": a["cond_256"].T, "mask": a["mask_SxS_bk1"].view(np.int32),
        "rms_w": a["L0_cond_rms_w"], "wg_W": a["L0_cond_wg_W"], "wg_b": a["L0_cond_wg_b"],
        "gg_W": a["L0_cond_gg_W"], "gg_b": a["L0_cond_gg_b"],
        "Wqkv": a["L0_attn_Wqkv"], "bqkv": a["L0_attn_bqkv"], "Wg": a["L0_attn_Wg"], "bg": a["L0_attn_bg"],
        "Wu": a["L0_attn_Wu"], "bu": a["L0_attn_bu"], "Wd": a["L0_attn_Wd"], "bd": a["L0_attn_bd"],
        "g1": a["L0_attn_g1"], "be1": a["L0_attn_b1"], "g2": a["L0_attn_g2"], "be2": a["L0_attn_b2"],
        "WqT": a["L0_cond2_Wq"].T, "WkT": a["L0_cond2_Wk"].T, "WvT": a["L0_cond2_Wv"].T,
        "WoT": a["L0_cond2_Wo"].T, "rms_scale": a["L0_cond2_rms_scale"], "WcT": a["L0_cond2_Wc"].T,
        "bc": a["L0_cond2_bc"], "gate_w": a["L0_ffn_gate_w"], "w_gate": a["L0_ffn_w_gate"],
        "w_up": a["L0_ffn_w_up"], "w_down": a["L0_ffn_w_down"], "sw_gate": a["L0_ffn_sw_gate"],
        "sw_up": a["L0_ffn_sw_up"], "sw_down": a["L0_ffn_sw_down"],
    }
    for n in ("1", "2", "3"):
        arrays["W" + n], arrays["b" + n] = a["L0_cond_W" + n], a["L0_cond_b" + n]
        if n != "3":
            b = arrays["b" + n]
            arrays[f"b{n}_cols"] = b.reshape(b.shape[0], -1, P).transpose(2, 0, 1)

    def cols(v):
        return v[:v.size // P * P].reshape(-1, P).T

    arrays["rms_w_cols"], arrays["bq_cols"] = cols(arrays["rms_w"]), cols(arrays["bqkv"][:x.shape[-1]])
    arrays["bg_cols"], arrays["bu_cols"] = cols(arrays["bg"]), cols(arrays["bu"])
    nc = bacc.Bacc("TRN2", target_bir_lowering=False, num_devices=1)
    arrays = {f"in_{k}": np.ascontiguousarray(v) for k, v in arrays.items()}
    d = {k[3:]: nc.dram_tensor(k, v.shape, mb.dt.from_np(v.dtype), kind="ExternalInput").ap()
         for k, v in arrays.items()}
    out = nc.dram_tensor("out", d["x"].shape, mb.dt.float32, kind="ExternalOutput").ap()
    adaln_block(nc, d, out)
    r = run(nc, [arrays], core_ids=[0])
    return r.results[0]["out"].reshape(x.shape)
```

```python
from contextlib import ExitStack

import concourse.bass as bass
from concourse import mybir

ALU = mybir.AluOpType
ACT = mybir.ActivationFunctionType
F32 = mybir.dt.float32
F32R = mybir.dt.float32r
BF16 = mybir.dt.bfloat16
I32 = mybir.dt.int32
U32 = mybir.dt.uint32
U8 = mybir.dt.uint8
AX = mybir.AxisListType

P = 128
GT = 512
ET = 256
PASSES = ((0, 0), (0, 1), (1, 0))
MASKED = -1e30


class Chain:

    def __init__(self, eng, sem):
        self.eng, self.sem, self.base, self.k = eng, sem, 0, 0

    def on(self, eng):
        self.eng = eng
        return self

    def link(self, ins):
        self.k += 1
        ins.then_inc(self.sem, 1)
        self.eng.wait_ge(self.sem, self.base + self.k)


def adaln_block(nc, d, out):
    T, D = d["x"].shape
    B = d["cond"].shape[0]
    S = T // B
    C = d["cond"].shape[1]
    NT, KC, G = T // P, D // P, T // GT
    TG = GT // P
    NB = NT // B
    E1, _, M1 = d["W1"].shape
    MC = M1 // P
    F = d["Wg"].shape[1]
    FC = -(-F // P)
    FR = F - (FC - 1) * P
    E2, _, H2 = d["w_gate"].shape
    HD = 16
    NH = D // HD
    HC = NH // KC
    VW = HD + 2
    LW = D + 2
    QT = S // P

    with ExitStack() as ctx:
        def sem(name):
            return ctx.enter_context(nc.semaphore(name))

        def sb(name, shape, dt=F32):
            return ctx.enter_context(nc.sbuf_tensor(name, shape, dt))

        psum = ctx.enter_context(nc.psum_tensor("psum", [P, 8, GT], F32))
        ps = [psum[:, i, :] for i in range(8)]
        ident = sb("ident", [P, P])
        act_hi = sb("act_hi", [P, KC, T], F32R)
        act_lo = sb("act_lo", [P, KC, T], F32R)
        actT = (act_hi, act_lo)
        y = sb("y", [P, NT, D])
        TILES = 2 * T // ET + 2 * (E1 - 2) + 2
        LONG = (TILES + T // ET) * ET
        x_rows = nc.dram_tensor("x_rows", [LONG, D], F32, kind="Internal").ap()
        y_rows = nc.dram_tensor("y_rows", [LONG, D], F32, kind="Internal").ap()
        top2 = sb("top2", [P, NT, 8])
        place = sb("place", [P, NT, 2], U32)
        tiles = sb("tiles", [P, 3, E1], I32)

        dve_chain = Chain(None, sem("dve_chain"))
        turned, hi_done, lo_done = sem("tr_turned"), sem("tr_hi"), sem("tr_lo")
        turns_done = [0]

        x_tok = d["x"].rearrange("(i p) d -> p i d", p=P)

        def transpose_stage(src):
            n0 = turns_done[0]
            turns_done[0] += KC * G
            with nc.Block() as block:
                @block.tensor
                def _(pe):
                    for u in range(KC * G):
                        k, g = u % KC, u // KC
                        if u >= 4:
                            pe.wait_ge(lo_done, n0 + u - 3)
                        for j in range(TG):
                            t = pe.transpose(ps[u % 4][:, j * P:(j + 1) * P],
                                             src[:, g * TG + j, k * P:(k + 1) * P], ident[:, :])
                        t.then_inc(turned, 1)

                @block.scalar
                def _(act):
                    for u in range(KC * G):
                        k, g = u % KC, u // KC
                        act.wait_ge(turned, n0 + u + 1)
                        act.activation(act_hi[:, k, g * GT:(g + 1) * GT], ps[u % 4][:, :],
                                       ACT.Copy).then_inc(hi_done, 1)

                @block.vector
                def _(dve):
                    for u in range(KC * G):
                        k, g = u % KC, u // KC
                        sl = slice(g * GT, (g + 1) * GT)
                        dve.wait_ge(hi_done, n0 + u + 1)
                        dve.tensor_tensor(act_lo[:, k, sl], ps[u % 4][:, :], act_hi[:, k, sl],
                                          ALU.subtract).then_inc(lo_done, 1)

        def norm_rows(chain, act_req, act_ack, n_done, var_ap, tmp, eps, scale=1.0):
            chain.link(chain.eng.tensor_scalar(tmp, var_ap, scale, eps, ALU.mult, ALU.add))
            chain.eng.tensor_copy(tmp, tmp).then_inc(act_req, 1)
            chain.eng.wait_ge(act_ack, n_done)
            chain.link(chain.eng.reciprocal(tmp, tmp))

        def stage_gate1():
            loaded, tok_in, w_in = [sem(f"g1_xT{g}") for g in range(G)], sem("g1_x"), sem("g1_w")
            idn = sem("g1_ident")
            wready, asplit = sem("g1_wready"), sem("g1_split")
            sq, logit, cbias = sem("g1_sq"), sem("g1_logit"), sem("g1_cbias")
            filled, selected, ranked, placed, scattered = (sem(f"g1_{x}") for x in (
                "filled", "selected", "ranked", "placed", "scattered"))
            root_in, root, ein, eout = sem("g1_rootin"), sem("g1_root"), sem("g1_ein"), sem("g1_eout")
            with ExitStack() as st:
                def sbl(name, shape, dt=F32):
                    return st.enter_context(nc.sbuf_tensor(name, shape, dt))
                xT = sbl("g1_xTraw", [P, KC, T])
                xk = sbl("g1_xtok", [P, NT, D])
                junk = sbl("g1_junk", [P, D])
                wg = sbl("g1_wg", [P, KC, E1])
                rw = sbl("g1_rw", [P, KC])
                wgh, wgl = sbl("g1_wgh", [P, KC, E1], F32R), sbl("g1_wgl", [P, KC, E1], F32R)
                bia, bib = sbl("g1_ba", [P, E1]), sbl("g1_bb", [P, E1])
                gg = sbl("g1_gg", [C, E1])
                cT, cTb = sbl("g1_cT", [C, B]), sbl("g1_cTb", [C, B, P])
                ss, r = sbl("g1_ss", [P, NT]), sbl("g1_r", [P, NT])
                bb = sbl("g1_bias", [P, B, E1])
                z, w8 = sbl("g1_z", [P, NT, E1]), sbl("g1_w8", [P, NT, E1])
                mx, sm = sbl("g1_mx", [P, NT]), sbl("g1_sm", [P, NT])
                top = top2
                idx, idf = sbl("g1_idx", [P, NT, 8], U32), sbl("g1_idf", [P, NT, 8])
                io = sbl("g1_iota", [P, E1])
                oh = [sbl(f"g1_oh{n}", [P, NT, E1]) for n in range(2)]
                sel, pos = sbl("g1_sel", [P, NT, E1]), sbl("g1_pos", [P, NT, E1])
                selsum, cnt = sbl("g1_selsum", [P, E1]), sbl("g1_cnt", [P, E1])
                thr, tri8 = sbl("g1_thr", [P, T // ET]), sbl("g1_tri8", [P, E1, E1])
                cmp_, nt, bt = sbl("g1_cmp", [P, E1, T // ET]), sbl("g1_nt", [P, E1]), sbl("g1_bt", [P, E1])
                pf = sbl("g1_pf", [P, NT, 2])
                ones, tri = sbl("g1_ones", [P, P]), sbl("g1_tri", [P, P])
                zero = sbl("g1_zero", [P, D])
                block = st.enter_context(nc.Block())

                @block.sync
                def _(sp):
                    for g in range(G):
                        sp.dma_start(xT[:, :, g * GT:(g + 1) * GT],
                                     d["xT"].rearrange("(k p) t -> p k t", p=P)[:, :, g * GT:(g + 1) * GT]).then_inc(loaded[g], 16)
                    sp.dma_start(wg[:, :, :], d["wg_W"].rearrange("(k p) e -> p k e", p=P)).then_inc(w_in, 16)
                    sp.dma_start(rw[:, :], d["rms_w_cols"]).then_inc(w_in, 16)
                    sp.dma_start(bia[:, :], d["wg_b"].partition_broadcast(P)).then_inc(w_in, 16)
                    sp.dma_start(bib[:, :], d["gg_b"].partition_broadcast(P)).then_inc(w_in, 16)
                    sp.dma_start(gg[:, :], d["gg_W"]).then_inc(w_in, 16)
                    sp.dma_start(cT[:, :], d["condT"]).then_inc(w_in, 16)
                    sp.wait_ge(idn, 8)
                    rows = x_rows[0:TILES * ET, :].rearrange("(p n) d -> p n d", p=P)
                    part = TILES * ET // P // 4
                    for n in range(4):
                        sp.dma_start(rows[:, n * part:(n + 1) * part, :],
                                     zero[:, :].unsqueeze(1).to_broadcast([P, part, D])).then_inc(filled, 16)

                @block.gpsimd
                def _(pool):
                    pool.memset(ident[:, :], 0.0).then_inc(idn, 1)
                    pool.wait_ge(idn, 1)
                    pool.affine_select(out=ident[:, :], in_=ident[:, :], compare_op=ALU.not_equal, fill=1.0,
                                       base=0, pattern=[[-1, P]], channel_multiplier=1).then_inc(idn, 1)
                    pool.iota(io[:, :], pattern=[[1, E1]], base=0, channel_multiplier=0,
                              allow_small_or_imprecise_dtypes=True).then_inc(idn, 1)
                    pool.iota(thr[:, :], pattern=[[ET, T // ET]], base=0, channel_multiplier=0,
                              allow_small_or_imprecise_dtypes=True).then_inc(idn, 1)
                    pool.memset(ones[:, :], 1.0).then_inc(idn, 1)
                    pool.memset(tri[:, :], 1.0).then_inc(idn, 1)
                    pool.memset(tri8[:, :, :], 1.0).then_inc(idn, 1)
                    pool.memset(zero[:, :], 0.0).then_inc(idn, 1)
                    pool.wait_ge(idn, 8)
                    pool.affine_select(out=tri[:, :], in_=tri[:, :], compare_op=ALU.is_gt, fill=0.0,
                                       base=0, pattern=[[1, P]], channel_multiplier=-1).then_inc(idn, 1)
                    pool.affine_select(out=tri8[:, :, :], in_=tri8[:, :, :], compare_op=ALU.is_gt, fill=0.0,
                                       base=0, pattern=[[1, E1], [-1, E1]], channel_multiplier=0).then_inc(idn, 1)
                    pool.wait_ge(filled, 16 * 4)
                    pool.wait_ge(placed, 1)
                    pool.wait_ge(tok_in, 16)
                    for i in range(NT):
                        for n in range(2):
                            pool.indirect_dma_start(
                                out=x_rows, out_offset=bass.IndirectOffsetOnAxis(ap=place[:, i, n:n + 1], axis=0),
                                in_=xk[:, i, :], in_offset=None).then_inc(scattered, 16)
                    pool.wait_ge(scattered, 16 * 2 * NT)

                @block.scalar
                def _(act):
                    act.dma_start(xk[:, :, :], x_tok).then_inc(tok_in, 16)
                    act.wait_ge(tok_in, 16)
                    for i in range(NT):
                        if i:
                            act.wait_ge(sq, i)
                        act.activation(junk[:, :], xk[:, i, :], ACT.Square,
                                       accum_out=ss[:, i:i + 1]).then_inc(sq, 1)
                    act.wait_ge(root_in, 1)
                    act.activation(r[:, :], r[:, :], ACT.Sqrt).then_inc(root, 1)
                    act.wait_ge(ein, 1)
                    act.activation(w8[:, :, :], z[:, :, :], ACT.Exp).then_inc(eout, 1)

                @block.vector
                def _(dve):
                    ch = dve_chain.on(dve)
                    dve.wait_ge(w_in, 96)
                    for k in range(KC):
                        ch.link(dve.tensor_scalar(wg[:, k, :], wg[:, k, :], rw[:, k:k + 1], None, ALU.mult))
                    ch.link(dve.tensor_copy(wgh[:, :, :], wg[:, :, :]))
                    dve.tensor_tensor(wgl[:, :, :], wg[:, :, :], wgh[:, :, :], ALU.subtract).then_inc(wready, 1)
                    dve.tensor_copy(cTb[:, :, :], cT[:, :].unsqueeze(2).to_broadcast([C, B, P])).then_inc(wready, 1)
                    ch.link(dve.tensor_tensor(bia[:, :], bia[:, :], bib[:, :], ALU.add))
                    for g in range(G):
                        sl = slice(g * GT, (g + 1) * GT)
                        dve.wait_ge(loaded[g], 16)
                        ch.link(dve.tensor_copy(act_hi[:, :, sl], xT[:, :, sl]))
                        dve.tensor_tensor(act_lo[:, :, sl], xT[:, :, sl], act_hi[:, :, sl],
                                          ALU.subtract).then_inc(asplit, 1)
                    dve.wait_ge(sq, NT)
                    norm_rows(ch, root_in, root, 1, ss[:, :], r[:, :], 1e-6, 1.0 / D)
                    dve.wait_ge(cbias, 1)
                    ch.link(dve.tensor_tensor(bb[:, :, :], ps[1][:, 0:B * E1].rearrange("p (b e) -> p b e", b=B),
                                              bia[:, :].unsqueeze(1).to_broadcast([P, B, E1]), ALU.add))
                    dve.wait_ge(logit, 1)
                    ch.link(dve.tensor_tensor(z[:, :, :], ps[0][:, 0:NT * E1].rearrange("p (i e) -> p i e", i=NT),
                                              r[:, :].unsqueeze(2).to_broadcast([P, NT, E1]), ALU.mult))
                    for b in range(B):
                        ch.link(dve.tensor_tensor(z[:, b * NB:(b + 1) * NB, :], z[:, b * NB:(b + 1) * NB, :],
                                                  bb[:, b, :].unsqueeze(1).to_broadcast([P, NB, E1]), ALU.add))
                    ch.link(dve.tensor_reduce(mx[:, :], z[:, :, :], AX.X, ALU.max))
                    dve.tensor_tensor(z[:, :, :], z[:, :, :], mx[:, :].unsqueeze(2).to_broadcast([P, NT, E1]),
                                      ALU.subtract).then_inc(ein, 1)
                    dve.wait_ge(eout, 1)
                    ch.link(dve.tensor_reduce(sm[:, :], w8[:, :, :], AX.X, ALU.add))
                    ch.link(dve.reciprocal(sm[:, :], sm[:, :]))
                    ch.link(dve.tensor_tensor(w8[:, :, :], w8[:, :, :],
                                              sm[:, :].unsqueeze(2).to_broadcast([P, NT, E1]), ALU.mult))
                    for i in range(NT):
                        last = dve.max(top[:, i, :], w8[:, i, :])
                    ch.link(last)
                    for i in range(NT):
                        last = dve.max_index(idx[:, i, :], top[:, i, :], w8[:, i, :])
                    ch.link(last)
                    ch.link(dve.tensor_copy(idf[:, :, :], idx[:, :, :]))
                    dve.wait_ge(idn, 3)
                    dve.wait_ge(idn, 10)
                    for n in range(2):
                        ch.link(dve.tensor_tensor(oh[n][:, :, :], io[:, :].unsqueeze(1).to_broadcast([P, NT, E1]),
                                                  idf[:, :, n:n + 1].to_broadcast([P, NT, E1]), ALU.is_equal))
                    ch.link(dve.tensor_tensor(sel[:, :, :], oh[0][:, :, :], oh[1][:, :, :], ALU.add))
                    dve.tensor_reduce(selsum[:, :], sel[:, :, :].rearrange("p i e -> p e i"), AX.X,
                                      ALU.add).then_inc(selected, 1)
                    dve.wait_ge(ranked, 1)
                    ch.link(dve.tensor_copy(cnt[:, :], ps[2][:, NT * E1:(NT + 1) * E1]))
                    ch.link(dve.tensor_tensor(cmp_[:, :, :], cnt[:, :].unsqueeze(2).to_broadcast([P, E1, T // ET]),
                                              thr[:, :].unsqueeze(1).to_broadcast([P, E1, T // ET]), ALU.is_gt))
                    ch.link(dve.tensor_reduce(nt[:, :], cmp_[:, :, :], AX.X, ALU.add))
                    ch.link(dve.tensor_scalar(nt[:, :], nt[:, :], 2.0, None, ALU.max))
                    ch.link(dve.tensor_tensor(tri8[:, :, :], tri8[:, :, :],
                                              nt[:, :].unsqueeze(1).to_broadcast([P, E1, E1]), ALU.mult))
                    ch.link(dve.tensor_reduce(bt[:, :], tri8[:, :, :], AX.X, ALU.add))
                    ch.link(dve.tensor_copy(tiles[:, 0, :], nt[:, :]))
                    ch.link(dve.tensor_copy(tiles[:, 1, :], bt[:, :]))
                    ch.link(dve.tensor_reduce(sm[:, 0:1], nt[:, :], AX.X, ALU.add))
                    ch.link(dve.tensor_scalar(tiles[:, 2, 0:1], sm[:, 0:1], -1.0, float(LONG // ET - 1),
                                              ALU.mult, ALU.add))
                    ch.link(dve.tensor_scalar(bt[:, :], bt[:, :], float(ET), float(ET), ALU.mult, ALU.add))
                    ch.link(dve.tensor_tensor(pos[:, :, :], ps[2][:, 0:NT * E1].rearrange("p (i e) -> p i e", i=NT),
                                              bt[:, :].unsqueeze(1).to_broadcast([P, NT, E1]), ALU.add))
                    for n in range(2):
                        ch.link(dve.tensor_tensor(oh[n][:, :, :], oh[n][:, :, :], pos[:, :, :], ALU.mult))
                        ch.link(dve.tensor_reduce(pf[:, :, n], oh[n][:, :, :], AX.X, ALU.add))
                    dve.tensor_copy(place[:, :, :], pf[:, :, :]).then_inc(placed, 1)

                @block.tensor
                def _(pe):
                    pe.wait_ge(wready, 2)
                    for b in range(B):
                        last = pe.matmul(ps[1][:, b * E1:(b + 1) * E1], cTb[:, b, :], gg[:, :], start=True, stop=True)
                    last.then_inc(cbias, 1)
                    w2 = (wgh, wgl)
                    for i in range(NT):
                        if i % TG == 0:
                            pe.wait_ge(asplit, i // TG + 1)
                        for n, (k, (a, b)) in enumerate((k, p) for k in range(KC) for p in PASSES):
                            last = pe.matmul(ps[0][:, i * E1:(i + 1) * E1], actT[a][:, k, i * P:(i + 1) * P],
                                             w2[b][:, k, :], start=n == 0, stop=n == 3 * KC - 1)
                    last.then_inc(logit, 1)
                    pe.wait_ge(selected, 1)
                    pe.matmul(ps[2][:, 0:NT * E1], tri[:, :], sel[:, :, :].rearrange("p i e -> p (i e)"),
                              start=True, stop=False)
                    for k in range(1, NT):
                        pe.matmul(ps[2][:, k * E1:NT * E1], ones[:, :],
                                  sel[:, 0:NT - k, :].rearrange("p i e -> p (i e)"), start=False, stop=k == NT - 1)
                    pe.matmul(ps[2][:, NT * E1:(NT + 1) * E1], ones[:, :], selsum[:, :],
                              start=False, stop=True, skip_group_check=True).then_inc(ranked, 1)

        def stage_experts1():
            win, wsp = [sem(f"e1_win{n}") for n in range(3)], sem("e1_wsplit")
            wch = sem("e1_dve")
            xin, xturned, xhi, xsp = sem("e1_xin"), sem("e1_xturned"), sem("e1_xhi"), sem("e1_xsplit")
            h_ps, evac, h_hi, h_s = sem("e1_hps"), sem("e1_evac"), sem("e1_hhi"), sem("e1_hsplit")
            o_ps, o_add, stored, zeroed = sem("e1_ops"), sem("e1_oadd"), sem("e1_stored"), sem("e1_zeroed")
            unused = sem("e1_unused")
            O2, O3 = KC * M1, KC * M1 + MC * M1
            NW = O3 + MC * D
            PARTS = ((0, O2, KC), (O2, O3, MC), (O3, NW, MC))
            CH = 2 * MC
            CP = CH // 2
            TT = ET // P
            assert TT * D == GT and 2 * ET == GT and KC * ET == GT
            with ExitStack() as st:
                def sbl(name, shape, dt=F32):
                    return st.enter_context(nc.sbuf_tensor(name, shape, dt))
                raw = sbl("e1_raw", [P, NW])
                w = [[sbl(f"e1_w{p}{h}", [P, NW], F32R) for h in "hl"] for p in range(2)]
                h1 = [sbl(f"e1_h1{h}", [P, MC, ET], F32R) for h in "hl"]
                h2 = [sbl(f"e1_h2{h}", [P, MC, ET], F32R) for h in "hl"]
                u = sbl("e1_u", [P, CP, 2, ET])
                xg, xs = sbl("e1_xg", [P, TT, D]), [sbl(f"e1_xs{h}", [P, KC, ET], F32R) for h in "hl"]
                yo, nobody = sbl("e1_yo", [P, TT, D]), sbl("e1_nobody", [P, TT, D])
                rawb, bias = sbl("e1_rawb", [P, 2, MC]), sbl("e1_bias", [P, 2, 2, MC])
                rawb3, bias3 = sbl("e1_rawb3", [P, D]), sbl("e1_bias3", [P, 2, D])
                block = st.enter_context(nc.Block())

                def experts(eng, between, step):
                    def turn(t, last):
                        for par in range(2):
                            e = bass.ds(2 * t + par, 1)
                            count = eng.value_load(tiles[0:1, 0, e], min_val=2, max_val=T // ET)
                            first = eng.value_load(tiles[0:1, 1, e], min_val=0, max_val=TILES - 3)
                            step(first, par, 1 - par, (t, par, last))
                            between(t, par, last)
                            with eng.Fori(1, count) as i:
                                step(first + i, par, par, None)
                    with eng.Fori(0, E1 // 2 - 1) as t:
                        turn(t, False)
                    turn(E1 // 2 - 1, True)
                    count = eng.value_load(tiles[0:1, 0, E1 - 1:E1], min_val=2, max_val=T // ET)
                    first = eng.value_load(tiles[0:1, 1, E1 - 1:E1], min_val=0, max_val=TILES - 3)
                    return first + count

                def load_rows(eng, n):
                    eng.dma_start(tile4(xg), rows(x_rows, n)).then_inc(xin, 16)

                rows = lambda v, n: v.rearrange("(n j p) d -> p n j d", p=P, j=TT)[:, bass.ds(n, 1), :, :]
                tile4 = lambda v: v[:, :, :].unsqueeze(1)

                @block.sync
                def _(sp):
                    def load_weights(e):
                        for n, (name, (o, o_end, c)) in enumerate(zip(("W1", "W2", "W3"), PARTS)):
                            src = d[name].rearrange("e (c p) n -> p e c n", p=P)[:, bass.ds(e, 1), :, :]
                            sp.dma_start(raw[:, o:o_end].rearrange("p (a c n) -> p a c n", a=1, c=c),
                                         src).then_inc(win[n], 16)
                            if n == 0:
                                for m in range(2):
                                    sp.dma_start(rawb[:, m:m + 1, :],
                                                 d[f"b{m + 1}_cols"][:, bass.ds(e, 1), :]).then_inc(win[n], 16)
                            if n == 2:
                                sp.dma_start(rawb3[:, :], d["b3"].rearrange("e d -> (e d)")[bass.ds(e * D, D)]
                                             .partition_broadcast(P)).then_inc(win[n], 16)

                    def store_rows(n):
                        sp.wait_ge(o_add, n + 2)
                        sp.dma_start(rows(y_rows, n), tile4(yo)).then_inc(stored, 16)

                    def step(n, par, par3, _):
                        store_rows(n)

                    def between(t, par, last):
                        if last:
                            return
                        e = 2 * t + par
                        sp.wait_ge(wsp, 3 * (e + 2))
                        load_weights(e + 2)

                    load_weights(0)
                    sp.wait_ge(wsp, 3)
                    load_weights(1)
                    n = experts(sp, between, step)
                    store_rows(n)

                @block.tensor
                def _(pe):
                    def turn_rows(n):
                        pe.wait_ge(xin, (n + 1) * 16)
                        for k in range(KC):
                            for j in range(TT):
                                last = pe.transpose(ps[5][:, k * ET + j * P:k * ET + (j + 1) * P],
                                                    xg[:, j, k * P:(k + 1) * P], ident[:, :])
                        last.then_inc(xturned, 1)

                    def hidden(wt, o, kc, src, n, half):
                        for m in range(MC):
                            c = half * MC + m
                            if m % 2 == 0:
                                pe.wait_ge(evac, n * CH + c + 2)
                            bank = ps[c // 2][:, (c % 2) * ET:(c % 2 + 1) * ET]
                            for k in range(kc):
                                if half and m == 0 and k % 2 == 0:
                                    pe.wait_ge(h_s, (n + 1) * CP + k // 2 + 1)
                                for i, (a, b) in enumerate(PASSES):
                                    last = pe.matmul(bank, wt[a][:, o + k * M1 + m * P:o + k * M1 + (m + 1) * P],
                                                     src[b][:, k, :], start=k + i == 0, stop=k == kc - 1 and i == 2)
                            last.then_inc(h_ps, 1)

                    def layer3(wt, n):
                        pe.wait_ge(h_s, (n + 1) * CP)
                        pe.wait_ge(o_add, n + 1)
                        for j in range(TT):
                            for i, (k, (a, b)) in enumerate((k, p) for k in range(MC) for p in PASSES):
                                last = pe.matmul(ps[4][:, j * D:(j + 1) * D], h2[a][:, k, j * P:(j + 1) * P],
                                                 wt[b][:, O3 + k * D:O3 + (k + 1) * D],
                                                 start=i == 0, stop=i == 3 * MC - 1)
                        last.then_inc(o_ps, 1)

                    def step(n, par, par3, at):
                        if at is not None:
                            pe.wait_ge(wsp, (2 * at[0] + at[1] + 1) * 3)
                        pe.wait_ge(xsp, n + 1)
                        hidden(w[par], 0, KC, xs, n, 0)
                        layer3(w[par3], n)
                        turn_rows(n + 1)
                        hidden(w[par], O2, MC, h1, n, 1)

                    turn_rows(0)
                    pe.wait_ge(zeroed, 5)
                    n = experts(pe, lambda *_: None, step)
                    layer3(w[1], n)

                @block.scalar
                def _(act):
                    act.nop().then_inc(evac, CH)

                    def rows_hi(n):
                        act.wait_ge(xturned, n + 1)
                        act.activation(xs[0][:, :, :], ps[5][:, :].rearrange("p (k t) -> p k t", k=KC),
                                       ACT.Copy).then_inc(xhi, 1)

                    def step(n, par, par3, at):
                        if at is not None:
                            act.wait_ge(wsp, (2 * at[0] + at[1] + 1) * 3)
                        load_rows(act, n + 2)
                        for c in range(CH):
                            if c == MC:
                                rows_hi(n + 1)
                            if c % 2 == 0:
                                act.wait_ge(h_ps, n * CH + c + 2)
                                act.wait_ge(h_s, n * CP + c // 2 + 1)
                            act.activation(u[:, c // 2, c % 2, :], ps[c // 2][:, (c % 2) * ET:(c % 2 + 1) * ET],
                                           ACT.Relu, bias=bias[:, par, c // MC, c % MC:c % MC + 1]).then_inc(evac, 1)

                    load_rows(act, 1)
                    rows_hi(0)
                    experts(act, lambda *_: None, step)

                @block.gpsimd
                def _(pool):
                    for v in (h2[0][:, :, :], h2[1][:, :, :], w[1][0][:, O3:NW], w[1][1][:, O3:NW]):
                        pool.memset(v.bitcast(F32), 0.0).then_inc(zeroed, 1)
                    pool.memset(bias3[:, 1, :], 0.0).then_inc(zeroed, 1)
                    pool.nop().then_inc(h_s, CP)
                    pool.memset(nobody[:, :, :], 0.0).then_inc(zeroed, 1)
                    pool.wait_ge(zeroed, 6)
                    count = pool.value_load(tiles[0:1, 0, E1 - 1:E1], min_val=2, max_val=T // ET)
                    first = pool.value_load(tiles[0:1, 1, E1 - 1:E1], min_val=0, max_val=TILES - 3)
                    with pool.Fori(first + count + 1, LONG // ET) as n:
                        pool.dma_start(rows(y_rows, n), tile4(nobody)).then_inc(unused, 16)

                    def step(n, par, par3, _):
                        for c in range(CP):
                            h = (h1, h2)[c // (CP // 2)]
                            k = 2 * (c % (CP // 2))
                            pool.wait_ge(h_hi, n * CP + c + 1)
                            pool.tensor_tensor(h[1][:, k:k + 2, :], u[:, c, :, :], h[0][:, k:k + 2, :],
                                               ALU.subtract).then_inc(h_s, 1)
                    n = experts(pool, lambda *_: None, step)
                    left = pool.value_load(tiles[0:1, 2, 0:1], min_val=1, max_val=LONG // ET)
                    pool.wait_ge(unused, left * 16)
                    pool.wait_ge(stored, n * 16 + 32)

                @block.vector
                def _(dve):
                    ch = Chain(dve, wch)
                    dve.nop().then_inc(o_add, 1)
                    dve.nop().then_inc(stored, 16)

                    def split_weights(par, e, n):
                        o, o_end, _ = PARTS[n]
                        dve.wait_ge(win[n], (e + 1) * (48, 16, 32)[n])
                        if n == 0:
                            ch.link(dve.tensor_copy(bias[:, par, :, :], rawb[:, :, :]))
                        if n == 2:
                            ch.link(dve.tensor_copy(bias3[:, par, :], rawb3[:, :]))
                        ch.link(dve.tensor_copy(w[par][0][:, o:o_end], raw[:, o:o_end]))
                        dve.tensor_tensor(w[par][1][:, o:o_end], raw[:, o:o_end], w[par][0][:, o:o_end],
                                          ALU.subtract).then_inc(wsp, 1)

                    def rows_lo(n):
                        dve.wait_ge(xhi, n + 1)
                        dve.tensor_tensor(xs[1][:, :, :], ps[5][:, :].rearrange("p (k t) -> p k t", k=KC),
                                          xs[0][:, :, :], ALU.subtract).then_inc(xsp, 1)

                    def hi(n, c):
                        h = (h1, h2)[c // (CP // 2)]
                        k = 2 * (c % (CP // 2))
                        dve.wait_ge(evac, (n + 1) * CH + 2 * c + 2)
                        dve.tensor_copy(h[0][:, k:k + 2, :], u[:, c, :, :]).then_inc(h_hi, 1)

                    def output(n, par3):
                        dve.wait_ge(o_ps, n + 1)
                        dve.wait_ge(stored, (n + 1) * 16)
                        dve.tensor_tensor(yo[:, :, :], ps[4][:, :].rearrange("p (j d) -> p j d", j=TT),
                                          bias3[:, par3, :].unsqueeze(1).to_broadcast([P, TT, D]),
                                          ALU.add).then_inc(o_add, 1)

                    def step(n, par, par3, at):
                        def next_weights(part):
                            if at is not None and not (at[2] and at[1]):
                                if part == 0:
                                    ch.base, ch.k = before + (2 * at[0] + at[1]) * 5, 0
                                split_weights(1 - par, 2 * at[0] + at[1] + 1, part)
                        for c in range(CP // 2):
                            hi(n, c)
                        next_weights(0)
                        output(n, par3)
                        rows_lo(n + 1)
                        next_weights(1)
                        for c in range(CP // 2, CP):
                            hi(n, c)
                        next_weights(2)

                    for n in range(3):
                        split_weights(0, 0, n)
                    before = ch.k
                    rows_lo(0)
                    dve.wait_ge(zeroed, 5)
                    n = experts(dve, lambda *_: None, step)
                    output(n, 1)

        def stage_combine():
            gathered, added = [sem(f"co_in{g}") for g in range(G)], sem("co_add")
            with ExitStack() as st:
                two = st.enter_context(nc.sbuf_tensor("co_two", [P, NT, 2, D], F32))
                block = st.enter_context(nc.Block())

                @block.gpsimd
                def _(pool):
                    for i in range(NT):
                        for n in range(2):
                            pool.indirect_dma_start(
                                out=two[:, i, n, :], out_offset=None, in_=y_rows,
                                in_offset=bass.IndirectOffsetOnAxis(ap=place[:, i, n:n + 1], axis=0))\
                                .then_inc(gathered[i // TG], 16)

                @block.vector
                def _(dve):
                    for g in range(G):
                        dve.wait_ge(gathered[g], 16 * 2 * TG)
                        for i in range(g * TG, (g + 1) * TG):
                            dve.tensor_scalar(y[:, i, :], two[:, i, 0, :], top2[:, i, 0:1], None,
                                              ALU.mult).then_inc(added, 1)
                        dve.wait_ge(added, (g + 1) * TG)
                        for i in range(g * TG, (g + 1) * TG):
                            dve.scalar_tensor_tensor(out=y[:, i, :], in0=two[:, i, 1, :], scalar=top2[:, i, 1:2],
                                                     in1=y[:, i, :], op0=ALU.mult, op1=ALU.add)

        def weights_split(dve, ch, pairs, done):
            for raw, hi, lo in pairs:
                ch.link(dve.tensor_copy(hi, raw))
                dve.tensor_tensor(lo, raw, hi, ALU.subtract).then_inc(done, 1)

        def stage_linear_attention():
            kvh = [ctx.enter_context(nc.sbuf_tensor(f"la_kv{h}", [P, B, KC, LW], F32R)) for h in "hl"]
            w_in, wsp = sem("la_win"), sem("la_wsplit")
            qps, qu, qm, qe = sem("la_qps"), sem("la_qu"), sem("la_qm"), sem("la_qe")
            kps, kt, ke, ks = sem("la_kps"), sem("la_kt"), sem("la_ke"), sem("la_ks")
            kvps, kvs, ones = sem("la_kvps"), sem("la_kvs"), sem("la_ones")
            with ExitStack() as st:
                def sbl(name, shape, dt=F32):
                    return st.enter_context(nc.sbuf_tensor(name, shape, dt))
                raw = sbl("la_raw", [P, KC, 3 * D])
                w = [sbl(f"la_w{h}", [P, KC, 3 * D], F32R) for h in "hl"]
                bq, bkv = sbl("la_bq", [P, KC]), sbl("la_bkv", [P, 2 * D])
                qu_sb, qe_sb = sbl("la_qusb", [P, 2, GT]), sbl("la_qesb", [P, 2, GT])
                kv32, kme = sbl("la_kv32", [P, 2, 2 * D]), sbl("la_kme", [P, 2, D])
                kt_s = [[sbl(f"la_kt{p}{h}", [P, 2 * D + 2], F32R) for h in "hl"] for p in range(2)]
                block = st.enter_context(nc.Block())
                NQ = KC * G

                @block.sync
                def _(sp):
                    sp.dma_start(raw[:, :, :], d["Wqkv"].rearrange("(k p) n -> p k n", p=P)).then_inc(w_in, 16)
                    sp.dma_start(bq[:, :], d["bq_cols"]).then_inc(w_in, 16)
                    sp.dma_start(bkv[:, :], d["bqkv"][D:3 * D].partition_broadcast(P)).then_inc(w_in, 16)

                @block.tensor
                def _(pe):
                    pe.wait_ge(wsp, 1)
                    for n in range(NQ):
                        m, g = n % KC, n // KC
                        if n >= 2:
                            pe.wait_ge(qu, n - 1)
                        for i, (k, (a, b)) in enumerate((k, p) for k in range(KC) for p in PASSES):
                            last = pe.matmul(ps[n % 2][:, :], w[a][:, k, m * P:(m + 1) * P],
                                             actT[b][:, k, g * GT:(g + 1) * GT], start=i == 0, stop=i == 3 * KC - 1)
                        last.then_inc(qps, 1)

                    def project(i):
                        if i >= 2:
                            pe.wait_ge(kt, i - 1)
                        for n, (k, (a, b)) in enumerate((k, p) for k in range(KC) for p in PASSES):
                            last = pe.matmul(ps[2 + i % 2][:, :], actT[a][:, k, i * P:(i + 1) * P],
                                             w[b][:, k, D:3 * D], start=n == 0, stop=n == 3 * KC - 1)
                        last.then_inc(kps, 1)

                    project(0)
                    for i in range(NT):
                        if i + 1 < NT:
                            project(i + 1)
                        pe.wait_ge(ks, i + 1)
                        b0, first, fin = i // NB, i % NB == 0, i % NB == NB - 1
                        if i == 0:
                            pe.wait_ge(ones, 6)
                        for c in range(KC):
                            for n, (a, b) in enumerate(PASSES):
                                last = pe.matmul(ps[4 + 2 * (b0 % 2) + c][:, 0:LW], kt_s[i % 2][a][:, c * P:(c + 1) * P],
                                                 kt_s[i % 2][b][:, D:D + LW], start=first and n == 0,
                                                 stop=fin and n == 2)
                        last.then_inc(kvps, 1)

                @block.scalar
                def _(act):
                    act.wait_ge(w_in, 48)
                    for n in range(NQ):
                        act.wait_ge(qps, n + 1)
                        if n >= 2:
                            act.wait_ge(qe, n - 1)
                        act.activation(qu_sb[:, n % 2, :], ps[n % 2][:, :], ACT.Identity,
                                       bias=bq[:, n % KC:n % KC + 1]).then_inc(qu, 1)
                        act.wait_ge(qm, 2 * n + 1)
                        act.activation(qe_sb[:, n % 2, :], qe_sb[:, n % 2, :], ACT.Exp).then_inc(qm, 1)
                    for i in range(NT):
                        act.wait_ge(ke, 2 * i + 1)
                        act.activation(kme[:, i % 2, :], kme[:, i % 2, :], ACT.Exp).then_inc(ke, 1)

                @block.gpsimd
                def _(pool):
                    for p_ in range(2):
                        pool.memset(kt_s[p_][0][:, 2 * D:2 * D + 2].bitcast(F32), 0.0).then_inc(ones, 1)
                        pool.memset(kt_s[p_][1][:, 2 * D:2 * D + 2].bitcast(F32), 0.0).then_inc(ones, 1)
                    pool.wait_ge(ones, 4)
                    for p_ in range(2):
                        pool.memset(kt_s[p_][0][:, 2 * D:2 * D + 1].bitcast(F32), 1.0).then_inc(ones, 1)

                @block.vector
                def _(dve):
                    ch = dve_chain.on(dve)
                    dve.wait_ge(w_in, 48)
                    weights_split(dve, ch, [(raw[:, :, :], w[0][:, :, :], w[1][:, :, :])], wsp)
                    for n in range(NQ):
                        m, g = n % KC, n // KC
                        sl = slice(g * GT, (g + 1) * GT)
                        dve.wait_ge(qu, n + 1)
                        dve.tensor_scalar(qe_sb[:, n % 2, :], qu_sb[:, n % 2, :], 0.0, None, ALU.min).then_inc(qm, 1)
                        dve.wait_ge(qm, 2 * n + 2)
                        ch.link(dve.scalar_tensor_tensor(out=qu_sb[:, n % 2, :], in0=qu_sb[:, n % 2, :], scalar=0.0,
                                                         in1=qe_sb[:, n % 2, :], op0=ALU.max, op1=ALU.add))
                        ch.link(dve.tensor_copy(qp[0][:, m, sl], qu_sb[:, n % 2, :]))
                        dve.tensor_tensor(qp[1][:, m, sl], qu_sb[:, n % 2, :], qp[0][:, m, sl],
                                          ALU.subtract).then_inc(qe, 1)
                        dve.wait_ge(qe, n + 1)
                    for i in range(NT):
                        s_ = i % 2
                        dve.wait_ge(kps, i + 1)
                        dve.tensor_tensor(kv32[:, s_, :], ps[2 + s_][:, :], bkv[:, :], ALU.add).then_inc(kt, 1)
                        dve.wait_ge(kt, i + 1)
                        dve.tensor_scalar(kme[:, s_, :], kv32[:, s_, 0:D], 0.0, None, ALU.min).then_inc(ke, 1)
                        dve.wait_ge(ke, 2 * i + 2)
                        ch.link(dve.scalar_tensor_tensor(out=kv32[:, s_, 0:D], in0=kv32[:, s_, 0:D], scalar=0.0,
                                                         in1=kme[:, s_, :], op0=ALU.max, op1=ALU.add))
                        if i >= 2:
                            dve.wait_ge(kvps, i - 1)
                        ch.link(dve.tensor_copy(kt_s[s_][0][:, 0:2 * D], kv32[:, s_, :]))
                        dve.tensor_tensor(kt_s[s_][1][:, 0:2 * D], kv32[:, s_, :], kt_s[s_][0][:, 0:2 * D],
                                          ALU.subtract).then_inc(ks, 1)
                        dve.wait_ge(ks, i + 1)
                    for b in range(B):
                        dve.wait_ge(kvps, (b + 1) * NB)
                        for c in range(KC):
                            bank = ps[4 + 2 * (b % 2) + c][:, 0:LW]
                            ch.link(dve.tensor_copy(kvh[0][:, b, c, :], bank))
                            ch.link(dve.tensor_tensor(kvh[1][:, b, c, :], bank, kvh[0][:, b, c, :], ALU.subtract))
            return kvh

        def layer_norm(ch, dve, act_sems, src, stats, mv, rstd, gb, n_done, eps=1e-5):
            req, ack = act_sems
            for i in range(NT):
                last = dve.bn_stats(stats[:, i, :], src[:, i, :])
            ch.link(last)
            for i in range(NT):
                last = dve.bn_aggr(mv[:, i, :], stats[:, i, :])
            ch.link(last)
            norm_rows(ch, req, ack, n_done, mv[:, :, 1], rstd[:, :], eps)
            for i in range(NT):
                last = dve.tensor_scalar(src[:, i, :], src[:, i, :], mv[:, i, 0:1], rstd[:, i:i + 1],
                                         ALU.subtract, ALU.mult)
            ch.link(last)
            for n, op in enumerate((ALU.mult, ALU.add)):
                ch.link(dve.tensor_tensor(src[:, :, :], src[:, :, :],
                                          gb[:, n, :].unsqueeze(1).to_broadcast([P, NT, D]), op))

        def stage_linear_out(kvh):
            nps, nuse = sem("lo_ps"), sem("lo_used")
            req, ack, gin = sem("lo_req"), sem("lo_ack"), sem("lo_gin")
            with ExitStack() as st:
                def sbl(name, shape, dt=F32):
                    return st.enter_context(nc.sbuf_tensor(name, shape, dt))
                den = sbl("lo_den", [P, NT])
                stats, mv, rstd = sbl("lo_stats", [P, NT, 6]), sbl("lo_mv", [P, NT, 2]), sbl("lo_rstd", [P, NT])
                gb = sbl("lo_gb", [P, 2, D])
                block = st.enter_context(nc.Block())

                @block.sync
                def _(sp):
                    for n, name in enumerate(("g1", "be1")):
                        sp.dma_start(gb[:, n, :], d[name].partition_broadcast(P)).then_inc(gin, 16)

                @block.tensor
                def _(pe):
                    for i in range(NT):
                        if i >= 4:
                            pe.wait_ge(nuse, i - 3)
                        for n, (c, (a, b)) in enumerate((c, p) for c in range(KC) for p in PASSES):
                            last = pe.matmul(ps[i % 4][:, 0:LW], qp[a][:, c, i * P:(i + 1) * P],
                                             kvh[b][:, i // NB, c, :], start=n == 0, stop=n == 3 * KC - 1)
                        last.then_inc(nps, 1)

                @block.scalar
                def _(act):
                    act.wait_ge(req, 1)
                    act.activation(rstd[:, :], rstd[:, :], ACT.Sqrt).then_inc(ack, 1)

                @block.vector
                def _(dve):
                    ch = dve_chain.on(dve)
                    for i in range(NT):
                        dve.wait_ge(nps, i + 1)
                        ch.link(dve.tensor_scalar(den[:, i:i + 1], ps[i % 4][:, D:D + 1], 1e-6, None, ALU.add))
                        ch.link(dve.reciprocal(den[:, i:i + 1], den[:, i:i + 1]))
                        dve.scalar_tensor_tensor(out=y[:, i, :], in0=ps[i % 4][:, 0:D], scalar=den[:, i:i + 1],
                                                 in1=y[:, i, :], op0=ALU.mult, op1=ALU.add).then_inc(nuse, 1)
                    dve.wait_ge(nuse, NT)
                    dve.wait_ge(gin, 32)
                    layer_norm(ch, dve, (req, ack), y, stats, mv, rstd, gb, 1)

        def stage_feed_forward():
            w_in, wsp = sem("ff_win"), sem("ff_wsplit")
            hps, sil, hsp, hhi = sem("ff_hps"), sem("ff_silu"), sem("ff_hsplit"), sem("ff_hhi")
            h32d, ops, used = sem("ff_h32"), sem("ff_ops"), sem("ff_used")
            req, ack, gin = sem("ff_req"), sem("ff_ack"), sem("ff_gin")
            padded = sem("ff_padded")
            with ExitStack() as st:
                def sbl(name, shape, dt=F32):
                    return st.enter_context(nc.sbuf_tensor(name, shape, dt))
                raw = sbl("ff_raw", [P, KC, F])
                wg = [sbl(f"ff_wg{h}", [P, KC, FC * P], F32R) for h in "hl"]
                wu = [sbl(f"ff_wu{h}", [P, KC, FC * P], F32R) for h in "hl"]
                wd = [sbl(f"ff_wd{h}", [P, FC, D], F32R) for h in "hl"]
                bg, bu = sbl("ff_bg", [P, FC]), sbl("ff_bu", [P, FC])
                sl_sb, h32 = sbl("ff_silusb", [P, 2, GT]), sbl("ff_h32sb", [P, 2, GT])
                hh = [sbl(f"ff_h{h}", [P, FC, GT], F32R) for h in "hl"]
                gb = sbl("ff_gb", [P, 3, D])
                stats, mv, rstd = sbl("ff_stats", [P, NT, 6]), sbl("ff_mv", [P, NT, 2]), sbl("ff_rstd", [P, NT])
                block = st.enter_context(nc.Block())

                @block.sync
                def _(sp):
                    sp.wait_ge(padded, 2)
                    sp.dma_start(raw[:, :, :], d["Wg"].rearrange("(k p) n -> p k n", p=P)).then_inc(w_in, 16)
                    for v, s_ in ((bg, "bg"), (bu, "bu")):
                        sp.dma_start(v[:, 0:FC - 1], d[s_ + "_cols"]).then_inc(gin, 16)
                        sp.dma_start(v[0:FR, FC - 1:FC], d[s_][(FC - 1) * P:F].rearrange("(p a) -> p a", a=1), allow_slow_non_contiguous=True).then_inc(gin, 16)
                    for n, name in enumerate(("g2", "be2", "bd")):
                        sp.dma_start(gb[:, n, :], d[name].partition_broadcast(P)).then_inc(gin, 16)
                    sp.wait_ge(wsp, 1)
                    sp.dma_start(raw[:, :, :], d["Wu"].rearrange("(k p) n -> p k n", p=P)).then_inc(w_in, 16)
                    sp.wait_ge(wsp, 2)
                    rawd = raw[:, :, :].rearrange("p k n -> p (k n)")
                    sp.dma_start(rawd[:, 0:(FC - 1) * D].rearrange("p (c n) -> p c n", n=D),
                                 d["Wd"][0:(FC - 1) * P].rearrange("(c p) n -> p c n", p=P)).then_inc(w_in, 16)
                    sp.wait_ge(wsp, 3)
                    sp.dma_start(rawd[0:FR, 0:D], d["Wd"][(FC - 1) * P:F]).then_inc(w_in, 16)

                @block.tensor
                def _(pe):
                    def up(s):
                        g, m = s // FC, s % FC
                        for v, (wt, bank) in enumerate(((wg, ps[s % 2]), (wu, ps[2 + s % 2]))):
                            if s == 0:
                                pe.wait_ge(wsp, v + 1)
                            if s >= 2:
                                pe.wait_ge((sil, h32d)[v], s - 1)
                            for n, (k, (a, b)) in enumerate((k, p) for k in range(KC) for p in PASSES):
                                last = pe.matmul(bank[:, :], wt[a][:, k, m * P:(m + 1) * P],
                                                 actT[b][:, k, g * GT:(g + 1) * GT], start=n == 0,
                                                 stop=n == 3 * KC - 1)
                            last.then_inc(hps, 1)

                    def down(g):
                        if g == 0:
                            pe.wait_ge(wsp, 4)
                        pe.wait_ge(hsp, (g + 1) * FC)
                        for j in range(TG):
                            i = g * TG + j
                            if i >= 4:
                                pe.wait_ge(used, i - 3)
                            for n, (m, (a, b)) in enumerate((m, p) for m in range(FC) for p in PASSES):
                                last = pe.matmul(ps[4 + j][:, 0:D], hh[a][:, m, j * P:(j + 1) * P],
                                                 wd[b][:, m, :], start=n == 0, stop=n == 3 * FC - 1)
                            last.then_inc(ops, 1)

                    up(0)
                    for g in range(G):
                        for m in range(1, FC):
                            up(g * FC + m)
                        if g + 1 < G:
                            up((g + 1) * FC)
                        down(g)

                @block.scalar
                def _(act):
                    act.wait_ge(gin, 16 * 7)
                    for s in range(G * FC):
                        m = s % FC
                        act.wait_ge(hps, 2 * s + 1)
                        if s >= 2:
                            act.wait_ge(h32d, s - 1)
                        act.activation(sl_sb[:, s % 2, :], ps[s % 2][:, :], ACT.Silu,
                                       bias=bg[:, m:m + 1]).then_inc(sil, 1)
                    act.wait_ge(req, 1)
                    act.activation(rstd[:, :], rstd[:, :], ACT.Sqrt).then_inc(ack, 1)

                @block.gpsimd
                def _(pool):
                    pool.memset(bg[:, FC - 1:FC], 0.0).then_inc(padded, 1)
                    pool.memset(bu[:, FC - 1:FC], 0.0).then_inc(padded, 1)
                    for s in range(G * FC):
                        m = s % FC
                        pool.wait_ge(hhi, s + 1)
                        pool.tensor_tensor(hh[1][:, m, :], h32[:, s % 2, :], hh[0][:, m, :],
                                           ALU.subtract).then_inc(hsp, 1)

                @block.vector
                def _(dve):
                    ch = dve_chain.on(dve)
                    for part in range(2):
                        for wt in (wg, wu):
                            dve.memset(wt[part][:, :, F:FC * P].bitcast(F32), 0.0)
                        last = dve.memset(wd[part][:, FC - 1, :].bitcast(F32), 0.0)
                    ch.link(last)
                    for n, (wt) in enumerate((wg, wu)):
                        dve.wait_ge(w_in, 16 * (n + 1))
                        weights_split(dve, ch, [(raw[:, :, :], wt[0][:, :, 0:F], wt[1][:, :, 0:F])], wsp)
                    rawd = raw[:, :, :].rearrange("p k n -> p (k n)")
                    dve.wait_ge(w_in, 48)
                    weights_split(dve, ch, [(rawd[:, 0:(FC - 1) * D], wd[0][:, 0:FC - 1, :].rearrange("p c n -> p (c n)"),
                                             wd[1][:, 0:FC - 1, :].rearrange("p c n -> p (c n)"))], wsp)
                    dve.wait_ge(w_in, 64)
                    weights_split(dve, ch, [(rawd[0:FR, 0:D], wd[0][0:FR, FC - 1, :], wd[1][0:FR, FC - 1, :])], wsp)
                    dve.wait_ge(gin, 16 * 7)
                    ch.link(dve.tensor_tensor(y[:, :, :], y[:, :, :],
                                              gb[:, 2, :].unsqueeze(1).to_broadcast([P, NT, D]), ALU.add))

                    def hidden(s):
                        m = s % FC
                        dve.wait_ge(sil, s + 1)
                        dve.wait_ge(hps, 2 * s + 2)
                        if s >= 2:
                            dve.wait_ge(hsp, s - 1)
                        dve.scalar_tensor_tensor(out=h32[:, s % 2, :], in0=ps[2 + s % 2][:, :],
                                                 scalar=bu[:, m:m + 1], in1=sl_sb[:, s % 2, :],
                                                 op0=ALU.add, op1=ALU.mult).then_inc(h32d, 1)
                        dve.wait_ge(h32d, s + 1)
                        if s >= FC:
                            dve.wait_ge(ops, (s // FC) * TG)
                        dve.tensor_copy(hh[0][:, m, :], h32[:, s % 2, :]).then_inc(hhi, 1)

                    def add(g):
                        for j in range(TG):
                            i = g * TG + j
                            dve.wait_ge(ops, i + 1)
                            dve.tensor_tensor(y[:, i, :], ps[4 + j][:, 0:D], y[:, i, :], ALU.add).then_inc(used, 1)

                    for g in range(G):
                        for m in range(FC):
                            hidden(g * FC + m)
                        add(g)
                    dve.wait_ge(used, NT)
                    layer_norm(ch, dve, (req, ack), y, stats, mv, rstd, gb, 1)

        def stage_residual():
            xin, radd = [sem(f"re_x{g}") for g in range(G)], sem("re_add")
            with ExitStack() as st:
                xk = st.enter_context(nc.sbuf_tensor("re_xtok", [P, NT, D], F32))
                block = st.enter_context(nc.Block())

                @block.sync
                def _(sp):
                    for g in range(G):
                        sp.dma_start(xk[:, g * TG:(g + 1) * TG, :], x_tok[:, g * TG:(g + 1) * TG, :]).then_inc(xin[g], 16)

                @block.vector
                def _(dve):
                    for g in range(G):
                        sl = slice(g * TG, (g + 1) * TG)
                        dve.wait_ge(xin[g], 16)
                        dve.tensor_tensor(y[:, sl, :], y[:, sl, :], xk[:, sl, :], ALU.add).then_inc(radd, 1)

        def stage_project(kT, v_tok, n_live, live_at, mbias, pen, onesb, identb):
            w_in, wsp = sem("pj_win"), sem("pj_wsplit")
            qps, qhi, qlo, vps, vev = (sem(f"pj_{x}") for x in ("qps", "qhi", "qlo", "vps", "vev"))
            m_in, cnt_in, cnt_ps, mready, cset = (sem(f"pj_{x}") for x in ("min", "cntin", "cntps", "mready", "cset"))
            with ExitStack() as st:
                def sbl(name, shape, dt=F32):
                    return st.enter_context(nc.sbuf_tensor(name, shape, dt))
                raw = sbl("pj_raw", [P, 3, KC, D])
                w = [sbl(f"pj_w{h}", [P, 3, KC, D], F32R) for h in "hl"]
                m32 = sbl("pj_m32", [P, QT, S // 4], I32)
                m8 = m32[:, :, :].bitcast(U8)
                free = sbl("pj_free", [P, QT, QT])
                cnt, rc, keys = sbl("pj_cnt", [P, QT]), sbl("pj_rc", [P, QT]), sbl("pj_keys", [P, QT])
                one = sbl("pj_one", [P, P])
                rank, rb, srt = sbl("pj_rank", [P, QT]), sbl("pj_rb", [P, QT]), sbl("pj_srt", [P, 8])
                lv, nl = sbl("pj_lv", [P, QT]), sbl("pj_nl", [P, 1])
                block = st.enter_context(nc.Block())

                @block.sync
                def _(sp):
                    for n, name in enumerate(("WqT", "WkT", "WvT")):
                        sp.dma_start(raw[:, n, :, :], d[name].rearrange("(k p) n -> p k n", p=P)).then_inc(w_in, 16)
                    sp.dma_start(m32[:, :, :], d["mask"].rearrange("(q p) t -> p q t", p=P)).then_inc(m_in, 16)

                @block.gpsimd
                def _(pool):
                    pool.memset(one[:, :], 1.0).then_inc(cset, 1)
                    pool.iota(rank[:, :], pattern=[[1, QT]], base=0, channel_multiplier=0,
                              allow_small_or_imprecise_dtypes=True).then_inc(cset, 1)

                @block.tensor
                def _(pe):
                    u = 0
                    for n in range(2):
                        pe.wait_ge(wsp, n + 1)
                        for m in range(KC):
                            for g in range(G):
                                if u >= 4:
                                    pe.wait_ge(qlo, u - 3)
                                for i, (k, (a, b)) in enumerate((k, p) for k in range(KC) for p in PASSES):
                                    last = pe.matmul(ps[u % 4][:, :], w[a][:, n, k, m * P:(m + 1) * P],
                                                     actT[b][:, k, g * GT:(g + 1) * GT], start=i == 0,
                                                     stop=i == 3 * KC - 1)
                                last.then_inc(qps, 1)
                                u += 1
                    pe.wait_ge(wsp, 3)
                    for i in range(NT):
                        if i >= 3:
                            pe.wait_ge(vev, i - 2)
                        for n, (k, (a, b)) in enumerate((k, p) for k in range(KC) for p in PASSES):
                            last = pe.matmul(ps[4 + i % 3][:, 0:D], actT[a][:, k, i * P:(i + 1) * P],
                                             w[b][:, 2, k, :], start=n == 0, stop=n == 3 * KC - 1)
                        last.then_inc(vps, 1)
                    pe.wait_ge(cset, 2)
                    pe.wait_ge(cnt_in, 1)
                    pe.matmul(ps[7][:, 0:QT], one[:, :], keys[:, :], start=True, stop=True).then_inc(cnt_ps, 1)

                @block.scalar
                def _(act):
                    for u in range(2 * KC * G):
                        m, g = u // G % KC, u % G
                        dst = (qp, kT)[u // (KC * G)][0]
                        act.wait_ge(qps, u + 1)
                        act.activation(dst[:, m, g * GT:(g + 1) * GT], ps[u % 4][:, :], ACT.Copy).then_inc(qhi, 1)
                    for i in range(NT):
                        act.wait_ge(vps, i + 1)
                        act.activation(v_tok[:, i, :], ps[4 + i % 3][:, 0:D], ACT.Copy).then_inc(vev, 1)

                @block.vector
                def _(dve):
                    ch = dve_chain.on(dve)
                    for n in range(3):
                        dve.wait_ge(w_in, 48)
                        weights_split(dve, ch, [(raw[:, n, :, :], w[0][:, n, :, :], w[1][:, n, :, :])], wsp)
                    for u in range(2 * KC * G):
                        m, g = u // G % KC, u % G
                        hi, lo = (qp, kT)[u // (KC * G)]
                        sl = slice(g * GT, (g + 1) * GT)
                        dve.wait_ge(qhi, u + 1)
                        dve.tensor_tensor(lo[:, m, sl], ps[u % 4][:, :], hi[:, m, sl], ALU.subtract).then_inc(qlo, 1)
                    dve.wait_ge(m_in, 16)
                    dve.tensor_scalar(mbias[:, :, :], m8, MASKED, None, ALU.mult).then_inc(mready, 1)
                    ch.link(dve.tensor_copy(identb[:, :], ident[:, :]))
                    ch.link(dve.tensor_reduce(free[:, :, :], m8.rearrange("p q (j t) -> p q j t", t=P),
                                              AX.X, ALU.add))
                    ch.link(dve.tensor_scalar(free[:, :, :], free[:, :, :], -1.0, float(P), ALU.mult, ALU.add))
                    ch.link(dve.tensor_reduce(cnt[:, :], free[:, :, :], AX.X, ALU.add))
                    ch.link(dve.reciprocal(rc[:, :], cnt[:, :]))
                    ch.link(dve.tensor_scalar(pen[:, :], rc[:, :], 0.0, None, ALU.mult))
                    dve.tensor_reduce(keys[:, :], free[:, :, :].rearrange("p q j -> p j q"), AX.X,
                                      ALU.add).then_inc(cnt_in, 1)
                    dve.wait_ge(cnt_ps, 1)
                    ch.link(dve.tensor_scalar(lv[:, :], ps[7][:, 0:QT], 0.0, None, ALU.is_gt))
                    ch.link(dve.tensor_reduce(nl[:, :], lv[:, :], AX.X, ALU.add))
                    ch.link(dve.tensor_scalar(nl[:, :], nl[:, :], 1.0, None, ALU.max))
                    ch.link(dve.tensor_copy(n_live[:, :], nl[:, :]))
                    dve.wait_ge(cset, 2)
                    ch.link(dve.tensor_scalar(rb[:, :], lv[:, :], 1000.0, -900.0, ALU.mult, ALU.add))
                    ch.link(dve.tensor_tensor(rb[:, :], rb[:, :], rank[:, :], ALU.subtract))
                    ch.link(dve.max(srt[:, :], rb[:, :]))
                    ch.link(dve.tensor_scalar(srt[:, :], srt[:, :], -1.0, 100.0, ALU.mult, ALU.add))
                    ch.link(dve.tensor_scalar(rb[:, :], srt[:, :], float(QT), None, ALU.is_lt))
                    ch.link(dve.tensor_tensor(srt[:, :], srt[:, :], rb[:, :], ALU.mult))
                    ch.link(dve.tensor_copy(live_at[:, :], srt[:, :]))
                    dve.wait_ge(mready, 1)

        def stage_attention(kT, v_tok, n_live, live_at, mbias, pen, identb):
            names = ("init", "kbhi", "kblo", "vb", "mb", "sps", "red", "mnew", "diff", "moved", "sub", "pex",
                     "ptps", "ptev", "pvps", "scaled", "added", "fin")
            (init, kb_hi, kb_lo, vb_set, mb_set, sps, red, mnew, diff, moved, sub, pex,
             ptps, ptev, pvps, scaled, added, fin) = (sem(f"at_{x}") for x in names)
            with ExitStack() as st:
                def sbl(name, shape, dt=F32):
                    return st.enter_context(nc.sbuf_tensor(name, shape, dt))
                hm = sbl("at_hm", [P, HC])
                ones = sbl("at_ones", [P, HC])
                assert KC * T == B * KC * HC * P
                kb = [v[:, :, :].rearrange("p k t -> p (k t)").rearrange("p (b c h t) -> p b c h t", b=B, c=KC, h=HC)
                      for v in actT]
                vb = sbl("at_vb", [P, B, NH, HD + 1])
                mb = sbl("at_mb", [P, QT, P], BF16)
                NP = HC * P
                pn = sbl("at_pn", [P, 2, NP + HC])
                pT = sbl("at_pT", [P, 2, HC, P])
                mx = sbl("at_mx", [P, B, QT, NH])
                mn = sbl("at_mn", [P, 2, HC])
                acc = sbl("at_acc", [P, B, QT, NH, HD + 1])
                rc = sbl("at_rc", [P, B * QT, NH])
                block = st.enter_context(nc.Block())
                NSTEP = QT * KC
                NS = B * NSTEP
                HB = GT // P
                SCALE = float(HD) ** -0.5
                scr = lambda s: psum[:, 2 * (s % 2):2 * (s % 2) + 2, :].rearrange("p b (h t) -> p (b h) t", t=P)
                ptb = psum[:, 4:6, :].rearrange("p b (h t) -> p (b h) t", t=P)
                at = lambda s: (s // NSTEP, (s % NSTEP) // KC, s % KC)
                hs = lambda c: slice(c * HC, (c + 1) * HC)

                def key_tile(eng, part, b, c, jt):
                    return eng.tensor_tensor(
                        kb[part][:, b, c, :, :],
                        kT[part][:, c, bass.ds(b * S + jt * P, P)].unsqueeze(1).to_broadcast([P, HC, P]),
                        hm[:, :].unsqueeze(2).to_broadcast([P, HC, P]), ALU.mult)

                @block.tensor
                def _(pe):
                    n = nc.tensor.value_load(n_live[0:1, 0:1], min_val=1, max_val=QT)
                    pe.nop().then_inc(ptps, 2)

                    def scores(j, s):
                        b, u, c = at(s)
                        step = j * NS + s
                        if s % NSTEP < KC:
                            pe.wait_ge(kb_hi, (j * B + b) * KC + c + 1)
                            pe.wait_ge(kb_lo, (j * B + b) * KC + c + 1)
                        if s == 0:
                            pe.wait_ge(mb_set, j + 1)
                            pe.wait_ge(vb_set, j + 1)
                        pe.wait_ge(sub, step + 1)
                        for h2 in range(HC // HB):
                            bank = ps[2 * (s % 2) + h2]
                            for i, (a, b_) in enumerate(PASSES):
                                pe.matmul(bank[:, :], qp[a][:, c, b * S + u * P:b * S + (u + 1) * P],
                                          kb[b_][:, b, c, h2 * HB:(h2 + 1) * HB, :], start=i == 0, stop=False)
                            last = pe.matmul(bank[:, :], identb[:, :],
                                             mb[:, u, :].unsqueeze(1).to_broadcast([P, HB, P]),
                                             start=False, stop=True)
                        last.then_inc(sps, 1)

                    def turn_over(j, s):
                        step = j * NS + s
                        pe.wait_ge(pex, step + 1)
                        pe.wait_ge(ptev, step + 1)
                        for h in range(HC):
                            last = pe.transpose(ptb[:, h, :], pn[:, s % 2, h * P:(h + 1) * P], ident[:, :])
                        last.then_inc(ptps, 1)

                    def values(j, s):
                        b, u, c = at(s)
                        step = j * NS + s
                        pe.wait_ge(ptev, step + 2)
                        pe.wait_ge(added, step + NS - 1)
                        for h in range(HC):
                            last = pe.matmul(ps[6 + s % 2][:, h * (HD + 1):(h + 1) * (HD + 1)],
                                             pT[:, s % 2, h, :], vb[:, b, c * HC + h, :],
                                             start=True, stop=True)
                        last.then_inc(pvps, 1)

                    with pe.Fori(0, n) as j:
                        scores(j, 0)
                        scores(j, 1)
                        for s in range(NS):
                            if s + 2 < NS:
                                scores(j, s + 2)
                            turn_over(j, s)
                            if s:
                                values(j, s - 1)
                        values(j, NS - 1)

                @block.scalar
                def _(act):
                    n = nc.scalar.value_load(n_live[0:1, 0:1], min_val=1, max_val=QT)
                    act.nop().then_inc(ptev, 1)

                    def exponentials(j, s):
                        step = j * NS + s
                        act.wait_ge(moved, step + NS + 1)
                        act.wait_ge(sub, step + 3)
                        act.activation(pn[:, s % 2, :], pn[:, s % 2, :], ACT.Exp, scale=SCALE).then_inc(pex, 1)

                    with act.Fori(0, n) as j:
                        exponentials(j, 0)
                        for s in range(NS):
                            if s + 1 < NS:
                                exponentials(j, s + 1)
                            act.wait_ge(ptps, j * NS + s + 3)
                            act.activation(pT[:, s % 2, :, :], ptb, ACT.Copy).then_inc(ptev, 1)

                @block.gpsimd
                def _(pool):
                    n = nc.gpsimd.value_load(n_live[0:1, 0:1], min_val=1, max_val=QT)
                    pool.memset(hm[:, :], 1.0).then_inc(init, 1)
                    pool.wait_ge(init, 1)
                    pool.affine_select(out=hm[:, :], in_=hm[:, :], compare_op=ALU.is_ge, fill=0.0, base=0,
                                       pattern=[[-HD, HC]], channel_multiplier=1).then_inc(init, 1)
                    pool.wait_ge(init, 2)
                    pool.affine_select(out=hm[:, :], in_=hm[:, :], compare_op=ALU.is_ge, fill=0.0, base=HD - 1,
                                       pattern=[[HD, HC]], channel_multiplier=-1).then_inc(init, 1)
                    pool.memset(vb[:, :, :, HD:HD + 1], 1.0).then_inc(init, 1)
                    pool.memset(ones[:, :], 1.0).then_inc(init, 1)
                    pool.memset(mx[:, :, :, :], 3.0 * MASKED).then_inc(init, 1)
                    pool.memset(acc[:, :, :, :, :], 0.0).then_inc(init, 1)
                    pool.wait_ge(init, 7)
                    pool.nop().then_inc(moved, NS)
                    pool.nop().then_inc(scaled, 2)

                    def scale(j, s):
                        b, u, c = at(s)
                        step = j * NS + s
                        pool.wait_ge(pex, step + 1)
                        pool.wait_ge(added, step + 1)
                        pool.tensor_tensor(acc[:, b, u, hs(c), :], acc[:, b, u, hs(c), :],
                                           pn[:, s % 2, NP:NP + HC].unsqueeze(2).to_broadcast([P, HC, HD + 1]),
                                           ALU.mult).then_inc(scaled, 1)

                    def factor(j, s):
                        b, u, c = at(s)
                        step = j * NS + s
                        pool.wait_ge(mnew, step + 1)
                        pool.wait_ge(scaled, step + 1)
                        pool.wait_ge(moved, step + 1)
                        pool.tensor_tensor(pn[:, s % 2, NP:NP + HC], mx[:, b, u, hs(c)], mn[:, s % 2, :],
                                           ALU.subtract).then_inc(diff, 1)
                        pool.wait_ge(diff, step + 1)
                        pool.tensor_tensor(mx[:, b, u, hs(c)], mn[:, s % 2, :], ones[:, :],
                                           ALU.mult).then_inc(moved, 1)

                    with pool.Fori(0, n) as j:
                        jt = nc.gpsimd.value_load(live_at[0:1, bass.ds(j, 1)], min_val=0, max_val=QT - 1)
                        pool.wait_ge(added, (j + 1) * NS)
                        for c in range(KC):
                            key_tile(pool, 1, 0, c, jt).then_inc(kb_lo, 1)
                        pool.tensor_copy(vb[:, :, :, 0:HD], v_tok[:, :, :].rearrange("p (b q) (h e) -> p b q h e", b=B, e=HD)
                                         [:, :, bass.ds(jt, 1), :, :].rearrange("p b q h e -> p (b q) h e")).then_inc(vb_set, 1)
                        for s in range(NS):
                            if s >= 2:
                                scale(j, s - 2)
                            factor(j, s)
                            if s % NSTEP in (2, 6) and s // NSTEP + 1 < B:
                                key_tile(pool, 1, s // NSTEP + 1, s % NSTEP // 4, jt).then_inc(kb_lo, 1)
                        for s in range(NS - 2, NS):
                            scale(j, s)

                @block.vector
                def _(dve):
                    n = nc.vector.value_load(n_live[0:1, 0:1], min_val=1, max_val=QT)
                    dve.wait_ge(init, 7)
                    dve.nop().then_inc(sub, 2)
                    dve.nop().then_inc(added, NS)
                    LAG = 4

                    def add(j, s):
                        b, u, c = at(s)
                        step = j * NS + s
                        dve.wait_ge(scaled, step + 3)
                        dve.wait_ge(pvps, step + 1)
                        dve.tensor_tensor(acc[:, b, u, hs(c), :],
                                          ps[6 + s % 2][:, 0:HC * (HD + 1)].rearrange("p (h e) -> p h e", e=HD + 1),
                                          acc[:, b, u, hs(c), :], ALU.add).then_inc(added, 1)

                    with dve.Fori(0, n) as j:
                        jt = nc.vector.value_load(live_at[0:1, bass.ds(j, 1)], min_val=0, max_val=QT - 1)
                        dve.wait_ge(added, (j + 1) * NS)
                        for c in range(KC):
                            key_tile(dve, 0, 0, c, jt).then_inc(kb_hi, 1)
                        dve.tensor_copy(mb[:, :, :], mbias[:, :, bass.ds(jt * P, P)]).then_inc(mb_set, 1)
                        for s in range(NS):
                            b, u, c = at(s)
                            step = j * NS + s
                            dve.wait_ge(sps, step + 1)
                            dve.wait_ge(moved, step + NS - 1)
                            dve.wait_ge(sub, step + 1)
                            dve.tensor_reduce(mn[:, s % 2, :], scr(s), AX.X, ALU.max).then_inc(red, 1)
                            if s >= LAG:
                                add(j, s - LAG)
                            if s % NSTEP in (2, 6) and b + 1 < B:
                                key_tile(dve, 0, b + 1, s % NSTEP // 4, jt).then_inc(kb_hi, 1)
                            dve.wait_ge(red, step + 1)
                            dve.tensor_tensor(mn[:, s % 2, :], mn[:, s % 2, :], mx[:, b, u, hs(c)], ALU.max).then_inc(mnew, 1)
                            dve.wait_ge(mnew, step + 1)
                            dve.wait_ge(ptps, step + 1)
                            dve.tensor_tensor(pn[:, s % 2, 0:NP].rearrange("p (h t) -> p h t", t=P), scr(s),
                                              mn[:, s % 2, :].unsqueeze(2).to_broadcast([P, HC, P]),
                                              ALU.subtract).then_inc(sub, 1)
                        for s in range(NS - LAG, NS):
                            add(j, s)
                    dve.wait_ge(added, (n + 1) * NS)
                    dve.reciprocal(rc[:, :, :], acc[:, :, :, :, HD].rearrange("p b u h -> p (b u) h")).then_inc(fin, 1)
                    dve.wait_ge(fin, 1)
                    for b in range(B):
                        last = dve.tensor_tensor(rc[:, b * QT:(b + 1) * QT, :], rc[:, b * QT:(b + 1) * QT, :],
                                                 pen[:, :].unsqueeze(2).to_broadcast([P, QT, NH]), ALU.add)
                    last.then_inc(fin, 1)
                    dve.wait_ge(fin, 2)
                    for i in range(B * QT):
                        dve.tensor_tensor(v_tok[:, i, :].rearrange("p (h e) -> p h e", e=HD),
                                          acc[:, i // QT, i % QT, :, 0:HD],
                                          rc[:, i, :].unsqueeze(2).to_broadcast([P, NH, HD]), ALU.mult)

        def stage_condition(xc, comb, E2):
            names = ("win", "wsp", "cin", "sil", "csb", "mod", "ops", "used", "sq", "req", "ack")
            w_in, wsp, cin, sil, csb, modp, ops, used, sq, req, ack = (sem(f"cd_{x}") for x in names)
            with ExitStack() as st:
                def sbl(name, shape, dt=F32):
                    return st.enter_context(nc.sbuf_tensor(name, shape, dt))
                raw = sbl("cd_raw", [P, KC, D])
                w = [sbl(f"cd_w{h}", [P, KC, D], F32R) for h in "hl"]
                wc, cT = sbl("cd_wc", [C, 2 * D]), sbl("cd_cT", [C, B])
                cb = sbl("cd_cb", [C, B, P])
                bc, rs = sbl("cd_bc", [P, 2 * D]), sbl("cd_rs", [P, D])
                mod = sbl("cd_mod", [P, B, 2 * D])
                ss, r = sbl("cd_ss", [P, NT]), sbl("cd_r", [P, NT])
                junk = sbl("cd_junk", [P, D])
                block = st.enter_context(nc.Block())

                @block.sync
                def _(sp):
                    sp.dma_start(raw[:, :, :], d["WoT"].rearrange("(k p) n -> p k n", p=P)).then_inc(w_in, 16)
                    sp.dma_start(wc[:, :], d["WcT"]).then_inc(cin, 16)
                    sp.dma_start(cT[:, :], d["condT"]).then_inc(cin, 16)
                    sp.dma_start(bc[:, :], d["bc"].partition_broadcast(P)).then_inc(cin, 16)
                    sp.dma_start(rs[:, :], d["rms_scale"].partition_broadcast(P)).then_inc(cin, 16)

                @block.tensor
                def _(pe):
                    pe.wait_ge(csb, 1)
                    for b in range(B):
                        pe.matmul(ps[4 + b][:, :], cb[:, b, :], wc[:, :], start=True, stop=True).then_inc(modp, 1)
                    pe.wait_ge(wsp, 1)
                    for i in range(NT):
                        if i >= 4:
                            pe.wait_ge(used, i - 3)
                        for n, (k, (a, b)) in enumerate((k, p) for k in range(KC) for p in PASSES):
                            last = pe.matmul(ps[i % 4][:, 0:D], actT[a][:, k, i * P:(i + 1) * P],
                                             w[b][:, k, :], start=n == 0, stop=n == 3 * KC - 1)
                        last.then_inc(ops, 1)

                @block.scalar
                def _(act):
                    act.wait_ge(cin, 64)
                    act.activation(cT[:, :], cT[:, :], ACT.Silu).then_inc(sil, 1)
                    for i in range(NT):
                        act.wait_ge(used, i + 1)
                        if i:
                            act.wait_ge(sq, i)
                        act.activation(junk[:, :], xc[:, i, :], ACT.Square, accum_out=ss[:, i:i + 1]).then_inc(sq, 1)
                    act.wait_ge(req, 1)
                    act.activation(r[:, :], r[:, :], ACT.Sqrt).then_inc(ack, 1)

                @block.vector
                def _(dve):
                    ch = dve_chain.on(dve)
                    dve.wait_ge(sil, 1)
                    dve.tensor_copy(cb[:, :, :], cT[:, :].unsqueeze(2).to_broadcast([C, B, P])).then_inc(csb, 1)
                    dve.wait_ge(w_in, 16)
                    weights_split(dve, ch, [(raw[:, :, :], w[0][:, :, :], w[1][:, :, :])], wsp)
                    for b in range(B):
                        dve.wait_ge(modp, b + 1)
                        ch.link(dve.tensor_tensor(mod[:, b, :], ps[4 + b][:, :], bc[:, :], ALU.add))
                        ch.link(dve.scalar_tensor_tensor(out=mod[:, b, D:2 * D], in0=mod[:, b, D:2 * D], scalar=1.0,
                                                         in1=rs[:, :], op0=ALU.add, op1=ALU.mult))
                    for i in range(NT):
                        dve.wait_ge(ops, i + 1)
                        dve.tensor_copy(xc[:, i, :], ps[i % 4][:, 0:D]).then_inc(used, 1)
                    dve.wait_ge(used, NT)
                    dve.wait_ge(sq, NT)
                    norm_rows(ch, req, ack, 1, ss[:, :], r[:, :], 1e-6, 1.0 / D)
                    for i in range(NT):
                        last = dve.tensor_scalar(xc[:, i, :], xc[:, i, :], r[:, i:i + 1], None, ALU.mult)
                    ch.link(last)
                    for b in range(B):
                        v = xc[:, b * NB:(b + 1) * NB, :]
                        ch.link(dve.tensor_tensor(v, v, mod[:, b, D:2 * D].unsqueeze(1).to_broadcast([P, NB, D]), ALU.mult))
                        ch.link(dve.tensor_tensor(v, v, mod[:, b, 0:D].unsqueeze(1).to_broadcast([P, NB, D]), ALU.add))

        def stage_gate2(xc, comb):
            names = ("gin", "sq", "gate_rows", "gps", "gsp", "lps", "ein", "eout", "isq", "iroot")
            gin, sq, r1, gps, gsp, lps, ein, eout, isq, iroot = (sem(f"g2_{x}") for x in names)
            with ExitStack() as st:
                def sbl(name, shape, dt=F32):
                    return st.enter_context(nc.sbuf_tensor(name, shape, dt))
                gw, gj = sbl("g2_gw", [E2, D]), sbl("g2_gj", [E2, D])
                gn = sbl("g2_gn", [E2, 1])
                gT = [sbl(f"g2_gT{h}", [P, KC, E2], F32R) for h in "hl"]
                ss, junk = sbl("g2_ss", [P, NT]), sbl("g2_junk", [P, D])
                z, sc, rep = sbl("g2_z", [P, NT, E2]), sbl("g2_sc", [P, NT, E2]), sbl("g2_rep", [P, NT, E2])
                top, sm = sbl("g2_top", [P, NT, 8]), sbl("g2_sm", [P, NT])
                block = st.enter_context(nc.Block())

                @block.sync
                def _(sp):
                    sp.dma_start(gw[:, :], d["gate_w"]).then_inc(gin, 16)

                @block.scalar
                def _(act):
                    act.wait_ge(gin, 16)
                    act.activation(gj[:, :], gw[:, :], ACT.Square, accum_out=gn[:, :]).then_inc(isq, 1)
                    for i in range(NT):
                        if i:
                            act.wait_ge(sq, i)
                        act.activation(junk[:, :], xc[:, i, :], ACT.Square, accum_out=ss[:, i:i + 1]).then_inc(sq, 1)
                    act.wait_ge(isq, 1)
                    act.activation(gn[:, :], gn[:, :], ACT.Sqrt).then_inc(iroot, 1)
                    act.wait_ge(sq, NT)
                    act.activation(ss[:, :], ss[:, :], ACT.Sqrt).then_inc(iroot, 1)
                    act.wait_ge(ein, 1)
                    act.activation(z[:, :, :], z[:, :, :], ACT.Exp, scale=-1.0).then_inc(eout, 1)

                @block.tensor
                def _(pe):
                    pe.wait_ge(r1, 1)
                    for k in range(KC):
                        last = pe.transpose(ps[0][:, k * E2:(k + 1) * E2], gw[:, k * P:(k + 1) * P], ident[0:E2, 0:E2])
                    last.then_inc(gps, 1)
                    pe.wait_ge(gsp, 1)
                    for i in range(NT):
                        for n, (k, (a, b)) in enumerate((k, p) for k in range(KC) for p in PASSES):
                            last = pe.matmul(ps[1][:, i * E2:(i + 1) * E2], actT[a][:, k, i * P:(i + 1) * P],
                                             gT[b][:, k, :], start=n == 0, stop=n == 3 * KC - 1)
                    last.then_inc(lps, 1)

                @block.vector
                def _(dve):
                    ch = dve_chain.on(dve)
                    bc3 = lambda v: v.unsqueeze(2).to_broadcast([P, NT, E2])
                    dve.wait_ge(iroot, 2)
                    ch.link(dve.tensor_scalar(gn[:, :], gn[:, :], 1e-12, None, ALU.max))
                    ch.link(dve.reciprocal(gn[:, :], gn[:, :]))
                    dve.tensor_scalar(gw[:, :], gw[:, :], gn[:, 0:1], None, ALU.mult).then_inc(r1, 1)
                    dve.wait_ge(gps, 1)
                    gsrc = ps[0][:, 0:KC * E2].rearrange("p (k e) -> p k e", k=KC)
                    ch.link(dve.tensor_copy(gT[0][:, :, :], gsrc))
                    dve.tensor_tensor(gT[1][:, :, :], gsrc, gT[0][:, :, :], ALU.subtract).then_inc(gsp, 1)
                    ch.link(dve.tensor_scalar(ss[:, :], ss[:, :], 1e-12, None, ALU.max))
                    ch.link(dve.reciprocal(ss[:, :], ss[:, :]))
                    dve.wait_ge(lps, 1)
                    dve.tensor_tensor(z[:, :, :], ps[1][:, 0:NT * E2].rearrange("p (i e) -> p i e", i=NT),
                                      bc3(ss[:, :]), ALU.mult).then_inc(ein, 1)
                    dve.wait_ge(eout, 1)
                    ch.link(dve.tensor_scalar(z[:, :, :], z[:, :, :], 1.0, None, ALU.add))
                    ch.link(dve.reciprocal(sc[:, :, :], z[:, :, :]))
                    for i in range(NT):
                        last = dve.max(top[:, i, :], sc[:, i, :])
                    ch.link(last)
                    for i in range(NT):
                        last = dve.match_replace(out=rep[:, i, :], in_to_replace=top[:, i, :],
                                                 in_values=sc[:, i, :], imm_value=-1.0)
                    ch.link(dve.tensor_reduce(sm[:, :], top[:, :, :], AX.X, ALU.add))
                    ch.link(dve.reciprocal(sm[:, :], sm[:, :]))
                    ch.link(dve.tensor_scalar(rep[:, :, :], rep[:, :, :], 0.0, None, ALU.is_lt))
                    ch.link(dve.tensor_tensor(sc[:, :, :], sc[:, :, :], rep[:, :, :], ALU.mult))
                    dve.memset(comb[:, :, E2:E2 + 1], 1.0)
                    ch.link(dve.tensor_tensor(comb[:, :, 0:E2], sc[:, :, :], bc3(sm[:, :]), ALU.mult))

        def stage_experts2(comb):
            names = ("wsp", "dve", "hps", "sil", "h32", "hhi", "hsp", "ops", "used", "out")
            win = [sem(f"e2_win{n}") for n in range(2)]
            wsp, dch, hps, sil, h32d, hhi, hsp, ops, used, stored = (sem(f"e2_{x}") for x in names)
            LAG = 2
            NE = E2 + 1
            NW = 2 * KC * H2 + D
            OU, OD = KC * H2, 2 * KC * H2
            SP_ = 2 * G
            HS = 4
            with ExitStack() as st:
                def sbl(name, shape, dt=F32):
                    return st.enter_context(nc.sbuf_tensor(name, shape, dt))
                raw = sbl("e2_raw", [P, 2, NW])
                w = [[sbl(f"e2_w{p}{h}", [P, NW], F32R) for h in "hl"] for p in range(2)]
                sl_sb, h32 = sbl("e2_silusb", [P, 2, GT]), sbl("e2_h32sb", [P, 2, GT])
                hh = [sbl(f"e2_h{h}", [P, HS, GT], F32R) for h in "hl"]
                block = st.enter_context(nc.Block())

                @block.sync
                def _(sp):
                    def load(e, slot):
                        for name, o, c, n in (("w_gate", 0, KC, H2), ("w_up", OU, KC, H2), ("w_down", OD, 1, D)):
                            src = d[name].rearrange("e (c p) n -> p e c n", p=P)[:, bass.ds(e, 1), :, :]
                            sp.dma_start(raw[:, slot, o:o + c * n].rearrange("p (a c n) -> p a c n", a=1, c=c),
                                         src).then_inc(win[slot], 16)
                    load(0, 0)
                    load(1, 1)
                    with sp.Fori(1, E2 // 2) as t:
                        for slot in range(2):
                            sp.wait_ge(wsp, 2 * t - 1 + slot)
                            load(2 * t + slot, slot)
                    sp.wait_ge(wsp, E2 - 1)
                    for name, o, c, n in (("sw_gate", 0, KC, H2), ("sw_up", OU, KC, H2), ("sw_down", OD, 1, D)):
                        sp.dma_start(raw[:, 0, o:o + c * n].rearrange("p (c n) -> p c n", c=c),
                                     d[name].rearrange("(c p) n -> p c n", p=P)).then_inc(win[0], 16)
                    o_tok = out.rearrange("(i p) d -> p i d", p=P)
                    for g in range(G):
                        sp.wait_ge(used, (E2 * G + g + 1) * TG + 4)
                        sp.dma_start(o_tok[:, g * TG:(g + 1) * TG, :], y[:, g * TG:(g + 1) * TG, :]).then_inc(stored, 16)
                    sp.wait_ge(stored, 16 * G)

                @block.tensor
                def _(pe):
                    def up(s, step, e):
                        par, g = (s // G) % 2, s % G
                        if g == 0:
                            pe.wait_ge(wsp, e + 1)
                        for v, (o, bank) in enumerate(((0, ps[s % 2]), (OU, ps[2 + s % 2]))):
                            pe.wait_ge((sil, h32d)[v], step + 1)
                            for n, (k, (a, b)) in enumerate((k, p) for k in range(KC) for p in PASSES):
                                last = pe.matmul(bank[:, :], w[par][a][:, o + k * H2:o + (k + 1) * H2],
                                                 actT[b][:, k, g * GT:(g + 1) * GT], start=n == 0,
                                                 stop=n == 3 * KC - 1)
                            last.then_inc(hps, 1)

                    def down(s, step):
                        par = (s // G) % 2
                        pe.wait_ge(hsp, step + 1)
                        for j in range(TG):
                            pe.wait_ge(used, step * TG + j + 1)
                            for n, (a, b) in enumerate(PASSES):
                                last = pe.matmul(ps[4 + j][:, 0:D], hh[a][:, s % HS, j * P:(j + 1) * P],
                                                 w[par][b][:, OD:OD + D], start=n == 0, stop=n == 2)
                            last.then_inc(ops, 1)

                    for s in range(LAG):
                        up(s, s, 0)
                    with pe.Fori(0, E2 // 2) as t:
                        for s in range(SP_):
                            up(s + LAG, t * SP_ + s + LAG, 2 * t + (s + LAG) // G)
                            down(s, t * SP_ + s)
                    for s in range(G):
                        if s + LAG < G:
                            up(s + LAG, E2 * G + s + LAG, E2)
                        down(s, E2 * G + s)

                def hidden_steps(eng, body):
                    for s in range(LAG):
                        body(s, s, None, 0, False)
                    with eng.Fori(0, E2 // 2 - 1) as t:
                        for s in range(SP_):
                            body(s + LAG, t * SP_ + s + LAG, s, t, False)
                    for s in range(SP_):
                        body(s + LAG, (E2 // 2 - 1) * SP_ + s + LAG, s, E2 // 2 - 1, True)
                    for s in range(G):
                        body(s + LAG if s + LAG < G else None, E2 * G + s + LAG, s, E2 // 2, True)

                @block.scalar
                def _(act):
                    act.nop().then_inc(sil, 2)

                    def body(s, step, *_):
                        if s is None:
                            return
                        act.wait_ge(hps, 2 * step + 1)
                        act.wait_ge(h32d, step + 1)
                        act.activation(sl_sb[:, s % 2, :], ps[s % 2][:, :], ACT.Silu).then_inc(sil, 1)
                    hidden_steps(act, body)

                @block.gpsimd
                def _(pool):
                    def body(s, step, *_):
                        if s is None:
                            return
                        pool.wait_ge(hhi, step + 1)
                        pool.tensor_tensor(hh[1][:, s % HS, :], h32[:, s % 2, :], hh[0][:, s % HS, :],
                                           ALU.subtract).then_inc(hsp, 1)
                    hidden_steps(pool, body)

                @block.vector
                def _(dve):
                    dve.nop().then_inc(h32d, 2)
                    dve.nop().then_inc(used, 4)

                    def split(par, loads, ch):
                        dve.wait_ge(win[par], 48 * loads)
                        ch.link(dve.tensor_copy(w[par][0][:, :], raw[:, par, :]))
                        dve.tensor_tensor(w[par][1][:, :], raw[:, par, :], w[par][0][:, :], ALU.subtract).then_inc(wsp, 1)

                    chains = [Chain(dve, dch), Chain(dve, sem("e2_dve2"))]
                    for par in range(2):
                        split(par, 1, chains[par])

                    def body(s, step, out_s, t, last_turn):
                        if s is not None:
                            dve.wait_ge(sil, step + 3)
                            dve.wait_ge(hps, 2 * step + 2)
                            if out_s is not None:
                                dve.wait_ge(hsp, step - 1)
                            dve.tensor_tensor(h32[:, s % 2, :], ps[2 + s % 2][:, :], sl_sb[:, s % 2, :],
                                              ALU.mult).then_inc(h32d, 1)
                            dve.wait_ge(h32d, step + 3)
                            dve.tensor_copy(hh[0][:, s % HS, :], h32[:, s % 2, :]).then_inc(hhi, 1)
                        if out_s is not None:
                            g = out_s % G
                            first = (step - LAG) * TG
                            for j in range(TG):
                                i = g * TG + j
                                dve.wait_ge(ops, first + j + 1)
                                dve.wait_ge(used, first + 1)
                                dve.scalar_tensor_tensor(out=y[:, i, :], in0=ps[4 + j][:, 0:D],
                                                         scalar=comb[:, i, bass.ds(2 * t + out_s // G, 1)],
                                                         in1=y[:, i, :], op0=ALU.mult, op1=ALU.add).then_inc(used, 1)
                            if g == G - 1 and s is not None:
                                par = out_s // G
                                if not (last_turn and par):
                                    chains[par].base, chains[par].k = t + 1, 0
                                    split(par, t + 2, chains[par])
                    hidden_steps(dve, body)

        stage_gate1()
        stage_experts1()
        stage_combine()
        qp = [sb(f"qp{h}", [P, KC, T], F32R) for h in "hl"]
        transpose_stage(y)
        kvh = stage_linear_attention()
        stage_linear_out(kvh)
        transpose_stage(y)
        stage_feed_forward()
        stage_residual()
        transpose_stage(y)
        v_tok = sb("v_tok", [P, NT, D])
        with ExitStack() as st:
            def sbm(name, shape, dt=F32):
                return st.enter_context(nc.sbuf_tensor(name, shape, dt))
            kT = [sbm(f"kT{h}", [P, KC, T], F32R) for h in "hl"]
            mbias = sbm("mbias", [P, QT, S], BF16)
            n_live, live_at = sbm("n_live", [P, 1], I32), sbm("live_at", [P, 8], I32)
            pen, identb = sbm("pen", [P, QT]), sbm("identb", [P, P], BF16)
            stage_project(kT, v_tok, n_live, live_at, mbias, pen, None, identb)
            stage_attention(kT, v_tok, n_live, live_at, mbias, pen, identb)
        transpose_stage(v_tok)
        comb = sb("comb", [P, NT, E2 + 1])
        stage_condition(v_tok, comb, E2)
        transpose_stage(v_tok)
        stage_gate2(v_tok, comb)
        stage_experts2(comb)


def kernel(**inputs):
    import numpy as np
    import concourse.bacc as bacc
    from concourse import mybir as mb
    from concourse.bass_utils import run_bass_kernel_spmd as run

    a = {k: np.asarray(v) for k, v in inputs.items()}
    x = a["x"]
    arrays = {
        "x": x.reshape(-1, x.shape[-1]), "xT": x.reshape(-1, x.shape[-1]).T,
        "cond": a["cond_256"], "condT": a["cond_256"].T, "mask": a["mask_SxS_bk1"].view(np.int32),
        "rms_w": a["L0_cond_rms_w"], "wg_W": a["L0_cond_wg_W"], "wg_b": a["L0_cond_wg_b"],
        "gg_W": a["L0_cond_gg_W"], "gg_b": a["L0_cond_gg_b"],
        "Wqkv": a["L0_attn_Wqkv"], "bqkv": a["L0_attn_bqkv"], "Wg": a["L0_attn_Wg"], "bg": a["L0_attn_bg"],
        "Wu": a["L0_attn_Wu"], "bu": a["L0_attn_bu"], "Wd": a["L0_attn_Wd"], "bd": a["L0_attn_bd"],
        "g1": a["L0_attn_g1"], "be1": a["L0_attn_b1"], "g2": a["L0_attn_g2"], "be2": a["L0_attn_b2"],
        "WqT": a["L0_cond2_Wq"].T, "WkT": a["L0_cond2_Wk"].T, "WvT": a["L0_cond2_Wv"].T,
        "WoT": a["L0_cond2_Wo"].T, "rms_scale": a["L0_cond2_rms_scale"], "WcT": a["L0_cond2_Wc"].T,
        "bc": a["L0_cond2_bc"], "gate_w": a["L0_ffn_gate_w"], "w_gate": a["L0_ffn_w_gate"],
        "w_up": a["L0_ffn_w_up"], "w_down": a["L0_ffn_w_down"], "sw_gate": a["L0_ffn_sw_gate"],
        "sw_up": a["L0_ffn_sw_up"], "sw_down": a["L0_ffn_sw_down"],
    }
    for n in ("1", "2", "3"):
        arrays["W" + n], arrays["b" + n] = a["L0_cond_W" + n], a["L0_cond_b" + n]
        if n != "3":
            b = arrays["b" + n]
            arrays[f"b{n}_cols"] = b.reshape(b.shape[0], -1, P).transpose(2, 0, 1)

    def cols(v):
        return v[:v.size // P * P].reshape(-1, P).T

    arrays["rms_w_cols"], arrays["bq_cols"] = cols(arrays["rms_w"]), cols(arrays["bqkv"][:x.shape[-1]])
    arrays["bg_cols"], arrays["bu_cols"] = cols(arrays["bg"]), cols(arrays["bu"])
    nc = bacc.Bacc("TRN2", target_bir_lowering=False, num_devices=1)
    arrays = {f"in_{k}": np.ascontiguousarray(v) for k, v in arrays.items()}
    d = {k[3:]: nc.dram_tensor(k, v.shape, mb.dt.from_np(v.dtype), kind="ExternalInput").ap()
         for k, v in arrays.items()}
    out = nc.dram_tensor("out", d["x"].shape, mb.dt.float32, kind="ExternalOutput").ap()
    adaln_block(nc, d, out)
    r = run(nc, [arrays], core_ids=[0])
    return r.results[0]["out"].reshape(x.shape)
```

```python
from contextlib import ExitStack

import concourse.bass as bass
from concourse import mybir

ALU = mybir.AluOpType
ACT = mybir.ActivationFunctionType
F32 = mybir.dt.float32
F32R = mybir.dt.float32r
BF16 = mybir.dt.bfloat16
I32 = mybir.dt.int32
U32 = mybir.dt.uint32
U8 = mybir.dt.uint8
AX = mybir.AxisListType

P = 128
GT = 512
ET = 256
PASSES = ((0, 0), (0, 1), (1, 0))
MASKED = -1e30


class Chain:

    def __init__(self, eng, sem):
        self.eng, self.sem, self.base, self.k = eng, sem, 0, 0

    def on(self, eng):
        self.eng = eng
        return self

    def link(self, ins):
        self.k += 1
        ins.then_inc(self.sem, 1)
        self.eng.wait_ge(self.sem, self.base + self.k)


def adaln_block(nc, d, out):
    T, D = d["x"].shape
    B = d["cond"].shape[0]
    S = T // B
    C = d["cond"].shape[1]
    NT, KC, G = T // P, D // P, T // GT
    TG = GT // P
    NB = NT // B
    E1, _, M1 = d["W1"].shape
    MC = M1 // P
    F = d["Wg"].shape[1]
    FC = -(-F // P)
    FR = F - (FC - 1) * P
    E2, _, H2 = d["w_gate"].shape
    HD = 16
    NH = D // HD
    HC = NH // KC
    LW = D + 2
    QT = S // P

    with ExitStack() as ctx:
        def sem(name):
            return ctx.enter_context(nc.semaphore(name))

        def sb(name, shape, dt=F32):
            return ctx.enter_context(nc.sbuf_tensor(name, shape, dt))

        psum = ctx.enter_context(nc.psum_tensor("psum", [P, 8, GT], F32))
        ps = [psum[:, i, :] for i in range(8)]
        ident = sb("ident", [P, P])
        act_hi = sb("act_hi", [P, KC, T], F32R)
        act_lo = sb("act_lo", [P, KC, T], F32R)
        actT = (act_hi, act_lo)
        y = sb("y", [P, NT, D])
        TILES = 2 * T // ET + 2 * (E1 - 2) + 2
        LONG = (TILES + T // ET) * ET
        x_rows = nc.dram_tensor("x_rows", [LONG, D], F32, kind="Internal").ap()
        y_rows = nc.dram_tensor("y_rows", [LONG, D], F32, kind="Internal").ap()
        top2 = sb("top2", [P, NT, 8])
        place = sb("place", [P, NT, 2], U32)
        tiles = sb("tiles", [P, 3, E1], I32)

        dve_chain = Chain(None, sem("dve_chain"))
        turned, hi_done, lo_done = sem("tr_turned"), sem("tr_hi"), sem("tr_lo")
        turns_done = [0]

        gate_sems = []

        x_tok = d["x"].rearrange("(i p) d -> p i d", p=P)

        def norm_rows(chain, act_req, act_ack, n_done, var_ap, tmp, eps, scale=1.0):
            chain.link(chain.eng.tensor_scalar(tmp, var_ap, scale, eps, ALU.mult, ALU.add))
            chain.eng.tensor_copy(tmp, tmp).then_inc(act_req, 1)
            chain.eng.wait_ge(act_ack, n_done)
            chain.link(chain.eng.reciprocal(tmp, tmp))

        def stage_gate1(load_weights):
            def sem(name):
                gate_sems.append(nc.alloc_semaphore(name=name))
                return gate_sems[-1]
            loaded, tok_in, w_in = [sem(f"g1_xT{g}") for g in range(G)], sem("g1_x"), sem("g1_w")
            unused = sem("g1_unused")
            idn, flat, flat_out = sem("g1_ident"), sem("g1_flat"), sem("g1_flatout")
            wready, asplit = sem("g1_wready"), sem("g1_split")
            sq, logit, cbias = sem("g1_sq"), sem("g1_logit"), sem("g1_cbias")
            filled, selected, ranked, placed, scattered = (sem(f"g1_{x}") for x in (
                "filled", "selected", "ranked", "placed", "scattered"))
            root_in, root, ein, eout = sem("g1_rootin"), sem("g1_root"), sem("g1_ein"), sem("g1_eout")
            with ExitStack() as st:
                def sbl(name, shape, dt=F32):
                    return st.enter_context(nc.sbuf_tensor(name, shape, dt))
                xT = sbl("g1_xTraw", [P, KC, T])
                xk = sbl("g1_xtok", [P, NT, D])
                junk = sbl("g1_junk", [P, D])
                lgT = sbl("g1_lgT", [E1, T])
                wg = sbl("g1_wg", [P, KC, E1])
                rw = sbl("g1_rw", [P, KC])
                wgh, wgl = sbl("g1_wgh", [P, KC, E1], F32R), sbl("g1_wgl", [P, KC, E1], F32R)
                bia, bib = sbl("g1_ba", [P, E1]), sbl("g1_bb", [P, E1])
                gg = sbl("g1_gg", [C, E1])
                cT, cTb = sbl("g1_cT", [C, B]), sbl("g1_cTb", [C, B, P])
                ss, r = sbl("g1_ss", [P, NT]), sbl("g1_r", [P, NT])
                bb = sbl("g1_bias", [P, B, E1])
                z, w8 = sbl("g1_z", [P, NT, E1]), sbl("g1_w8", [P, NT, E1])
                mx, sm = sbl("g1_mx", [P, NT]), sbl("g1_sm", [P, NT])
                top = top2
                idx, idf = sbl("g1_idx", [P, NT, 8], U32), sbl("g1_idf", [P, NT, 8])
                io = sbl("g1_iota", [P, E1])
                oh = [sbl(f"g1_oh{n}", [P, NT, E1]) for n in range(2)]
                sel, pos = sbl("g1_sel", [P, NT, E1], BF16), sbl("g1_pos", [P, NT, E1])
                selsum, cnt = sbl("g1_selsum", [P, E1], BF16), sbl("g1_cnt", [P, E1])
                thr, tri8 = sbl("g1_thr", [P, T // ET]), sbl("g1_tri8", [P, E1, E1])
                cmp_, nt, bt = sbl("g1_cmp", [P, E1, T // ET]), sbl("g1_nt", [P, E1]), sbl("g1_bt", [P, E1])
                pf = sbl("g1_pf", [P, NT, 2])
                ones, tri = sbl("g1_ones", [P, P], BF16), sbl("g1_tri", [P, P], BF16)
                zero = sbl("g1_zero", [P, D])
                block = st.enter_context(nc.Block())

                @block.sync
                def _(sp):
                    sp.dma_start(wg[:, :, :], d["wg_W"].rearrange("(k p) e -> p k e", p=P)).then_inc(w_in, 16)
                    sp.dma_start(rw[:, :], d["rms_w_cols"]).then_inc(w_in, 16)
                    sp.dma_start(bia[:, :], d["wg_b"].partition_broadcast(P)).then_inc(w_in, 16)
                    sp.dma_start(bib[:, :], d["gg_b"].partition_broadcast(P)).then_inc(w_in, 16)
                    sp.dma_start(gg[:, :], d["gg_W"]).then_inc(w_in, 16)
                    sp.dma_start(cT[:, :], d["condT"]).then_inc(w_in, 16)
                    for g in range(G):
                        sp.dma_start(xT[:, :, g * GT:(g + 1) * GT],
                                     d["xT"].rearrange("(k p) t -> p k t", p=P)[:, :, g * GT:(g + 1) * GT]).then_inc(loaded[g], 16)
                    sp.wait_ge(idn, 8)
                    rows = x_rows[0:TILES * ET, :].rearrange("(p n) d -> p n d", p=P)
                    part = TILES * ET // P // 4
                    for n in range(4):
                        sp.dma_start(rows[:, n * part:(n + 1) * part, :],
                                     zero[:, :].unsqueeze(1).to_broadcast([P, part, D])).then_inc(filled, 16)
                    load_weights(sp, 0)
                    sp.wait_ge(placed, 1)
                    count = sp.value_load(tiles[0:1, 0, E1 - 1:E1], min_val=2, max_val=T // ET)
                    first = sp.value_load(tiles[0:1, 1, E1 - 1:E1], min_val=0, max_val=TILES - 3)
                    with sp.Fori(first + count + 1, LONG // ET) as n:
                        for j in range(ET // P):
                            sp.dma_start(y_rows.rearrange("(n j p) d -> p n j d", p=P, j=ET // P)[:, bass.ds(n, 1), j, :],
                                         zero[:, :].unsqueeze(1)).then_inc(unused, 16)

                @block.gpsimd
                def _(pool):
                    pool.memset(ident[:, :], 0.0).then_inc(idn, 1)
                    pool.wait_ge(idn, 1)
                    pool.affine_select(out=ident[:, :], in_=ident[:, :], compare_op=ALU.not_equal, fill=1.0,
                                       base=0, pattern=[[-1, P]], channel_multiplier=1).then_inc(idn, 1)
                    pool.iota(io[:, :], pattern=[[1, E1]], base=0, channel_multiplier=0,
                              allow_small_or_imprecise_dtypes=True).then_inc(idn, 1)
                    pool.iota(thr[:, :], pattern=[[ET, T // ET]], base=0, channel_multiplier=0,
                              allow_small_or_imprecise_dtypes=True).then_inc(idn, 1)
                    pool.memset(ones[:, :], 1.0).then_inc(idn, 1)
                    pool.memset(tri[:, :], 1.0).then_inc(idn, 1)
                    pool.memset(tri8[:, :, :], 1.0).then_inc(idn, 1)
                    pool.memset(zero[:, :], 0.0).then_inc(idn, 1)
                    pool.wait_ge(idn, 8)
                    pool.affine_select(out=tri[:, :], in_=tri[:, :], compare_op=ALU.is_gt, fill=0.0,
                                       base=0, pattern=[[1, P]], channel_multiplier=-1).then_inc(idn, 1)
                    pool.affine_select(out=tri8[:, :, :], in_=tri8[:, :, :], compare_op=ALU.is_gt, fill=0.0,
                                       base=0, pattern=[[1, E1], [-1, E1]], channel_multiplier=0).then_inc(idn, 1)
                    pool.wait_ge(filled, 16 * 4)
                    pool.wait_ge(placed, 1)
                    pool.wait_ge(tok_in, 16)
                    for i in range(NT):
                        for n in range(2):
                            pool.indirect_dma_start(
                                out=x_rows, out_offset=bass.IndirectOffsetOnAxis(ap=place[:, i, n:n + 1], axis=0),
                                in_=xk[:, i, :], in_offset=None).then_inc(scattered, 16)
                    pool.wait_ge(scattered, 16 * 2 * NT)
                    left = pool.value_load(tiles[0:1, 2, 0:1], min_val=1, max_val=LONG // ET)
                    pool.wait_ge(unused, left * (16 * ET // P))

                @block.scalar
                def _(act):
                    act.dma_start(xk[:, :, :], x_tok).then_inc(tok_in, 16)
                    act.wait_ge(tok_in, 16)
                    for i in range(NT):
                        if i:
                            act.wait_ge(sq, i)
                        act.activation(junk[:, :], xk[:, i, :], ACT.Square,
                                       accum_out=ss[:, i:i + 1]).then_inc(sq, 1)
                    for g in range(G):
                        act.wait_ge(flat, g + 1)
                        act.activation(lgT[:, g * GT:(g + 1) * GT], ps[3 + g][0:E1, :], ACT.Copy).then_inc(flat_out, 1)
                    act.wait_ge(root_in, 1)
                    act.activation(r[:, :], r[:, :], ACT.Sqrt).then_inc(root, 1)
                    act.wait_ge(ein, 1)
                    act.activation(w8[:, :, :], z[:, :, :], ACT.Exp).then_inc(eout, 1)

                @block.vector
                def _(dve):
                    ch = dve_chain.on(dve)
                    dve.wait_ge(w_in, 96)
                    for k in range(KC):
                        ch.link(dve.tensor_scalar(wg[:, k, :], wg[:, k, :], rw[:, k:k + 1], None, ALU.mult))
                    ch.link(dve.tensor_copy(wgh[:, :, :], wg[:, :, :]))
                    dve.tensor_tensor(wgl[:, :, :], wg[:, :, :], wgh[:, :, :], ALU.subtract).then_inc(wready, 1)
                    dve.tensor_copy(cTb[:, :, :], cT[:, :].unsqueeze(2).to_broadcast([C, B, P])).then_inc(wready, 1)
                    ch.link(dve.tensor_tensor(bia[:, :], bia[:, :], bib[:, :], ALU.add))
                    for g in range(G):
                        sl = slice(g * GT, (g + 1) * GT)
                        dve.wait_ge(loaded[g], 16)
                        ch.link(dve.tensor_copy(act_hi[:, :, sl], xT[:, :, sl]))
                        dve.tensor_tensor(act_lo[:, :, sl], xT[:, :, sl], act_hi[:, :, sl],
                                          ALU.subtract).then_inc(asplit, 1)
                    dve.wait_ge(sq, NT)
                    norm_rows(ch, root_in, root, 1, ss[:, :], r[:, :], 1e-6, 1.0 / D)
                    dve.wait_ge(cbias, 1)
                    ch.link(dve.tensor_tensor(bb[:, :, :], ps[1][:, 0:B * E1].rearrange("p (b e) -> p b e", b=B),
                                              bia[:, :].unsqueeze(1).to_broadcast([P, B, E1]), ALU.add))
                    dve.wait_ge(logit, 1)
                    ch.link(dve.tensor_tensor(z[:, :, :], ps[0][:, 0:NT * E1].rearrange("p (i e) -> p i e", i=NT),
                                              r[:, :].unsqueeze(2).to_broadcast([P, NT, E1]), ALU.mult))
                    for b in range(B):
                        ch.link(dve.tensor_tensor(z[:, b * NB:(b + 1) * NB, :], z[:, b * NB:(b + 1) * NB, :],
                                                  bb[:, b, :].unsqueeze(1).to_broadcast([P, NB, E1]), ALU.add))
                    ch.link(dve.tensor_reduce(mx[:, :], z[:, :, :], AX.X, ALU.max))
                    dve.tensor_tensor(z[:, :, :], z[:, :, :], mx[:, :].unsqueeze(2).to_broadcast([P, NT, E1]),
                                      ALU.subtract).then_inc(ein, 1)
                    dve.wait_ge(eout, 1)
                    ch.link(dve.tensor_reduce(sm[:, :], w8[:, :, :], AX.X, ALU.add))
                    ch.link(dve.reciprocal(sm[:, :], sm[:, :]))
                    ch.link(dve.tensor_tensor(w8[:, :, :], w8[:, :, :],
                                              sm[:, :].unsqueeze(2).to_broadcast([P, NT, E1]), ALU.mult))
                    for i in range(NT):
                        last = dve.max(top[:, i, :], w8[:, i, :])
                    ch.link(last)
                    for i in range(NT):
                        last = dve.max_index(idx[:, i, :], top[:, i, :], w8[:, i, :])
                    ch.link(last)
                    ch.link(dve.tensor_copy(idf[:, :, :], idx[:, :, :]))
                    dve.wait_ge(idn, 10)
                    for n in range(2):
                        ch.link(dve.tensor_tensor(oh[n][:, :, :], io[:, :].unsqueeze(1).to_broadcast([P, NT, E1]),
                                                  idf[:, :, n:n + 1].to_broadcast([P, NT, E1]), ALU.is_equal))
                    ch.link(dve.tensor_tensor(sel[:, :, :], oh[0][:, :, :], oh[1][:, :, :], ALU.add))
                    ch.link(dve.tensor_reduce(cnt[:, :], sel[:, :, :].rearrange("p i e -> p e i"), AX.X, ALU.add))
                    dve.tensor_copy(selsum[:, :], cnt[:, :]).then_inc(selected, 1)
                    dve.wait_ge(ranked, 1)
                    ch.link(dve.tensor_copy(cnt[:, :], ps[2][:, NT * E1:(NT + 1) * E1]))
                    ch.link(dve.tensor_tensor(cmp_[:, :, :], cnt[:, :].unsqueeze(2).to_broadcast([P, E1, T // ET]),
                                              thr[:, :].unsqueeze(1).to_broadcast([P, E1, T // ET]), ALU.is_gt))
                    ch.link(dve.tensor_reduce(nt[:, :], cmp_[:, :, :], AX.X, ALU.add))
                    ch.link(dve.tensor_scalar(nt[:, :], nt[:, :], 2.0, None, ALU.max))
                    ch.link(dve.tensor_tensor(tri8[:, :, :], tri8[:, :, :],
                                              nt[:, :].unsqueeze(1).to_broadcast([P, E1, E1]), ALU.mult))
                    ch.link(dve.tensor_reduce(bt[:, :], tri8[:, :, :], AX.X, ALU.add))
                    ch.link(dve.tensor_copy(tiles[:, 0, :], nt[:, :]))
                    ch.link(dve.tensor_copy(tiles[:, 1, :], bt[:, :]))
                    ch.link(dve.tensor_reduce(sm[:, 0:1], nt[:, :], AX.X, ALU.add))
                    ch.link(dve.tensor_scalar(tiles[:, 2, 0:1], sm[:, 0:1], -1.0, float(LONG // ET - 1),
                                              ALU.mult, ALU.add))
                    ch.link(dve.tensor_scalar(bt[:, :], bt[:, :], float(ET), float(ET), ALU.mult, ALU.add))
                    ch.link(dve.tensor_tensor(pos[:, :, :], ps[2][:, 0:NT * E1].rearrange("p (i e) -> p i e", i=NT),
                                              bt[:, :].unsqueeze(1).to_broadcast([P, NT, E1]), ALU.add))
                    for n in range(2):
                        ch.link(dve.tensor_tensor(oh[n][:, :, :], oh[n][:, :, :], pos[:, :, :], ALU.mult))
                        ch.link(dve.tensor_reduce(pf[:, :, n], oh[n][:, :, :], AX.X, ALU.add))
                    dve.tensor_copy(place[:, :, :], pf[:, :, :]).then_inc(placed, 1)

                @block.tensor
                def _(pe):
                    pe.wait_ge(wready, 2)
                    for b in range(B):
                        last = pe.matmul(ps[1][:, b * E1:(b + 1) * E1], cTb[:, b, :], gg[:, :], start=True, stop=True)
                    last.then_inc(cbias, 1)
                    w2 = (wgh, wgl)
                    for g in range(G):
                        pe.wait_ge(asplit, g + 1)
                        for n, (k, (a, b)) in enumerate((k, p) for k in range(KC) for p in PASSES):
                            last = pe.matmul(ps[3 + g][0:E1, :], w2[a][:, k, :], actT[b][:, k, g * GT:(g + 1) * GT],
                                             start=n == 0, stop=n == 3 * KC - 1)
                        last.then_inc(flat, 1)
                    pe.wait_ge(idn, 8)
                    for i in range(NT):
                        if i % TG == 0:
                            pe.wait_ge(flat_out, i // TG + 1)
                        last = pe.transpose(ps[0][:, i * E1:(i + 1) * E1], lgT[:, i * P:(i + 1) * P],
                                            ident[0:E1, 0:E1])
                    last.then_inc(logit, 1)
                    pe.wait_ge(selected, 1)
                    pe.matmul(ps[2][:, 0:NT * E1], tri[:, :], sel[:, :, :].rearrange("p i e -> p (i e)"),
                              start=True, stop=False)
                    for k in range(1, NT):
                        pe.matmul(ps[2][:, k * E1:NT * E1], ones[:, :],
                                  sel[:, 0:NT - k, :].rearrange("p i e -> p (i e)"), start=False, stop=k == NT - 1)
                    pe.matmul(ps[2][:, NT * E1:(NT + 1) * E1], ones[:, :], selsum[:, :],
                              start=False, stop=True, skip_group_check=True).then_inc(ranked, 1)

        O2, O3 = KC * M1, KC * M1 + MC * M1
        NW = O3 + MC * D
        PARTS = ((0, O2, KC), (O2, O3, MC), (O3, NW, MC))

        def expert1_loader(raw, rawb, rawb3, win):
            def load_weights(sp, e):
                for n, (name, (o, o_end, c)) in enumerate(zip(("W1", "W2", "W3"), PARTS)):
                    src = d[name].rearrange("e (c p) n -> p e c n", p=P)[:, bass.ds(e, 1), :, :]
                    sp.dma_start(raw[:, o:o_end].rearrange("p (a c n) -> p a c n", a=1, c=c), src).then_inc(win[n], 16)
                    if n == 0:
                        for m in range(2):
                            sp.dma_start(rawb[:, m:m + 1, :], d[f"b{m + 1}_cols"][:, bass.ds(e, 1), :]).then_inc(win[n], 16)
                    if n == 2:
                        sp.dma_start(rawb3[:, :], d["b3"].rearrange("e d -> (e d)")[bass.ds(e * D, D)]
                                     .partition_broadcast(P)).then_inc(win[n], 16)
            return load_weights

        def stage_experts1(raw, rawb, rawb3, win, load_weights):
            wsp, wch = sem("e1_wsplit"), sem("e1_dve")
            xin, xturned, xhi, xsp = sem("e1_xin"), sem("e1_xturned"), sem("e1_xhi"), sem("e1_xsplit")
            h_ps, evac, h_hi, h_s = sem("e1_hps"), sem("e1_evac"), sem("e1_hhi"), sem("e1_hsplit")
            o_ps, o_add, stored, zeroed = sem("e1_ops"), sem("e1_oadd"), sem("e1_stored"), sem("e1_zeroed")
            CH = 2 * MC
            CP = CH // 2
            TT = ET // P
            assert TT * D == GT and 2 * ET == GT and KC * ET == GT
            with ExitStack() as st:
                def sbl(name, shape, dt=F32):
                    return st.enter_context(nc.sbuf_tensor(name, shape, dt))
                w = [[sbl(f"e1_w{p}{h}", [P, NW], F32R) for h in "hl"] for p in range(2)]
                h1 = [sbl(f"e1_h1{h}", [P, MC, ET], F32R) for h in "hl"]
                h2 = [sbl(f"e1_h2{h}", [P, MC, ET], F32R) for h in "hl"]
                u = sbl("e1_u", [P, CP, 2, ET])
                xg, xs = sbl("e1_xg", [P, TT, D]), [sbl(f"e1_xs{h}", [P, KC, ET], F32R) for h in "hl"]
                yo = sbl("e1_yo", [P, TT, D])
                bias, bias3 = sbl("e1_bias", [P, 2, 2, MC]), sbl("e1_bias3", [P, 2, D])
                nc.clear_and_free_semaphores(gate_sems)
                block = st.enter_context(nc.Block())

                def experts(eng, between, step):
                    def turn(t, last):
                        for par in range(2):
                            e = bass.ds(2 * t + par, 1)
                            count = eng.value_load(tiles[0:1, 0, e], min_val=2, max_val=T // ET)
                            first = eng.value_load(tiles[0:1, 1, e], min_val=0, max_val=TILES - 3)
                            step(first, par, 1 - par, (t, par, last))
                            between(t, par, last)
                            with eng.Fori(1, count) as i:
                                step(first + i, par, par, None)
                    with eng.Fori(0, E1 // 2 - 1) as t:
                        turn(t, False)
                    turn(E1 // 2 - 1, True)
                    count = eng.value_load(tiles[0:1, 0, E1 - 1:E1], min_val=2, max_val=T // ET)
                    first = eng.value_load(tiles[0:1, 1, E1 - 1:E1], min_val=0, max_val=TILES - 3)
                    return first + count

                def load_rows(eng, n):
                    eng.dma_start(tile4(xg), rows(x_rows, n)).then_inc(xin, 16)

                rows = lambda v, n: v.rearrange("(n j p) d -> p n j d", p=P, j=TT)[:, bass.ds(n, 1), :, :]
                tile4 = lambda v: v[:, :, :].unsqueeze(1)

                @block.sync
                def _(sp):
                    def store_rows(n):
                        sp.wait_ge(o_add, n + 2)
                        sp.dma_start(rows(y_rows, n), tile4(yo)).then_inc(stored, 16)

                    def step(n, par, par3, _):
                        store_rows(n)

                    def between(t, par, last):
                        if last:
                            return
                        e = 2 * t + par
                        sp.wait_ge(wsp, 3 * (e + 2))
                        load_weights(sp, e + 2)

                    sp.wait_ge(wsp, 3)
                    load_weights(sp, 1)
                    n = experts(sp, between, step)
                    store_rows(n)

                @block.tensor
                def _(pe):
                    def turn_rows(n):
                        pe.wait_ge(xin, (n + 1) * 16)
                        for k in range(KC):
                            for j in range(TT):
                                last = pe.transpose(ps[5][:, k * ET + j * P:k * ET + (j + 1) * P],
                                                    xg[:, j, k * P:(k + 1) * P], ident[:, :])
                        last.then_inc(xturned, 1)

                    def hidden(wt, o, kc, src, n, half):
                        for m in range(MC):
                            c = half * MC + m
                            if m % 2 == 0:
                                pe.wait_ge(evac, n * CH + c + 2)
                            bank = ps[c // 2][:, (c % 2) * ET:(c % 2 + 1) * ET]
                            for k in range(kc):
                                if half and m == 0 and k % 2 == 0:
                                    pe.wait_ge(h_s, (n + 1) * CP + k // 2 + 1)
                                for i, (a, b) in enumerate(PASSES):
                                    last = pe.matmul(bank, wt[a][:, o + k * M1 + m * P:o + k * M1 + (m + 1) * P],
                                                     src[b][:, k, :], start=k + i == 0, stop=k == kc - 1 and i == 2)
                            last.then_inc(h_ps, 1)

                    def layer3(wt, n):
                        pe.wait_ge(h_s, (n + 1) * CP)
                        pe.wait_ge(o_add, n + 1)
                        for j in range(TT):
                            for i, (k, (a, b)) in enumerate((k, p) for k in range(MC) for p in PASSES):
                                last = pe.matmul(ps[4][:, j * D:(j + 1) * D], h2[a][:, k, j * P:(j + 1) * P],
                                                 wt[b][:, O3 + k * D:O3 + (k + 1) * D],
                                                 start=i == 0, stop=i == 3 * MC - 1)
                        last.then_inc(o_ps, 1)

                    def step(n, par, par3, at):
                        if at is not None:
                            pe.wait_ge(wsp, (2 * at[0] + at[1]) * 3 + 1)
                        pe.wait_ge(xsp, n + 1)
                        hidden(w[par], 0, KC, xs, n, 0)
                        layer3(w[par3], n)
                        turn_rows(n + 1)
                        if at is not None:
                            pe.wait_ge(wsp, (2 * at[0] + at[1]) * 3 + 3)
                        hidden(w[par], O2, MC, h1, n, 1)

                    turn_rows(0)
                    pe.wait_ge(zeroed, 5)
                    n = experts(pe, lambda *_: None, step)
                    layer3(w[1], n)

                @block.scalar
                def _(act):
                    act.nop().then_inc(evac, CH)

                    def rows_hi(n):
                        act.wait_ge(xturned, n + 1)
                        act.activation(xs[0][:, :, :], ps[5][:, :].rearrange("p (k t) -> p k t", k=KC),
                                       ACT.Copy).then_inc(xhi, 1)

                    def step(n, par, par3, at):
                        if at is not None:
                            act.wait_ge(wsp, (2 * at[0] + at[1]) * 3 + 1)
                        load_rows(act, n + 2)
                        for c in range(CH):
                            if c == MC:
                                rows_hi(n + 1)
                            if c % 2 == 0:
                                act.wait_ge(h_ps, n * CH + c + 2)
                                act.wait_ge(h_s, n * CP + c // 2 + 1)
                            act.activation(u[:, c // 2, c % 2, :], ps[c // 2][:, (c % 2) * ET:(c % 2 + 1) * ET],
                                           ACT.Relu, bias=bias[:, par, c // MC, c % MC:c % MC + 1]).then_inc(evac, 1)

                    load_rows(act, 1)
                    rows_hi(0)
                    experts(act, lambda *_: None, step)

                @block.gpsimd
                def _(pool):
                    for v in (h2[0][:, :, :], h2[1][:, :, :], w[1][0][:, O3:NW], w[1][1][:, O3:NW]):
                        pool.memset(v.bitcast(F32), 0.0).then_inc(zeroed, 1)
                    pool.memset(bias3[:, 1, :], 0.0).then_inc(zeroed, 1)
                    pool.nop().then_inc(h_s, CP)
                    def step(n, par, par3, _):
                        for c in range(CP):
                            h = (h1, h2)[c // (CP // 2)]
                            k = 2 * (c % (CP // 2))
                            pool.wait_ge(h_hi, n * CP + c + 1)
                            pool.tensor_tensor(h[1][:, k:k + 2, :], u[:, c, :, :], h[0][:, k:k + 2, :],
                                               ALU.subtract).then_inc(h_s, 1)
                    n = experts(pool, lambda *_: None, step)
                    pool.wait_ge(stored, n * 16 + 32)

                @block.vector
                def _(dve):
                    ch = Chain(dve, wch)
                    dve.nop().then_inc(o_add, 1)
                    dve.nop().then_inc(stored, 16)

                    def split_weights(par, e, n):
                        o, o_end, _ = PARTS[n]
                        dve.wait_ge(win[n], (e + 1) * (48, 16, 32)[n])
                        if n == 0:
                            ch.link(dve.tensor_copy(bias[:, par, :, :], rawb[:, :, :]))
                        if n == 2:
                            ch.link(dve.tensor_copy(bias3[:, par, :], rawb3[:, :]))
                        ch.link(dve.tensor_copy(w[par][0][:, o:o_end], raw[:, o:o_end]))
                        dve.tensor_tensor(w[par][1][:, o:o_end], raw[:, o:o_end], w[par][0][:, o:o_end],
                                          ALU.subtract).then_inc(wsp, 1)

                    def rows_lo(n):
                        dve.wait_ge(xhi, n + 1)
                        dve.tensor_tensor(xs[1][:, :, :], ps[5][:, :].rearrange("p (k t) -> p k t", k=KC),
                                          xs[0][:, :, :], ALU.subtract).then_inc(xsp, 1)

                    def hi(n, c):
                        h = (h1, h2)[c // (CP // 2)]
                        k = 2 * (c % (CP // 2))
                        dve.wait_ge(evac, (n + 1) * CH + 2 * c + 2)
                        dve.tensor_copy(h[0][:, k:k + 2, :], u[:, c, :, :]).then_inc(h_hi, 1)

                    def output(n, par3):
                        dve.wait_ge(o_ps, n + 1)
                        dve.wait_ge(stored, (n + 1) * 16)
                        dve.tensor_tensor(yo[:, :, :], ps[4][:, :].rearrange("p (j d) -> p j d", j=TT),
                                          bias3[:, par3, :].unsqueeze(1).to_broadcast([P, TT, D]),
                                          ALU.add).then_inc(o_add, 1)

                    def step(n, par, par3, at):
                        def next_weights(part):
                            if at is not None and not (at[2] and at[1]):
                                if part == 0:
                                    ch.base, ch.k = before + (2 * at[0] + at[1]) * 5, 0
                                split_weights(1 - par, 2 * at[0] + at[1] + 1, part)
                        for c in range(CP // 2):
                            hi(n, c)
                        next_weights(0)
                        output(n, par3)
                        rows_lo(n + 1)
                        next_weights(1)
                        for c in range(CP // 2, CP):
                            hi(n, c)
                        next_weights(2)

                    split_weights(0, 0, 0)
                    rows_lo(0)
                    for n in range(1, 3):
                        split_weights(0, 0, n)
                    before = ch.k
                    dve.wait_ge(zeroed, 5)
                    n = experts(dve, lambda *_: None, step)
                    output(n, 1)

        def weights_split(dve, ch, pairs, done):
            for raw, hi, lo in pairs:
                ch.link(dve.tensor_copy(hi, raw))
                dve.tensor_tensor(lo, raw, hi, ALU.subtract).then_inc(done, 1)

        def norm_root(chain, req, var_ap, tmp, eps, scale=1.0):
            chain.eng.tensor_scalar(tmp, var_ap, scale, eps, ALU.mult, ALU.add).then_inc(req, 1)

        def stage_linear_attention(qp, ff_raw, ff_in):
            gathered = [sem(f"la_in{g}") for g in range(G)]
            w_in, wsp, ones, gin = sem("la_win"), sem("la_wsplit"), sem("la_ones"), sem("la_gin")
            half, summed = sem("la_half"), sem("la_summed")
            qps, qact, qsum, qhi = sem("la_qps"), sem("la_qact"), sem("la_qsum"), sem("la_qhi")
            kps, kt, ke, ksum, khi = sem("la_kps"), sem("la_kt"), sem("la_ke"), sem("la_ksum"), sem("la_khi")
            qlo, klo = [sem(f"la_qlo{n}") for n in range(2)], [sem(f"la_klo{n}") for n in range(2)]
            kvps, kvdone, nps, nuse = sem("la_kvps"), sem("la_kvdone"), sem("la_nps"), sem("la_nuse")
            rreq, root, densum, scaled, gained = (sem(f"la_{x}") for x in ("rreq", "root", "densum", "scaled", "gained"))
            normed = [sem(f"la_normed{n}") for n in range(2)]
            n0 = turns_done[0]
            turns_done[0] += 2 * KC * G
            with ExitStack() as st:
                def sbl(name, shape, dt=F32):
                    return st.enter_context(nc.sbuf_tensor(name, shape, dt))
                two = sbl("la_two", [P, NT, 2, D])
                raw = sbl("la_raw", [P, KC, 3 * D])
                w = [sbl(f"la_w{h}", [P, KC, 3 * D], F32R) for h in "hl"]
                bq, bkv = sbl("la_bq", [P, KC]), sbl("la_bkv", [P, 2 * D])
                qe_sb, qr_sb = sbl("la_qesb", [P, 2, GT]), sbl("la_qrsb", [P, 2, GT])
                KS = 3
                kv32, ke_sb = sbl("la_kv32", [P, KS, 2 * D]), sbl("la_kesb", [P, KS, D])
                kt_s = [[sbl(f"la_kt{p}{h}", [P, 2 * D + 2], F32R) for h in "hl"] for p in range(2)]
                kvh = [sbl(f"la_kv{h}", [P, B, KC, LW], F32R) for h in "hl"]
                den = sbl("la_den", [P, NT])
                stats, mv, rstd = sbl("la_stats", [P, NT, 6]), sbl("la_mv", [P, NT, 2]), sbl("la_rstd", [P, NT])
                gb = sbl("la_gb", [P, 2, D])
                block = st.enter_context(nc.Block())
                NQ = KC * G
                OL = NB // TG
                KLAG = 2

                def next_up(i):
                    g = i // TG
                    return g + 1 if i % TG == (g == 0) and g + 1 < G else None
                order = []
                for i in range(-1, NT):
                    if i == -1:
                        order += [("t", k) for k in range(KC)]
                    elif i % TG == 0:
                        order += [("q", i // TG * KC + k) for k in range(KC)]
                    if i > 0 and next_up(i - 1):
                        order += [("t", next_up(i - 1) * KC + k) for k in range(KC)]
                    if i >= NT - TG:
                        order += [("o", (i - NT + TG) * 2 + k) for k in range(2)]
                for g in range(OL):
                    order += [("o", NB + g * TG + j) for j in range(TG)] + [("r", g * KC + k) for k in range(KC)]
                order += [("r", k) for k in range(OL * KC, NQ)]
                assert B == 2 and NB == 2 * TG
                bank_of = {u: ps[(0, 1, 2, 7)[n % 4]] for n, u in enumerate(order)}
                before = {u: order[n - 4] for n, u in enumerate(order) if n >= 4}

                def low_parts(eng, sems, n, total):
                    eng.wait_ge(sems[n // (total // 2)], n % (total // 2) + 1)

                def query_lo(eng, n):
                    m, sl = split_at(n)
                    eng.wait_ge(qhi, n + 1)
                    eng.tensor_tensor(qp[1][:, m, sl], qr_sb[:, n % 2, :], qp[0][:, m, sl],
                                      ALU.subtract).then_inc(qlo[n // (NQ // 2)], 1)

                def keys_lo(eng, i):
                    eng.wait_ge(khi, i + 1)
                    eng.tensor_tensor(kt_s[i % 2][1][:, 0:2 * D], kv32[:, i % KS, :], kt_s[i % 2][0][:, 0:2 * D],
                                      ALU.subtract).then_inc(klo[i // (NT // 2)], 1)

                @block.sync
                def _(sp):
                    sp.dma_start(raw[:, :, :], d["Wqkv"].rearrange("(k p) n -> p k n", p=P)).then_inc(w_in, 16)
                    sp.dma_start(bq[:, :], d["bq_cols"]).then_inc(w_in, 16)
                    sp.dma_start(bkv[:, :], d["bqkv"][D:3 * D].partition_broadcast(P)).then_inc(w_in, 16)
                    for n, name in enumerate(("g1", "be1")):
                        sp.dma_start(gb[:, n, :], d[name].partition_broadcast(P)).then_inc(gin, 16)
                    for n, name in enumerate(("Wg", "Wu")):
                        sp.dma_start(ff_raw[n][:, :, :], d[name].rearrange("(k p) n -> p k n", p=P)).then_inc(ff_in[n], 16)

                @block.tensor
                def _(pe):
                    def take(u):
                        if u in before:
                            kind, n = before[u]
                            if kind in "tr":
                                pe.wait_ge(lo_done, n0 + n + 1 + (NQ if kind == "r" else 0))
                            elif kind == "q":
                                pe.wait_ge(qact, n + 1)
                            else:
                                pe.wait_ge(nuse, n + 1)
                        return bank_of[u]

                    def turn(kind, g):
                        if kind == "t":
                            pe.wait_ge(summed, g + 1)
                        else:
                            pe.wait_ge(normed[g // OL], g % OL + 1)
                        for k in range(KC):
                            bank = take((kind, g * KC + k))
                            for j in range(TG):
                                last = pe.transpose(bank[:, j * P:(j + 1) * P],
                                                    y[:, g * TG + j, k * P:(k + 1) * P], ident[:, :])
                            last.then_inc(turned, 1)

                    def query(g):
                        pe.wait_ge(lo_done, n0 + (g + 1) * KC)
                        for m in range(KC):
                            bank = take(("q", g * KC + m))
                            for i, (k, (a, b)) in enumerate((k, p) for k in range(KC) for p in PASSES):
                                last = pe.matmul(bank, w[a][:, k, m * P:(m + 1) * P],
                                                 actT[b][:, k, g * GT:(g + 1) * GT], start=i == 0, stop=i == 3 * KC - 1)
                            last.then_inc(qps, 1)

                    def project(i):
                        if i >= 2:
                            pe.wait_ge(kt, i - 1)
                        for n, (k, (a, b)) in enumerate((k, p) for k in range(KC) for p in PASSES):
                            last = pe.matmul(ps[3 + i % 2], actT[a][:, k, i * P:(i + 1) * P],
                                             w[b][:, k, D:3 * D], start=n == 0, stop=n == 3 * KC - 1)
                        last.then_inc(kps, 1)

                    def keys_values(i):
                        low_parts(pe, klo, i, NT)
                        b, first, fin = i // NB, i % NB == 0, i % NB == NB - 1
                        if i == 0:
                            pe.wait_ge(ones, 6)
                        if b and first:
                            pe.wait_ge(kvdone, b)
                        for c in range(KC):
                            for n, (p_, q_) in enumerate(PASSES):
                                last = pe.matmul(ps[5 + c][:, 0:LW], kt_s[i % 2][p_][:, c * P:(c + 1) * P],
                                                 kt_s[i % 2][q_][:, D:D + LW], start=first and n == 0,
                                                 stop=fin and n == 2)
                        last.then_inc(kvps, 1)

                    def output(i):
                        if i % NB == 0:
                            pe.wait_ge(kvdone, i // NB + 1)
                            low_parts(pe, qlo, (i // NB + 1) * OL * KC - 1, NQ)
                        bank = take(("o", i))
                        for n, (c, (a, b)) in enumerate((c, p) for c in range(KC) for p in PASSES):
                            last = pe.matmul(bank[:, 0:LW], qp[a][:, c, i * P:(i + 1) * P],
                                             kvh[b][:, i // NB, c, :], start=n == 0, stop=n == 3 * KC - 1)
                        last.then_inc(nps, 1)

                    turn("t", 0)
                    pe.wait_ge(wsp, 1)
                    for i in range(NT):
                        if i % TG == 0:
                            query(i // TG)
                        project(i)
                        if i >= KLAG:
                            keys_values(i - KLAG)
                        if i and next_up(i - 1):
                            turn("t", next_up(i - 1))
                        if i >= NT - TG:
                            for k in range(2):
                                output((i - NT + TG) * 2 + k)
                    for i in range(NT - KLAG, NT):
                        keys_values(i)
                    for i in range(NB, NT):
                        output(i)
                        if i % TG == TG - 1:
                            turn("r", i // TG - OL)
                    for g in range(OL, G):
                        turn("r", g)

                def turned_bank(n):
                    return bank_of[("t", n) if n < NQ else ("r", n - NQ)]

                def split_at(n):
                    return n % KC, slice(n // KC % G * GT, (n // KC % G + 1) * GT)

                @block.scalar
                def _(act):
                    def halves(g):
                        act.wait_ge(gathered[g], 16 * 2 * TG)
                        for i in range(g * TG, (g + 1) * TG):
                            act.activation(y[:, i, :], two[:, i, 0, :], ACT.Copy, scale=top2[:, i, 0:1]).then_inc(half, 1)

                    def hi(n):
                        k, sl = split_at(n)
                        act.wait_ge(turned, n0 + n + 1)
                        act.activation(act_hi[:, k, sl], turned_bank(n), ACT.Copy).then_inc(hi_done, 1)

                    def query(n):
                        act.wait_ge(qps, n + 1)
                        if n >= 2:
                            low_parts(act, qlo, n - 2, NQ)
                        act.activation(qe_sb[:, n % 2, :], bank_of["q", n], ACT.Exp,
                                       bias=bq[:, n % KC:n % KC + 1])
                        act.activation(qr_sb[:, n % 2, :], bank_of["q", n], ACT.Relu,
                                       bias=bq[:, n % KC:n % KC + 1]).then_inc(qact, 1)

                    def keys(i):
                        act.wait_ge(kt, i + 1)
                        if i >= KS:
                            act.wait_ge(ksum, i - KS + 1)
                        act.activation(ke_sb[:, i % KS, :], kv32[:, i % KS, 0:D], ACT.Exp).then_inc(ke, 1)

                    act.wait_ge(w_in, 48)
                    halves(0)
                    for k in range(KC):
                        hi(k)
                    for i in range(NT):
                        g = i // TG
                        if i % TG == 0:
                            for k in range(KC):
                                query(g * KC + k)
                        if i and next_up(i - 1):
                            for k in range(KC):
                                hi(next_up(i - 1) * KC + k)
                        keys(i)
                        if next_up(i):
                            halves(next_up(i))
                    for g in range(G):
                        act.wait_ge(rreq, g + 1)
                        act.activation(rstd[:, g * TG:(g + 1) * TG], rstd[:, g * TG:(g + 1) * TG], ACT.Sqrt).then_inc(root, 1)
                        if g >= OL - 1 and g + 1 < G:
                            for k in range(KC):
                                hi(NQ + (g + 1 - OL) * KC + k)
                    for k in range(OL * KC, NQ):
                        hi(NQ + k)

                @block.gpsimd
                def _(pool):
                    for p_ in range(2):
                        pool.memset(kt_s[p_][0][:, 2 * D:2 * D + 2].bitcast(F32), 0.0).then_inc(ones, 1)
                        pool.memset(kt_s[p_][1][:, 2 * D:2 * D + 2].bitcast(F32), 0.0).then_inc(ones, 1)
                    pool.wait_ge(ones, 4)
                    for p_ in range(2):
                        pool.memset(kt_s[p_][0][:, 2 * D:2 * D + 1].bitcast(F32), 1.0).then_inc(ones, 1)
                    for i in range(NT):
                        for n in range(2):
                            pool.indirect_dma_start(
                                out=two[:, i, n, :], out_offset=None, in_=y_rows,
                                in_offset=bass.IndirectOffsetOnAxis(ap=place[:, i, n:n + 1], axis=0))\
                                .then_inc(gathered[i // TG], 16)
                    for i in range(NT // 2, NT):
                        if i % TG == 0:
                            for n in range(i // TG * KC, (i // TG + 1) * KC):
                                query_lo(pool, n)
                        keys_lo(pool, i)
                    pool.wait_ge(gin, 32)
                    for g in range(OL):
                        sl = slice(g * TG, (g + 1) * TG)
                        pool.wait_ge(scaled, g + 1)
                        pool.tensor_tensor(y[:, sl, :], y[:, sl, :], group_rows(gb[:, 0, :]), ALU.mult).then_inc(gained, 1)
                        pool.wait_ge(gained, g + 1)
                        pool.tensor_tensor(y[:, sl, :], y[:, sl, :], group_rows(gb[:, 1, :]), ALU.add).then_inc(normed[0], 1)

                @block.vector
                def _(dve):
                    ch = dve_chain.on(dve)

                    def combine(g):
                        dve.wait_ge(half, (g + 1) * TG)
                        for i in range(g * TG, (g + 1) * TG):
                            last = dve.scalar_tensor_tensor(out=y[:, i, :], in0=two[:, i, 1, :], scalar=top2[:, i, 1:2],
                                                            in1=y[:, i, :], op0=ALU.mult, op1=ALU.add)
                        last.then_inc(summed, 1)

                    def lo(n):
                        k, sl = split_at(n)
                        dve.wait_ge(hi_done, n0 + n + 1)
                        dve.tensor_tensor(act_lo[:, k, sl], turned_bank(n), act_hi[:, k, sl],
                                          ALU.subtract).then_inc(lo_done, 1)

                    def query(n):
                        m, sl = split_at(n)
                        dve.wait_ge(qact, n + 1)
                        dve.scalar_tensor_tensor(out=qr_sb[:, n % 2, :], in0=qe_sb[:, n % 2, :], scalar=1.0,
                                                 in1=qr_sb[:, n % 2, :], op0=ALU.min, op1=ALU.add).then_inc(qsum, 1)
                        dve.wait_ge(qsum, n + 1)
                        dve.tensor_copy(qp[0][:, m, sl], qr_sb[:, n % 2, :]).then_inc(qhi, 1)
                        if n < NQ // 2:
                            query_lo(dve, n)

                    def bias(i):
                        dve.wait_ge(kps, i + 1)
                        if i >= KS:
                            low_parts(dve, klo, i - KS, NT)
                        dve.tensor_tensor(kv32[:, i % KS, :], ps[3 + i % 2], bkv[:, :], ALU.add).then_inc(kt, 1)

                    def keys(i):
                        s_ = i % KS
                        dve.wait_ge(ke, i + 1)
                        ch.link(dve.tensor_scalar(kv32[:, s_, 0:D], kv32[:, s_, 0:D], 0.0, None, ALU.max))
                        dve.scalar_tensor_tensor(out=kv32[:, s_, 0:D], in0=ke_sb[:, s_, :], scalar=1.0,
                                                 in1=kv32[:, s_, 0:D], op0=ALU.min, op1=ALU.add).then_inc(ksum, 1)
                        dve.wait_ge(ksum, i + 1)
                        if i >= 2:
                            dve.wait_ge(kvps, i - 1)
                        dve.tensor_copy(kt_s[i % 2][0][:, 0:2 * D], kv32[:, s_, :]).then_inc(khi, 1)
                        if i < NT // 2:
                            keys_lo(dve, i)

                    def finish(b):
                        dve.wait_ge(kvps, (b + 1) * NB)
                        for c in range(KC):
                            ch.link(dve.tensor_copy(kvh[0][:, b, c, :], ps[5 + c][:, 0:LW]))
                            last = dve.tensor_tensor(kvh[1][:, b, c, :], ps[5 + c][:, 0:LW], kvh[0][:, b, c, :], ALU.subtract)
                        last.then_inc(kvdone, 1)

                    def stats_of(i):
                        dve.wait_ge(nuse, i + 1)
                        return dve.bn_stats(stats[:, i, :], y[:, i, :])

                    def output(i):
                        bank = bank_of["o", i]
                        dve.wait_ge(nps, i + 1)
                        dve.tensor_scalar(den[:, i:i + 1], bank[:, D:D + 1], 1e-6, None, ALU.add).then_inc(densum, 1)
                        if i % TG:
                            stats_of(i - 1)
                        dve.wait_ge(densum, i + 1)
                        ch.link(dve.reciprocal(den[:, i:i + 1], den[:, i:i + 1]))
                        dve.scalar_tensor_tensor(out=y[:, i, :], in0=bank[:, 0:D], scalar=den[:, i:i + 1],
                                                 in1=y[:, i, :], op0=ALU.mult, op1=ALU.add).then_inc(nuse, 1)
                        if i % TG == TG - 1:
                            ch.link(stats_of(i))
                            for j in range(i + 1 - TG, i + 1):
                                last = dve.bn_aggr(mv[:, j, :], stats[:, j, :])
                            ch.link(last)
                            sl = slice(i + 1 - TG, i + 1)
                            norm_root(ch, rreq, mv[:, sl, 1], rstd[:, sl], 1e-5)

                    def norm(g):
                        norm_group(ch, y, g, mv, rstd, root, g + 1)
                        if g < OL:
                            dve.nop().then_inc(scaled, 1)
                        else:
                            gain_group(ch, y, g, gb[:, 0, :], group_rows(gb[:, 1, :])).then_inc(normed[1], 1)

                    dve.wait_ge(w_in, 48)
                    weights_split(dve, ch, [(raw[:, :, :], w[0][:, :, :], w[1][:, :, :])], wsp)
                    combine(0)
                    for k in range(KC):
                        lo(k)
                    for i in range(NT):
                        g = i // TG
                        if i % TG == 0:
                            for k in range(KC):
                                query(g * KC + k)
                        bias(i)
                        if i == NB + KLAG:
                            finish(0)
                        if i:
                            keys(i - 1)
                        if i and next_up(i - 1):
                            for k in range(KC):
                                lo(next_up(i - 1) * KC + k)
                        if next_up(i):
                            combine(next_up(i))
                        if i > NT - TG:
                            for k in range(2):
                                output((i - NT + TG - 1) * 2 + k)
                    keys(NT - 1)
                    for k in range(2):
                        output(NB - 2 + k)
                    finish(1)
                    dve.wait_ge(gin, 32)
                    for g in range(OL):
                        norm(g)
                    for i in range(NB, NT):
                        output(i)
                        if i % TG == TG - 1:
                            for k in range(KC):
                                lo(NQ + (i // TG - OL) * KC + k)
                        if i == NB + TG + 1:
                            norm(OL)
                    for g in range(OL + 1, G):
                        norm(g)
                    for k in range(OL * KC, NQ):
                        lo(NQ + k)

        def group_rows(row):
            return row.unsqueeze(1).to_broadcast([P, TG, D])

        def norm_group(ch, src, g, mv, rstd, root, n_root):
            dve = ch.eng
            sl = slice(g * TG, (g + 1) * TG)
            dve.wait_ge(root, n_root)
            ch.link(dve.reciprocal(rstd[:, sl], rstd[:, sl]))
            for i in range(g * TG, (g + 1) * TG):
                last = dve.tensor_scalar(src[:, i, :], src[:, i, :], mv[:, i, 0:1], rstd[:, i:i + 1],
                                         ALU.subtract, ALU.mult)
            ch.link(last)

        def gain_group(ch, src, g, gain, plus):
            sl = slice(g * TG, (g + 1) * TG)
            ch.link(ch.eng.tensor_tensor(src[:, sl, :], src[:, sl, :], group_rows(gain), ALU.mult))
            return ch.eng.tensor_tensor(src[:, sl, :], src[:, sl, :], plus, ALU.add)

        def stage_feed_forward(raw, raw_in, pj_raw, pj_in):
            d_in, wsp, gin, bin_, padded = (sem(f"ff_{x}") for x in ("din", "wsplit", "gin", "bin", "padded"))
            xin, biased, xbiased = [sem(f"ff_x{g}") for g in range(G)], sem("ff_biased"), sem("ff_xbiased")
            hps, sil, h32d, hhi, hsp = (sem(f"ff_{x}") for x in ("hps", "silu", "h32", "hhi", "hsplit"))
            ops, used, rreq, root, normed = (sem(f"ff_{x}") for x in ("ops", "used", "rreq", "root", "normed"))
            n0 = turns_done[0]
            turns_done[0] += KC * G
            with ExitStack() as st:
                def sbl(name, shape, dt=F32):
                    return st.enter_context(nc.sbuf_tensor(name, shape, dt))
                rawd = sbl("ff_rawd", [P, FC, D])
                wg = [sbl(f"ff_wg{h}", [P, KC, FC * P], F32R) for h in "hl"]
                wu = [sbl(f"ff_wu{h}", [P, KC, FC * P], F32R) for h in "hl"]
                wd = [sbl(f"ff_wd{h}", [P, FC, D], F32R) for h in "hl"]
                bg, bu = sbl("ff_bg", [P, FC]), sbl("ff_bu", [P, FC])
                sl_sb, h32 = sbl("ff_silusb", [P, 2, GT]), sbl("ff_h32sb", [P, 2, GT])
                hh = [sbl(f"ff_h{h}", [P, FC, GT], F32R) for h in "hl"]
                gb, xk = sbl("ff_gb", [P, 3, D]), sbl("ff_x", [P, NT, D])
                stats, mv, rstd = sbl("ff_stats", [P, NT, 6]), sbl("ff_mv", [P, NT, 2]), sbl("ff_rstd", [P, NT])
                block = st.enter_context(nc.Block())
                NS = G * FC

                @block.sync
                def _(sp):
                    sp.wait_ge(padded, 3)
                    for v, s_ in ((bg, "bg"), (bu, "bu")):
                        sp.dma_start(v[:, 0:FC - 1], d[s_ + "_cols"]).then_inc(bin_, 16)
                        sp.dma_start(v[0:FR, FC - 1:FC], d[s_][(FC - 1) * P:F].rearrange("(p a) -> p a", a=1),
                                     allow_slow_non_contiguous=True).then_inc(bin_, 16)
                    sp.dma_start(rawd[:, 0:FC - 1, :],
                                 d["Wd"][0:(FC - 1) * P].rearrange("(c p) n -> p c n", p=P)).then_inc(d_in, 16)
                    sp.dma_start(rawd[0:FR, FC - 1, :], d["Wd"][(FC - 1) * P:F]).then_inc(d_in, 16)
                    for n, name in enumerate(("g2", "be2", "bd")):
                        sp.dma_start(gb[:, n, :], d[name].partition_broadcast(P)).then_inc(gin, 16)
                    for g in range(G):
                        sp.dma_start(xk[:, g * TG:(g + 1) * TG, :], x_tok[:, g * TG:(g + 1) * TG, :]).then_inc(xin[g], 16)
                    for n, name in enumerate(("WqT", "WkT", "WvT")):
                        sp.dma_start(pj_raw[:, n, :, :], d[name].rearrange("(k p) n -> p k n", p=P)).then_inc(pj_in, 16)

                @block.tensor
                def _(pe):
                    def up(s):
                        g, m = s // FC, s % FC
                        for v, (wt, bank) in enumerate(((wg, ps[s % 2]), (wu, ps[2 + s % 2]))):
                            if s == 0:
                                pe.wait_ge(wsp, v + 1)
                            if s >= 2:
                                pe.wait_ge((sil, h32d)[v], s - 1)
                            for n, (k, (a, b)) in enumerate((k, p) for k in range(KC) for p in PASSES):
                                last = pe.matmul(bank, wt[a][:, k, m * P:(m + 1) * P],
                                                 actT[b][:, k, g * GT:(g + 1) * GT], start=n == 0,
                                                 stop=n == 3 * KC - 1)
                            last.then_inc(hps, 1)

                    def down(g):
                        if g == 0:
                            pe.wait_ge(wsp, 3)
                        pe.wait_ge(hsp, (g + 1) * FC)
                        for j in range(TG):
                            i = g * TG + j
                            if i >= 2:
                                pe.wait_ge(used, i - 1)
                            for n, (m, (a, b)) in enumerate((m, p) for m in range(FC) for p in PASSES):
                                last = pe.matmul(ps[4 + i % 2][:, 0:D], hh[a][:, m, j * P:(j + 1) * P],
                                                 wd[b][:, m, :], start=n == 0, stop=n == 3 * FC - 1)
                            last.then_inc(ops, 1)

                    def turn(g):
                        pe.wait_ge(normed, g + 1)
                        for k in range(KC):
                            if g:
                                pe.wait_ge(lo_done, n0 + (g - 1) * KC + k + 1)
                            for j in range(TG):
                                last = pe.transpose(ps[6 + k % 2][:, j * P:(j + 1) * P],
                                                    y[:, g * TG + j, k * P:(k + 1) * P], ident[:, :])
                            last.then_inc(turned, 1)

                    up(0)
                    for g in range(G):
                        for m in range(1, FC):
                            up(g * FC + m)
                        if g + 1 < G:
                            up((g + 1) * FC)
                        if g:
                            turn(g - 1)
                        down(g)
                    turn(G - 1)

                @block.scalar
                def _(act):
                    def hi(g):
                        sl = slice(g * GT, (g + 1) * GT)
                        for k in range(KC):
                            act.wait_ge(turned, n0 + g * KC + k + 1)
                            act.activation(act_hi[:, k, sl], ps[6 + k % 2], ACT.Copy).then_inc(hi_done, 1)

                    def take_root(g):
                        sl = slice(g * TG, (g + 1) * TG)
                        act.wait_ge(rreq, g + 1)
                        act.activation(rstd[:, sl], rstd[:, sl], ACT.Sqrt).then_inc(root, 1)

                    act.wait_ge(bin_, 16 * 4)
                    for s in range(NS):
                        g, m = s // FC, s % FC
                        act.wait_ge(hps, 2 * s + 1)
                        if s >= 2:
                            act.wait_ge(h32d, s - 1)
                        act.activation(sl_sb[:, s % 2, :], ps[s % 2], ACT.Silu,
                                       bias=bg[:, m:m + 1]).then_inc(sil, 1)
                        if g and m == 2:
                            take_root(g - 1)
                        if g >= 2 and m == 0:
                            hi(g - 2)
                    hi(G - 2)
                    take_root(G - 1)
                    hi(G - 1)

                @block.gpsimd
                def _(pool):
                    pool.memset(bg[:, FC - 1:FC], 0.0).then_inc(padded, 1)
                    pool.memset(bu[:, FC - 1:FC], 0.0).then_inc(padded, 1)
                    pool.memset(rawd[:, FC - 1, :], 0.0).then_inc(padded, 1)
                    for s in range(NS):
                        g, m = s // FC, s % FC
                        pool.wait_ge(hhi, s + 1)
                        pool.tensor_tensor(hh[1][:, m, :], h32[:, s % 2, :], hh[0][:, m, :],
                                           ALU.subtract).then_inc(hsp, 1)
                        if m in (1, 3):
                            sl = slice(g * TG, (g + 1) * TG)
                            if m == 1:
                                pool.wait_ge(gin, 48)
                                pool.tensor_tensor(y[:, sl, :], y[:, sl, :], group_rows(gb[:, 2, :]), ALU.add).then_inc(biased, 1)
                            else:
                                pool.wait_ge(xin[g], 16)
                                pool.tensor_tensor(xk[:, sl, :], xk[:, sl, :], group_rows(gb[:, 1, :]), ALU.add).then_inc(xbiased, 1)

                @block.vector
                def _(dve):
                    ch = dve_chain.on(dve)
                    for part in range(2):
                        for wt in (wg, wu):
                            last = dve.memset(wt[part][:, :, F:FC * P].bitcast(F32), 0.0)
                    ch.link(last)
                    for n, wt in enumerate((wg, wu)):
                        dve.wait_ge(raw_in[n], 16)
                        weights_split(dve, ch, [(raw[n][:, :, :], wt[0][:, :, 0:F], wt[1][:, :, 0:F])], wsp)

                    def hidden(s):
                        m = s % FC
                        dve.wait_ge(sil, s + 1)
                        dve.wait_ge(hps, 2 * s + 2)
                        if s >= 2:
                            dve.wait_ge(hsp, s - 1)
                        dve.scalar_tensor_tensor(out=h32[:, s % 2, :], in0=ps[2 + s % 2],
                                                 scalar=bu[:, m:m + 1], in1=sl_sb[:, s % 2, :],
                                                 op0=ALU.add, op1=ALU.mult).then_inc(h32d, 1)
                        dve.wait_ge(h32d, s + 1)
                        if s >= FC:
                            dve.wait_ge(ops, (s // FC) * TG)
                        dve.tensor_copy(hh[0][:, m, :], h32[:, s % 2, :]).then_inc(hhi, 1)

                    def lo(g):
                        sl = slice(g * GT, (g + 1) * GT)
                        for k in range(KC):
                            dve.wait_ge(hi_done, n0 + g * KC + k + 1)
                            dve.tensor_tensor(act_lo[:, k, sl], ps[6 + k % 2], act_hi[:, k, sl],
                                              ALU.subtract).then_inc(lo_done, 1)

                    def add(g):
                        dve.wait_ge(biased, g + 1)
                        for i in range(g * TG, (g + 1) * TG):
                            dve.wait_ge(ops, i + 1)
                            dve.tensor_tensor(y[:, i, :], ps[4 + i % 2][:, 0:D], y[:, i, :], ALU.add).then_inc(used, 1)
                        for i in range(g * TG, (g + 1) * TG):
                            dve.wait_ge(used, i + 1)
                            last = dve.bn_stats(stats[:, i, :], y[:, i, :])
                        ch.link(last)
                        for i in range(g * TG, (g + 1) * TG):
                            last = dve.bn_aggr(mv[:, i, :], stats[:, i, :])
                        ch.link(last)
                        sl = slice(g * TG, (g + 1) * TG)
                        norm_root(ch, rreq, mv[:, sl, 1], rstd[:, sl], 1e-5)

                    def gain(g):
                        dve.wait_ge(xbiased, g + 1)
                        gain_group(ch, y, g, gb[:, 0, :], xk[:, g * TG:(g + 1) * TG, :]).then_inc(normed, 1)

                    for s in range(NS):
                        g, m = s // FC, s % FC
                        if s != FC * g or g == 0:
                            hidden(s)
                        if s == 0:
                            dve.wait_ge(d_in, 32)
                            weights_split(dve, ch, [(rawd[:, :, :], wd[0][:, :, :], wd[1][:, :, :])], wsp)
                        if g and m == 0:
                            if g >= 2:
                                lo(g - 2)
                            add(g - 1)
                            hidden(s)
                        if g and m == 3:
                            norm_group(ch, y, g - 1, mv, rstd, root, g)
                        if g and m == 4:
                            gain(g - 1)
                    lo(G - 2)
                    add(G - 1)
                    norm_group(ch, y, G - 1, mv, rstd, root, G)
                    gain(G - 1)
                    lo(G - 1)

        def stage_project(raw, w_in, kT, v_tok, n_live, live_at, mbias, pen, identb):
            wsp = sem("pj_wsplit")
            qps, qhi, qlo, vps, vev = (sem(f"pj_{x}") for x in ("qps", "qhi", "qlo", "vps", "vev"))
            m_in, cnt_in, cnt_ps, mready, cset = (sem(f"pj_{x}") for x in ("min", "cntin", "cntps", "mready", "cset"))
            with ExitStack() as st:
                def sbl(name, shape, dt=F32):
                    return st.enter_context(nc.sbuf_tensor(name, shape, dt))
                w = [sbl(f"pj_w{h}", [P, 3, KC, D], F32R) for h in "hl"]
                m32 = sbl("pj_m32", [P, QT, S // 4], I32)
                m8 = m32[:, :, :].bitcast(U8)
                free = sbl("pj_free", [P, QT, QT])
                cnt, rc, keys = sbl("pj_cnt", [P, QT]), sbl("pj_rc", [P, QT]), sbl("pj_keys", [P, QT])
                one = sbl("pj_one", [P, P])
                rank, rb, srt = sbl("pj_rank", [P, QT]), sbl("pj_rb", [P, QT]), sbl("pj_srt", [P, 8])
                lv, nl = sbl("pj_lv", [P, QT]), sbl("pj_nl", [P, 1])
                block = st.enter_context(nc.Block())

                @block.sync
                def _(sp):
                    sp.dma_start(m32[:, :, :], d["mask"].rearrange("(q p) t -> p q t", p=P)).then_inc(m_in, 16)

                @block.gpsimd
                def _(pool):
                    pool.memset(one[:, :], 1.0).then_inc(cset, 1)
                    pool.iota(rank[:, :], pattern=[[1, QT]], base=0, channel_multiplier=0,
                              allow_small_or_imprecise_dtypes=True).then_inc(cset, 1)

                @block.tensor
                def _(pe):
                    u = 0
                    for n in range(2):
                        pe.wait_ge(wsp, n + 1)
                        for m in range(KC):
                            for g in range(G):
                                if u >= 4:
                                    pe.wait_ge(qlo, u - 3)
                                for i, (k, (a, b)) in enumerate((k, p) for k in range(KC) for p in PASSES):
                                    last = pe.matmul(ps[u % 4][:, :], w[a][:, n, k, m * P:(m + 1) * P],
                                                     actT[b][:, k, g * GT:(g + 1) * GT], start=i == 0,
                                                     stop=i == 3 * KC - 1)
                                last.then_inc(qps, 1)
                                u += 1
                    pe.wait_ge(wsp, 3)
                    for i in range(NT):
                        if i >= 3:
                            pe.wait_ge(vev, i - 2)
                        for n, (k, (a, b)) in enumerate((k, p) for k in range(KC) for p in PASSES):
                            last = pe.matmul(ps[4 + i % 3][:, 0:D], actT[a][:, k, i * P:(i + 1) * P],
                                             w[b][:, 2, k, :], start=n == 0, stop=n == 3 * KC - 1)
                        last.then_inc(vps, 1)
                        if i == NT * 3 // 4:
                            pe.wait_ge(cset, 2)
                            pe.wait_ge(cnt_in, 1)
                            pe.matmul(ps[7][:, 0:QT], one[:, :], keys[:, :], start=True, stop=True).then_inc(cnt_ps, 1)

                @block.scalar
                def _(act):
                    for u in range(2 * KC * G):
                        m, g = u // G % KC, u % G
                        dst = (qp, kT)[u // (KC * G)][0]
                        act.wait_ge(qps, u + 1)
                        act.activation(dst[:, m, g * GT:(g + 1) * GT], ps[u % 4][:, :], ACT.Copy).then_inc(qhi, 1)
                    for i in range(NT):
                        act.wait_ge(vps, i + 1)
                        act.activation(v_tok[:, i, :], ps[4 + i % 3][:, 0:D], ACT.Copy).then_inc(vev, 1)

                @block.vector
                def _(dve):
                    ch = dve_chain.on(dve)
                    for n in range(3):
                        dve.wait_ge(w_in, 48)
                        weights_split(dve, ch, [(raw[:, n, :, :], w[0][:, n, :, :], w[1][:, n, :, :])], wsp)
                    for u in range(2 * KC * G):
                        m, g = u // G % KC, u % G
                        hi, lo = (qp, kT)[u // (KC * G)]
                        sl = slice(g * GT, (g + 1) * GT)
                        dve.wait_ge(qhi, u + 1)
                        dve.tensor_tensor(lo[:, m, sl], ps[u % 4][:, :], hi[:, m, sl], ALU.subtract).then_inc(qlo, 1)
                        if u % 2 == 0:
                            q = u // 2
                            dve.wait_ge(m_in, 16)
                            dve.tensor_scalar(mbias[:, q, :], m8[:, q, :], MASKED, None, ALU.mult).then_inc(mready, 1)
                            last = dve.tensor_reduce(free[:, q, :], m8[:, q, :].rearrange("p (j t) -> p j t", t=P),
                                                     AX.X, ALU.add)
                    assert QT == KC * G
                    ch.link(last)
                    ch.link(dve.tensor_copy(identb[:, :], ident[:, :]))
                    ch.link(dve.tensor_scalar(free[:, :, :], free[:, :, :], -1.0, float(P), ALU.mult, ALU.add))
                    ch.link(dve.tensor_reduce(cnt[:, :], free[:, :, :], AX.X, ALU.add))
                    ch.link(dve.reciprocal(rc[:, :], cnt[:, :]))
                    ch.link(dve.tensor_scalar(pen[:, :], rc[:, :], 0.0, None, ALU.mult))
                    dve.tensor_reduce(keys[:, :], free[:, :, :].rearrange("p q j -> p j q"), AX.X,
                                      ALU.add).then_inc(cnt_in, 1)
                    dve.wait_ge(cnt_ps, 1)
                    ch.link(dve.tensor_scalar(lv[:, :], ps[7][:, 0:QT], 0.0, None, ALU.is_gt))
                    ch.link(dve.tensor_reduce(nl[:, :], lv[:, :], AX.X, ALU.add))
                    ch.link(dve.tensor_scalar(nl[:, :], nl[:, :], 1.0, None, ALU.max))
                    ch.link(dve.tensor_copy(n_live[:, :], nl[:, :]))
                    dve.wait_ge(cset, 2)
                    ch.link(dve.tensor_scalar(rb[:, :], lv[:, :], 1000.0, -900.0, ALU.mult, ALU.add))
                    ch.link(dve.tensor_tensor(rb[:, :], rb[:, :], rank[:, :], ALU.subtract))
                    ch.link(dve.max(srt[:, :], rb[:, :]))
                    ch.link(dve.tensor_scalar(srt[:, :], srt[:, :], -1.0, 100.0, ALU.mult, ALU.add))
                    ch.link(dve.tensor_scalar(rb[:, :], srt[:, :], float(QT), None, ALU.is_lt))
                    ch.link(dve.tensor_tensor(srt[:, :], srt[:, :], rb[:, :], ALU.mult))
                    ch.link(dve.tensor_copy(live_at[:, :], srt[:, :]))
                    dve.wait_ge(mready, QT)

        def stage_attention(kT, v_tok, n_live, live_at, mbias, pen, identb, load_ahead):
            names = ("init", "kbhi", "kblo", "vb", "mb", "sps", "red", "mnew", "diff", "moved", "sub", "pex",
                     "ptps", "ptev", "pvps", "scaled", "added", "fin", "zeroed")
            (init, kb_hi, kb_lo, vb_set, mb_set, sps, red, mnew, diff, moved, sub, pex,
             ptps, ptev, pvps, scaled, added, fin, zeroed) = (sem(f"at_{x}") for x in names)
            with ExitStack() as st:
                def sbl(name, shape, dt=F32):
                    return st.enter_context(nc.sbuf_tensor(name, shape, dt))
                hm = sbl("at_hm", [P, HC])
                ones = sbl("at_ones", [P, HC])
                assert KC * T == B * KC * HC * P
                kb = [v[:, :, :].rearrange("p k t -> p (k t)").rearrange("p (b c h t) -> p b c h t", b=B, c=KC, h=HC)
                      for v in actT]
                vb = sbl("at_vb", [P, B, NH, HD + 1])
                mb = sbl("at_mb", [P, QT, P], BF16)
                NP = HC * P
                pn = sbl("at_pn", [P, 2, NP + HC])
                pT = sbl("at_pT", [P, 2, HC, P])
                mx = sbl("at_mx", [P, B, QT, NH])
                mn = sbl("at_mn", [P, 2, HC])
                acc = sbl("at_acc", [P, B, QT, NH, HD + 1])
                rc = sbl("at_rc", [P, B * QT, NH])
                block = st.enter_context(nc.Block())
                NSTEP = QT * KC
                NS = B * NSTEP
                HB = GT // P
                SCALE = float(HD) ** -0.5
                scr = lambda s: psum[:, 2 * (s % 2):2 * (s % 2) + 2, :].rearrange("p b (h t) -> p (b h) t", t=P)
                ptb = psum[:, 4:6, :].rearrange("p b (h t) -> p (b h) t", t=P)
                at = lambda s: (s // NSTEP, (s % NSTEP) // KC, s % KC)
                hs = lambda c: slice(c * HC, (c + 1) * HC)

                def key_tile(eng, part, b, c, jt):
                    return eng.tensor_tensor(
                        kb[part][:, b, c, :, :],
                        kT[part][:, c, bass.ds(b * S + jt * P, P)].unsqueeze(1).to_broadcast([P, HC, P]),
                        hm[:, :].unsqueeze(2).to_broadcast([P, HC, P]), ALU.mult)

                @block.sync
                def _(sp):
                    load_ahead(sp)

                @block.tensor
                def _(pe):
                    n = nc.tensor.value_load(n_live[0:1, 0:1], min_val=1, max_val=QT)
                    pe.nop().then_inc(ptps, 2)

                    def scores(j, s):
                        b, u, c = at(s)
                        step = j * NS + s
                        if s % NSTEP < KC:
                            pe.wait_ge(kb_hi, (j * B + b) * KC + c + 1)
                            pe.wait_ge(kb_lo, (j * B + b) * KC + c + 1)
                        if s == 0:
                            pe.wait_ge(mb_set, j + 1)
                        pe.wait_ge(sub, step + 1)
                        for h2 in range(HC // HB):
                            bank = ps[2 * (s % 2) + h2]
                            for i, (a, b_) in enumerate(PASSES):
                                pe.matmul(bank[:, :], qp[a][:, c, b * S + u * P:b * S + (u + 1) * P],
                                          kb[b_][:, b, c, h2 * HB:(h2 + 1) * HB, :], start=i == 0, stop=False)
                            last = pe.matmul(bank[:, :], identb[:, :],
                                             mb[:, u, :].unsqueeze(1).to_broadcast([P, HB, P]),
                                             start=False, stop=True)
                        last.then_inc(sps, 1)

                    def turn_over(j, s):
                        step = j * NS + s
                        pe.wait_ge(pex, step + 1)
                        pe.wait_ge(ptev, step + 1)
                        for h in range(HC):
                            last = pe.transpose(ptb[:, h, :], pn[:, s % 2, h * P:(h + 1) * P], ident[:, :])
                        last.then_inc(ptps, 1)

                    def values(j, s):
                        b, u, c = at(s)
                        step = j * NS + s
                        if s == 0:
                            pe.wait_ge(vb_set, j + 1)
                        pe.wait_ge(ptev, step + 2)
                        pe.wait_ge(added, step + NS - 1)
                        for h in range(HC):
                            last = pe.matmul(ps[6 + s % 2][:, h * (HD + 1):(h + 1) * (HD + 1)],
                                             pT[:, s % 2, h, :], vb[:, b, c * HC + h, :],
                                             start=True, stop=True)
                        last.then_inc(pvps, 1)

                    with pe.Fori(0, n) as j:
                        scores(j, 0)
                        scores(j, 1)
                        for s in range(NS):
                            if s + 2 < NS:
                                scores(j, s + 2)
                            turn_over(j, s)
                            if s:
                                values(j, s - 1)
                        values(j, NS - 1)

                @block.scalar
                def _(act):
                    n = nc.scalar.value_load(n_live[0:1, 0:1], min_val=1, max_val=QT)
                    act.nop().then_inc(ptev, 1)

                    def exponentials(j, s):
                        step = j * NS + s
                        act.wait_ge(moved, step + NS + 1)
                        act.wait_ge(sub, step + 3)
                        act.activation(pn[:, s % 2, :], pn[:, s % 2, :], ACT.Exp, scale=SCALE).then_inc(pex, 1)

                    with act.Fori(0, n) as j:
                        exponentials(j, 0)
                        for s in range(NS):
                            if s + 1 < NS:
                                exponentials(j, s + 1)
                            act.wait_ge(ptps, j * NS + s + 3)
                            act.activation(pT[:, s % 2, :, :], ptb, ACT.Copy).then_inc(ptev, 1)

                @block.gpsimd
                def _(pool):
                    n = nc.gpsimd.value_load(n_live[0:1, 0:1], min_val=1, max_val=QT)
                    pool.memset(hm[:, :], 1.0).then_inc(init, 1)
                    pool.wait_ge(init, 1)
                    pool.affine_select(out=hm[:, :], in_=hm[:, :], compare_op=ALU.is_ge, fill=0.0, base=0,
                                       pattern=[[-HD, HC]], channel_multiplier=1).then_inc(init, 1)
                    pool.wait_ge(init, 2)
                    pool.affine_select(out=hm[:, :], in_=hm[:, :], compare_op=ALU.is_ge, fill=0.0, base=HD - 1,
                                       pattern=[[HD, HC]], channel_multiplier=-1).then_inc(init, 1)
                    pool.memset(vb[:, :, :, HD:HD + 1], 1.0).then_inc(init, 1)
                    pool.memset(ones[:, :], 1.0).then_inc(init, 1)
                    pool.memset(mx[:, :, :, :], 3.0 * MASKED).then_inc(init, 1)
                    pool.wait_ge(init, 6)
                    pool.nop().then_inc(moved, NS)
                    pool.nop().then_inc(scaled, 2)

                    def scale(j, s):
                        b, u, c = at(s)
                        step = j * NS + s
                        pool.wait_ge(pex, step + 1)
                        pool.wait_ge(added, step + 1)
                        if s == 0:
                            pool.wait_ge(zeroed, 1)
                        pool.tensor_tensor(acc[:, b, u, hs(c), :], acc[:, b, u, hs(c), :],
                                           pn[:, s % 2, NP:NP + HC].unsqueeze(2).to_broadcast([P, HC, HD + 1]),
                                           ALU.mult).then_inc(scaled, 1)

                    def factor(j, s):
                        b, u, c = at(s)
                        step = j * NS + s
                        pool.wait_ge(mnew, step + 1)
                        pool.wait_ge(scaled, step + 1)
                        pool.wait_ge(moved, step + 1)
                        pool.tensor_tensor(pn[:, s % 2, NP:NP + HC], mx[:, b, u, hs(c)], mn[:, s % 2, :],
                                           ALU.subtract).then_inc(diff, 1)
                        pool.wait_ge(diff, step + 1)
                        pool.tensor_tensor(mx[:, b, u, hs(c)], mn[:, s % 2, :], ones[:, :],
                                           ALU.mult).then_inc(moved, 1)

                    with pool.Fori(0, n) as j:
                        jt = nc.gpsimd.value_load(live_at[0:1, bass.ds(j, 1)], min_val=0, max_val=QT - 1)
                        pool.wait_ge(added, (j + 1) * NS)
                        for c in range(KC):
                            key_tile(pool, 1, 0, c, jt).then_inc(kb_lo, 1)
                        pool.tensor_copy(vb[:, :, :, 0:HD], v_tok[:, :, :].rearrange("p (b q) (h e) -> p b q h e", b=B, e=HD)
                                         [:, :, bass.ds(jt, 1), :, :].rearrange("p b q h e -> p (b q) h e")).then_inc(vb_set, 1)
                        for s in range(NS):
                            if s >= 2:
                                scale(j, s - 2)
                            factor(j, s)
                            if s % NSTEP in (2, 6) and s // NSTEP + 1 < B:
                                key_tile(pool, 1, s // NSTEP + 1, s % NSTEP // 4, jt).then_inc(kb_lo, 1)
                        for s in range(NS - 2, NS):
                            scale(j, s)

                @block.vector
                def _(dve):
                    n = nc.vector.value_load(n_live[0:1, 0:1], min_val=1, max_val=QT)
                    dve.memset(acc[:, :, :, :, :], 0.0).then_inc(zeroed, 1)
                    dve.wait_ge(init, 6)
                    dve.nop().then_inc(sub, 2)
                    dve.nop().then_inc(added, NS)
                    LAG = 4

                    def add(j, s):
                        b, u, c = at(s)
                        step = j * NS + s
                        dve.wait_ge(scaled, step + 3)
                        dve.wait_ge(pvps, step + 1)
                        dve.tensor_tensor(acc[:, b, u, hs(c), :],
                                          ps[6 + s % 2][:, 0:HC * (HD + 1)].rearrange("p (h e) -> p h e", e=HD + 1),
                                          acc[:, b, u, hs(c), :], ALU.add).then_inc(added, 1)

                    with dve.Fori(0, n) as j:
                        jt = nc.vector.value_load(live_at[0:1, bass.ds(j, 1)], min_val=0, max_val=QT - 1)
                        dve.wait_ge(added, (j + 1) * NS)
                        for c in range(KC):
                            key_tile(dve, 0, 0, c, jt).then_inc(kb_hi, 1)
                        dve.tensor_copy(mb[:, :, :], mbias[:, :, bass.ds(jt * P, P)]).then_inc(mb_set, 1)
                        for s in range(NS):
                            b, u, c = at(s)
                            step = j * NS + s
                            dve.wait_ge(sps, step + 1)
                            dve.wait_ge(moved, step + NS - 1)
                            dve.wait_ge(sub, step + 1)
                            dve.tensor_reduce(mn[:, s % 2, :], scr(s), AX.X, ALU.max).then_inc(red, 1)
                            if s >= LAG:
                                add(j, s - LAG)
                            if s % NSTEP in (2, 6) and b + 1 < B:
                                key_tile(dve, 0, b + 1, s % NSTEP // 4, jt).then_inc(kb_hi, 1)
                            dve.wait_ge(red, step + 1)
                            dve.tensor_tensor(mn[:, s % 2, :], mn[:, s % 2, :], mx[:, b, u, hs(c)], ALU.max).then_inc(mnew, 1)
                            dve.wait_ge(mnew, step + 1)
                            dve.wait_ge(ptps, step + 1)
                            dve.tensor_tensor(pn[:, s % 2, 0:NP].rearrange("p (h t) -> p h t", t=P), scr(s),
                                              mn[:, s % 2, :].unsqueeze(2).to_broadcast([P, HC, P]),
                                              ALU.subtract).then_inc(sub, 1)
                        for s in range(NS - LAG, NS):
                            add(j, s)
                    dve.wait_ge(added, (n + 1) * NS)
                    dve.reciprocal(rc[:, :, :], acc[:, :, :, :, HD].rearrange("p b u h -> p (b u) h")).then_inc(fin, 1)
                    dve.wait_ge(fin, 1)
                    for b in range(B):
                        last = dve.tensor_tensor(rc[:, b * QT:(b + 1) * QT, :], rc[:, b * QT:(b + 1) * QT, :],
                                                 pen[:, :].unsqueeze(2).to_broadcast([P, QT, NH]), ALU.add)
                    last.then_inc(fin, 1)
                    dve.wait_ge(fin, 2)
                    for i in range(B * QT):
                        dve.tensor_tensor(v_tok[:, i, :].rearrange("p (h e) -> p h e", e=HD),
                                          acc[:, i // QT, i % QT, :, 0:HD],
                                          rc[:, i, :].unsqueeze(2).to_broadcast([P, NH, HD]), ALU.mult)

        def stage_condition(xc, comb, pre, loaded, e2_raw, e2_w, e2_in, e2_split):
            raw, wc, cT, bc, rs, gw = pre
            names = ("sil", "csb", "mod", "wsp", "ops", "copied", "sq", "rreq", "root", "normed", "sq2",
                     "rturned", "rhi", "rlo", "gsq", "groot", "gnormed", "gps", "gsp", "lps", "zin", "zout", "root2", "flat", "flatout")
            (sil, csb, modp, wsp, ops, copied, sq, rreq, root, normed, sq2,
             rturned, rhi, rlo, gsq, groot, gnormed, gps, gsp, lps, zin, zout, root2, flat, flat_out) = (sem(f"cd_{x}") for x in names)
            n0 = turns_done[0]
            turns_done[0] += KC * G
            with ExitStack() as st:
                def sbl(name, shape, dt=F32):
                    return st.enter_context(nc.sbuf_tensor(name, shape, dt))
                w = [sbl(f"cd_w{h}", [P, KC, D], F32R) for h in "hl"]
                cb, mod = sbl("cd_cb", [C, B, P]), sbl("cd_mod", [P, B, 2 * D])
                ss, r, ss2 = sbl("cd_ss", [P, NT]), sbl("cd_r", [P, NT]), sbl("cd_ss2", [P, NT])
                junk = sbl("cd_junk", [P, 2, 2, D])
                lgT = sbl("cd_lgT", [E2, T])
                gj, gn = sbl("cd_gj", [E2, D]), sbl("cd_gn", [E2, 1])
                gT = [sbl(f"cd_gT{h}", [P, KC, E2], F32R) for h in "hl"]
                z, sc, rep = sbl("cd_z", [P, NT, E2]), sbl("cd_sc", [P, NT, E2]), sbl("cd_rep", [P, NT, E2])
                top, sm = sbl("cd_top", [P, NT, 8]), sbl("cd_sm", [P, NT])
                block = st.enter_context(nc.Block())
                tiles_of = lambda g: range(g * TG, (g + 1) * TG)

                @block.tensor
                def _(pe):
                    def turn(g, first_bank, done, free, n):
                        for k in range(KC):
                            if g:
                                pe.wait_ge(free, n + (g - 1) * KC + k + 1)
                            for j in range(TG):
                                last = pe.transpose(ps[first_bank + k % 2][:, j * P:(j + 1) * P],
                                                    xc[:, g * TG + j, k * P:(k + 1) * P], ident[:, :])
                            last.then_inc(done, 1)

                    def product(g):
                        pe.wait_ge(lo_done, n0 + (g + 1) * KC)
                        for i in tiles_of(g):
                            if i >= 2:
                                pe.wait_ge(copied, i - 1)
                            for n, (k, (a, b)) in enumerate((k, p) for k in range(KC) for p in PASSES):
                                last = pe.matmul(ps[2 + i % 2][:, 0:D], actT[a][:, k, i * P:(i + 1) * P],
                                                 w[b][:, k, :], start=n == 0, stop=n == 3 * KC - 1)
                            last.then_inc(ops, 1)
                            if i % TG == TG // 2 - 1 and g + 1 < G:
                                turn(g + 1, 0, turned, lo_done, n0)

                    def logits(g):
                        pe.wait_ge(rlo, (g + 1) * KC)
                        if g:
                            pe.wait_ge(flat_out, g)
                        for n, (k, (a, b)) in enumerate((k, p) for k in range(KC) for p in PASSES):
                            last = pe.matmul(ps[7][0:E2, :], gT[a][:, k, :], actT[b][:, k, g * GT:(g + 1) * GT],
                                             start=n == 0, stop=n == 3 * KC - 1)
                        last.then_inc(flat, 1)

                    def turn_logits(g):
                        pe.wait_ge(flat_out, g + 1)
                        for i in tiles_of(g):
                            last = pe.transpose(ps[6][:, i * E2:(i + 1) * E2], lgT[:, i * P:(i + 1) * P],
                                                ident[0:E2, 0:E2])
                        last.then_inc(lps, 1)

                    def turn_result(g):
                        pe.wait_ge(normed, g + 1)
                        turn(g, 4, rturned, rlo, 0)

                    turn(0, 0, turned, lo_done, n0)
                    pe.wait_ge(csb, 1)
                    for b in range(B):
                        pe.matmul(ps[6 + b], cb[:, b, :], wc[:, :], start=True, stop=True).then_inc(modp, 1)
                    pe.wait_ge(wsp, 1)
                    for g in range(G + 1):
                        if g < G:
                            product(g)
                        if g == 0:
                            pe.wait_ge(gnormed, 1)
                            pe.wait_ge(normed, 1)
                            for k in range(KC):
                                last = pe.transpose(ps[6][:, k * E2:(k + 1) * E2], gw[:, k * P:(k + 1) * P],
                                                    ident[0:E2, 0:E2])
                            last.then_inc(gps, 1)
                            pe.wait_ge(gsp, 1)
                        else:
                            turn_result(g - 1)
                            if g >= 3:
                                turn_logits(g - 3)
                            if g >= 2:
                                logits(g - 2)
                    turn_logits(G - 2)
                    logits(G - 1)
                    turn_logits(G - 1)

                @block.scalar
                def _(act):
                    def hi(g, banks, wait, done, n):
                        sl = slice(g * GT, (g + 1) * GT)
                        for k in range(KC):
                            act.wait_ge(wait, n + g * KC + k + 1)
                            act.activation(act_hi[:, k, sl], ps[banks + k % 2], ACT.Copy).then_inc(done, 1)

                    def logits_out(g):
                        act.wait_ge(flat, g + 1)
                        act.activation(lgT[:, g * GT:(g + 1) * GT], ps[7][0:E2, :], ACT.Copy).then_inc(flat_out, 1)

                    def squares(g, ready, per, sums, done):
                        for i in tiles_of(g):
                            if per and i % TG == TG // 2 and g + 1 < G:
                                hi(g + 1, 0, turned, hi_done, n0)
                            if per and i % 2 == 0:
                                for j in (i, i + 1):
                                    act.wait_ge(ops, j + 1)
                                    act.activation(xc[:, j, :], ps[2 + j % 2][:, 0:D], ACT.Copy).then_inc(copied, 1)
                            act.wait_ge(ready, i + 1 if per else g + 1)
                            if i >= 2:
                                act.wait_ge(done, i - 1)
                            act.activation(junk[:, per, i % 2, :], xc[:, i, :], ACT.Square,
                                           accum_out=sums[:, i:i + 1]).then_inc(done, 1)

                    act.wait_ge(loaded, 16 * 6)
                    act.activation(cT[:, :], cT[:, :], ACT.Silu).then_inc(sil, 1)
                    act.activation(gj[:, :], gw[:, :], ACT.Square, accum_out=gn[:, :]).then_inc(gsq, 1)
                    hi(0, 0, turned, hi_done, n0)
                    act.wait_ge(gsq, 1)
                    act.activation(gn[:, :], gn[:, :], ACT.Sqrt).then_inc(groot, 1)
                    for g in range(G + 1):
                        if g < G:
                            squares(g, copied, 1, ss, sq)
                            act.wait_ge(rreq, g + 1)
                            sl = slice(g * TG, (g + 1) * TG)
                            act.activation(r[:, sl], r[:, sl], ACT.Sqrt).then_inc(root, 1)
                        if g:
                            hi(g - 1, 4, rturned, rhi, 0)
                            squares(g - 1, normed, 0, ss2, sq2)
                            if g >= 2:
                                logits_out(g - 2)
                    logits_out(G - 1)
                    act.wait_ge(sq2, NT)
                    act.activation(ss2[:, :], ss2[:, :], ACT.Sqrt).then_inc(root2, 1)
                    act.wait_ge(zin, 1)
                    act.activation(z[:, :, :], z[:, :, :], ACT.Exp, scale=-1.0).then_inc(zout, 1)

                @block.vector
                def _(dve):
                    ch = dve_chain.on(dve)
                    bc3 = lambda v: v.unsqueeze(2).to_broadcast([P, NT, E2])

                    def lo(g, banks, wait, done, n):
                        sl = slice(g * GT, (g + 1) * GT)
                        for k in range(KC):
                            dve.wait_ge(wait, n + g * KC + k + 1)
                            dve.tensor_tensor(act_lo[:, k, sl], ps[banks + k % 2], act_hi[:, k, sl],
                                              ALU.subtract).then_inc(done, 1)

                    def norm(g):
                        sl, b = slice(g * TG, (g + 1) * TG), g * TG // NB
                        dve.wait_ge(root, g + 1)
                        ch.link(dve.reciprocal(r[:, sl], r[:, sl]))
                        for i in tiles_of(g):
                            last = dve.scalar_tensor_tensor(out=xc[:, i, :], in0=xc[:, i, :], scalar=r[:, i:i + 1],
                                                            in1=mod[:, b, D:2 * D], op0=ALU.mult, op1=ALU.mult)
                        ch.link(last)
                        dve.tensor_tensor(xc[:, sl, :], xc[:, sl, :], group_rows(mod[:, b, 0:D]), ALU.add).then_inc(normed, 1)

                    dve.wait_ge(loaded, 16 * 6)
                    dve.wait_ge(sil, 1)
                    dve.tensor_copy(cb[:, :, :], cT[:, :].unsqueeze(2).to_broadcast([C, B, P])).then_inc(csb, 1)
                    weights_split(dve, ch, [(raw[:, :, :], w[0][:, :, :], w[1][:, :, :])], wsp)
                    lo(0, 0, hi_done, lo_done, n0)
                    for b in range(B):
                        dve.wait_ge(modp, b + 1)
                        ch.link(dve.tensor_tensor(mod[:, b, :], ps[6 + b], bc[:, :], ALU.add))
                        ch.link(dve.scalar_tensor_tensor(out=mod[:, b, D:2 * D], in0=mod[:, b, D:2 * D], scalar=1.0,
                                                         in1=rs[:, :], op0=ALU.add, op1=ALU.mult))
                    dve.wait_ge(groot, 1)
                    ch.link(dve.tensor_scalar(gn[:, :], gn[:, :], 1e-12, None, ALU.max))
                    ch.link(dve.reciprocal(gn[:, :], gn[:, :]))
                    dve.tensor_scalar(gw[:, :], gw[:, :], gn[:, 0:1], None, ALU.mult).then_inc(gnormed, 1)
                    for g in range(G + 1):
                        if g < G:
                            if g + 1 < G:
                                lo(g + 1, 0, hi_done, lo_done, n0)
                            dve.wait_ge(sq, (g + 1) * TG)
                            norm_root(ch, rreq, ss[:, g * TG:(g + 1) * TG], r[:, g * TG:(g + 1) * TG], 1e-6, 1.0 / D)
                        if g in (1, 2):
                            dve.wait_ge(e2_in[g - 1], 48)
                            ch.link(dve.tensor_copy(e2_w[g - 1][0][:, :], e2_raw[:, g - 1, :]))
                            dve.tensor_tensor(e2_w[g - 1][1][:, :], e2_raw[:, g - 1, :], e2_w[g - 1][0][:, :],
                                              ALU.subtract).then_inc(e2_split, 1)
                        if g:
                            lo(g - 1, 4, rhi, rlo, 0)
                        if g < G:
                            norm(g)
                        if g == 0:
                            dve.wait_ge(gps, 1)
                            gsrc = ps[6][:, 0:KC * E2].rearrange("p (k e) -> p k e", k=KC)
                            ch.link(dve.tensor_copy(gT[0][:, :, :], gsrc))
                            dve.tensor_tensor(gT[1][:, :, :], gsrc, gT[0][:, :, :], ALU.subtract).then_inc(gsp, 1)
                    dve.wait_ge(root2, 1)
                    ch.link(dve.tensor_scalar(ss2[:, :], ss2[:, :], 1e-12, None, ALU.max))
                    ch.link(dve.reciprocal(ss2[:, :], ss2[:, :]))
                    dve.wait_ge(lps, G)
                    dve.tensor_tensor(z[:, :, :], ps[6][:, 0:NT * E2].rearrange("p (i e) -> p i e", i=NT),
                                      bc3(ss2[:, :]), ALU.mult).then_inc(zin, 1)
                    dve.wait_ge(zout, 1)
                    ch.link(dve.tensor_scalar(z[:, :, :], z[:, :, :], 1.0, None, ALU.add))
                    ch.link(dve.reciprocal(sc[:, :, :], z[:, :, :]))
                    for i in range(NT):
                        last = dve.max(top[:, i, :], sc[:, i, :])
                    ch.link(last)
                    for i in range(NT):
                        last = dve.match_replace(out=rep[:, i, :], in_to_replace=top[:, i, :],
                                                 in_values=sc[:, i, :], imm_value=-1.0)
                    ch.link(last)
                    ch.link(dve.tensor_reduce(sm[:, :], top[:, :, :], AX.X, ALU.add))
                    ch.link(dve.reciprocal(sm[:, :], sm[:, :]))
                    ch.link(dve.tensor_scalar(rep[:, :, :], rep[:, :, :], 0.0, None, ALU.is_lt))
                    ch.link(dve.tensor_tensor(sc[:, :, :], sc[:, :, :], rep[:, :, :], ALU.mult))
                    dve.memset(comb[:, :, E2:E2 + 1], 1.0)
                    ch.link(dve.tensor_tensor(comb[:, :, 0:E2], sc[:, :, :], bc3(sm[:, :]), ALU.mult))

        OU, OD, NW2 = KC * H2, 2 * KC * H2, 2 * KC * H2 + D

        def load_expert2(sp, raw, win, e, slot):
            for name, o, c, n in (("w_gate", 0, KC, H2), ("w_up", OU, KC, H2), ("w_down", OD, 1, D)):
                src = d[name].rearrange("e (c p) n -> p e c n", p=P)[:, bass.ds(e, 1), :, :]
                sp.dma_start(raw[:, slot, o:o + c * n].rearrange("p (a c n) -> p a c n", a=1, c=c),
                             src).then_inc(win[slot], 16)

        def stage_experts2(comb, raw, w, win, wsp):
            names = ("dve", "hps", "sil", "h32", "hhi", "hsp", "ops", "used", "out")
            dch, hps, sil, h32d, hhi, hsp, ops, used, stored = (sem(f"e2_{x}") for x in names)
            LAG = 2
            SP_ = 2 * G
            HS = 4
            with ExitStack() as st:
                def sbl(name, shape, dt=F32):
                    return st.enter_context(nc.sbuf_tensor(name, shape, dt))
                sl_sb, h32 = sbl("e2_silusb", [P, 2, GT]), sbl("e2_h32sb", [P, 2, GT])
                hh = [sbl(f"e2_h{h}", [P, HS, GT], F32R) for h in "hl"]
                block = st.enter_context(nc.Block())

                @block.sync
                def _(sp):
                    with sp.Fori(1, E2 // 2) as t:
                        for slot in range(2):
                            sp.wait_ge(wsp, 2 * t - 1 + slot)
                            load_expert2(sp, raw, win, 2 * t + slot, slot)
                    sp.wait_ge(wsp, E2 - 1)
                    for name, o, c, n in (("sw_gate", 0, KC, H2), ("sw_up", OU, KC, H2), ("sw_down", OD, 1, D)):
                        sp.dma_start(raw[:, 0, o:o + c * n].rearrange("p (c n) -> p c n", c=c),
                                     d[name].rearrange("(c p) n -> p c n", p=P)).then_inc(win[0], 16)
                    o_tok = out.rearrange("(i p) d -> p i d", p=P)
                    for g in range(G):
                        sp.wait_ge(used, (E2 * G + g + 1) * TG + 4)
                        sp.dma_start(o_tok[:, g * TG:(g + 1) * TG, :], y[:, g * TG:(g + 1) * TG, :]).then_inc(stored, 16)
                    sp.wait_ge(stored, 16 * G)

                @block.tensor
                def _(pe):
                    def up(s, step, e):
                        par, g = (s // G) % 2, s % G
                        if g == 0:
                            pe.wait_ge(wsp, e + 1)
                        for v, (o, bank) in enumerate(((0, ps[s % 2]), (OU, ps[2 + s % 2]))):
                            pe.wait_ge((sil, h32d)[v], step + 1)
                            for n, (k, (a, b)) in enumerate((k, p) for k in range(KC) for p in PASSES):
                                last = pe.matmul(bank[:, :], w[par][a][:, o + k * H2:o + (k + 1) * H2],
                                                 actT[b][:, k, g * GT:(g + 1) * GT], start=n == 0,
                                                 stop=n == 3 * KC - 1)
                            last.then_inc(hps, 1)

                    def down(s, step):
                        par = (s // G) % 2
                        pe.wait_ge(hsp, step + 1)
                        for j in range(TG):
                            pe.wait_ge(used, step * TG + j + 1)
                            for n, (a, b) in enumerate(PASSES):
                                last = pe.matmul(ps[4 + j][:, 0:D], hh[a][:, s % HS, j * P:(j + 1) * P],
                                                 w[par][b][:, OD:OD + D], start=n == 0, stop=n == 2)
                            last.then_inc(ops, 1)

                    for s in range(LAG):
                        up(s, s, 0)
                    with pe.Fori(0, E2 // 2) as t:
                        for s in range(SP_):
                            up(s + LAG, t * SP_ + s + LAG, 2 * t + (s + LAG) // G)
                            down(s, t * SP_ + s)
                    for s in range(G):
                        if s + LAG < G:
                            up(s + LAG, E2 * G + s + LAG, E2)
                        down(s, E2 * G + s)

                def hidden_steps(eng, body):
                    for s in range(LAG):
                        body(s, s, None, 0, False)
                    with eng.Fori(0, E2 // 2 - 1) as t:
                        for s in range(SP_):
                            body(s + LAG, t * SP_ + s + LAG, s, t, False)
                    for s in range(SP_):
                        body(s + LAG, (E2 // 2 - 1) * SP_ + s + LAG, s, E2 // 2 - 1, True)
                    for s in range(G):
                        body(s + LAG if s + LAG < G else None, E2 * G + s + LAG, s, E2 // 2, True)

                @block.scalar
                def _(act):
                    act.nop().then_inc(sil, 2)

                    def body(s, step, *_):
                        if s is None:
                            return
                        act.wait_ge(hps, 2 * step + 1)
                        act.wait_ge(h32d, step + 1)
                        act.activation(sl_sb[:, s % 2, :], ps[s % 2][:, :], ACT.Silu).then_inc(sil, 1)
                    hidden_steps(act, body)

                @block.gpsimd
                def _(pool):
                    def body(s, step, *_):
                        if s is None:
                            return
                        pool.wait_ge(hhi, step + 1)
                        pool.tensor_tensor(hh[1][:, s % HS, :], h32[:, s % 2, :], hh[0][:, s % HS, :],
                                           ALU.subtract).then_inc(hsp, 1)
                    hidden_steps(pool, body)

                @block.vector
                def _(dve):
                    dve.nop().then_inc(h32d, 2)
                    dve.nop().then_inc(used, 4)

                    def split(par, loads, ch):
                        dve.wait_ge(win[par], 48 * loads)
                        ch.link(dve.tensor_copy(w[par][0][:, :], raw[:, par, :]))
                        dve.tensor_tensor(w[par][1][:, :], raw[:, par, :], w[par][0][:, :], ALU.subtract).then_inc(wsp, 1)

                    chains = [Chain(dve, dch), Chain(dve, sem("e2_dve2"))]
                    def body(s, step, out_s, t, last_turn):
                        if s is not None:
                            dve.wait_ge(sil, step + 3)
                            dve.wait_ge(hps, 2 * step + 2)
                            if out_s is not None:
                                dve.wait_ge(hsp, step - 1)
                            dve.tensor_tensor(h32[:, s % 2, :], ps[2 + s % 2][:, :], sl_sb[:, s % 2, :],
                                              ALU.mult).then_inc(h32d, 1)
                            dve.wait_ge(h32d, step + 3)
                            dve.tensor_copy(hh[0][:, s % HS, :], h32[:, s % 2, :]).then_inc(hhi, 1)
                        if out_s is not None:
                            g = out_s % G
                            first = (step - LAG) * TG
                            for j in range(TG):
                                i = g * TG + j
                                dve.wait_ge(ops, first + j + 1)
                                dve.wait_ge(used, first + 1)
                                dve.scalar_tensor_tensor(out=y[:, i, :], in0=ps[4 + j][:, 0:D],
                                                         scalar=comb[:, i, bass.ds(2 * t + out_s // G, 1)],
                                                         in1=y[:, i, :], op0=ALU.mult, op1=ALU.add).then_inc(used, 1)
                            if g == G - 1 and s is not None:
                                par = out_s // G
                                if not (last_turn and par):
                                    chains[par].base, chains[par].k = t, 0
                                    split(par, t + 2, chains[par])
                    hidden_steps(dve, body)

        with ExitStack() as st:
            raw1 = [st.enter_context(nc.sbuf_tensor(f"e1_raw{n}", shape, F32))
                    for n, shape in (("", [P, NW]), ("b", [P, 2, MC]), ("b3", [P, D]))]
            win1 = [sem(f"e1_win{n}") for n in range(3)]
            load_weights = expert1_loader(*raw1, win1)
            stage_gate1(load_weights)
            stage_experts1(*raw1, win1, load_weights)
        qp = [sb(f"qp{h}", [P, KC, T], F32R) for h in "hl"]
        pj_raw, pj_in = sb("pj_raw", [P, 3, KC, D]), sem("pj_in")
        with ExitStack() as st:
            ff_raw = [st.enter_context(nc.sbuf_tensor(f"ff_raw{n}", [P, KC, F], F32)) for n in range(2)]
            ff_in = [sem(f"ff_in{n}") for n in range(2)]
            stage_linear_attention(qp, ff_raw, ff_in)
            stage_feed_forward(ff_raw, ff_in, pj_raw, pj_in)
        v_tok = sb("v_tok", [P, NT, D])
        pre = (sb("cd_raw", [P, KC, D]), sb("cd_wc", [C, 2 * D]), sb("cd_cT", [C, B]), sb("cd_bc", [P, 2 * D]),
               sb("cd_rs", [P, D]), sb("cd_gw", [E2, D]))
        e2_raw = sb("e2_raw", [P, 2, NW2])
        pre_in, e2_in, e2_split = sem("cd_loaded"), [sem(f"e2_in{n}") for n in range(2)], sem("e2_split")

        def load_ahead(sp):
            raw, wc, cT, bc, rs, gw = pre
            sp.dma_start(cT[:, :], d["condT"]).then_inc(pre_in, 16)
            sp.dma_start(gw[:, :], d["gate_w"]).then_inc(pre_in, 16)
            sp.dma_start(raw[:, :, :], d["WoT"].rearrange("(k p) n -> p k n", p=P)).then_inc(pre_in, 16)
            sp.dma_start(wc[:, :], d["WcT"]).then_inc(pre_in, 16)
            sp.dma_start(bc[:, :], d["bc"].partition_broadcast(P)).then_inc(pre_in, 16)
            sp.dma_start(rs[:, :], d["rms_scale"].partition_broadcast(P)).then_inc(pre_in, 16)
            for slot in range(2):
                load_expert2(sp, e2_raw, e2_in, slot, slot)

        with ExitStack() as st:
            def sbm(name, shape, dt=F32):
                return st.enter_context(nc.sbuf_tensor(name, shape, dt))
            kT = [sbm(f"kT{h}", [P, KC, T], F32R) for h in "hl"]
            mbias = sbm("mbias", [P, QT, S], BF16)
            n_live, live_at = sbm("n_live", [P, 1], I32), sbm("live_at", [P, 8], I32)
            pen, identb = sbm("pen", [P, QT]), sbm("identb", [P, P], BF16)
            stage_project(pj_raw, pj_in, kT, v_tok, n_live, live_at, mbias, pen, identb)
            stage_attention(kT, v_tok, n_live, live_at, mbias, pen, identb, load_ahead)
        comb = sb("comb", [P, NT, E2 + 1])
        e2_w = [[sb(f"e2_w{p}{h}", [P, NW2], F32R) for h in "hl"] for p in range(2)]
        stage_condition(v_tok, comb, pre, pre_in, e2_raw, e2_w, e2_in, e2_split)
        stage_experts2(comb, e2_raw, e2_w, e2_in, e2_split)


def kernel(**inputs):
    import numpy as np
    import concourse.bacc as bacc
    from concourse import mybir as mb
    from concourse.bass_utils import run_bass_kernel_spmd as run

    a = {k: np.asarray(v) for k, v in inputs.items()}
    x = a["x"]
    arrays = {
        "x": x.reshape(-1, x.shape[-1]), "xT": x.reshape(-1, x.shape[-1]).T,
        "cond": a["cond_256"], "condT": a["cond_256"].T, "mask": a["mask_SxS_bk1"].view(np.int32),
        "rms_w": a["L0_cond_rms_w"], "wg_W": a["L0_cond_wg_W"], "wg_b": a["L0_cond_wg_b"],
        "gg_W": a["L0_cond_gg_W"], "gg_b": a["L0_cond_gg_b"],
        "Wqkv": a["L0_attn_Wqkv"], "bqkv": a["L0_attn_bqkv"], "Wg": a["L0_attn_Wg"], "bg": a["L0_attn_bg"],
        "Wu": a["L0_attn_Wu"], "bu": a["L0_attn_bu"], "Wd": a["L0_attn_Wd"], "bd": a["L0_attn_bd"],
        "g1": a["L0_attn_g1"], "be1": a["L0_attn_b1"], "g2": a["L0_attn_g2"], "be2": a["L0_attn_b2"],
        "WqT": a["L0_cond2_Wq"].T, "WkT": a["L0_cond2_Wk"].T, "WvT": a["L0_cond2_Wv"].T,
        "WoT": a["L0_cond2_Wo"].T, "rms_scale": a["L0_cond2_rms_scale"], "WcT": a["L0_cond2_Wc"].T,
        "bc": a["L0_cond2_bc"], "gate_w": a["L0_ffn_gate_w"], "w_gate": a["L0_ffn_w_gate"],
        "w_up": a["L0_ffn_w_up"], "w_down": a["L0_ffn_w_down"], "sw_gate": a["L0_ffn_sw_gate"],
        "sw_up": a["L0_ffn_sw_up"], "sw_down": a["L0_ffn_sw_down"],
    }
    for n in ("1", "2", "3"):
        arrays["W" + n], arrays["b" + n] = a["L0_cond_W" + n], a["L0_cond_b" + n]
        if n != "3":
            b = arrays["b" + n]
            arrays[f"b{n}_cols"] = b.reshape(b.shape[0], -1, P).transpose(2, 0, 1)

    def cols(v):
        return v[:v.size // P * P].reshape(-1, P).T

    arrays["rms_w_cols"], arrays["bq_cols"] = cols(arrays["rms_w"]), cols(arrays["bqkv"][:x.shape[-1]])
    arrays["bg_cols"], arrays["bu_cols"] = cols(arrays["bg"]), cols(arrays["bu"])
    nc = bacc.Bacc("TRN2", target_bir_lowering=False, num_devices=1)
    arrays = {f"in_{k}": np.ascontiguousarray(v) for k, v in arrays.items()}
    d = {k[3:]: nc.dram_tensor(k, v.shape, mb.dt.from_np(v.dtype), kind="ExternalInput").ap()
         for k, v in arrays.items()}
    out = nc.dram_tensor("out", d["x"].shape, mb.dt.float32, kind="ExternalOutput").ap()
    adaln_block(nc, d, out)
    r = run(nc, [arrays], core_ids=[0])
    return r.results[0]["out"].reshape(x.shape)
```
